# Optimizing a Trainium2 kernel written in Bass

```python
import numpy as np
import jax
import jax.numpy as jnp

def _softmax(x, axis=-1):
    return jax.nn.softmax(x, axis=axis)

def _gelu(x):
    return jax.nn.gelu(x, approximate=True)

def _silu(x):
    return jax.nn.silu(x)

def _sigmoid(x):
    return jax.nn.sigmoid(x)

def _layernorm(x, axis=-1, eps=1e-05):
    m = jnp.mean(x, axis=axis, keepdims=True)
    v = jnp.var(x, axis=axis, keepdims=True)
    return (x - m) / jnp.sqrt(v + eps)

def _scatter_add(tgt, idx, src, axis=0):
    return tgt.at[idx].add(src)

def _segment_sum(src, seg, n):
    return jax.ops.segment_sum(src, seg, n)
kernel_name = 'mk_early_fusion_d1_tok_img768_r4_80e11c'

def setup_inputs(seed: int=0):
    np.random.seed(seed)
    _w = jnp.asarray

    def _rec_inputs():
        import jax
        import jax.numpy as jnp
        _rk = jax.random.key(seed)
        x = -0.000356955 + 1 * jax.random.normal(jax.random.fold_in(_rk, 1), (64, 3, 224, 224), jnp.float32)
        txt = 0.0581724 + 1.9779 * jax.random.normal(jax.random.fold_in(_rk, 2), (64, 77, 192), jnp.float32)
        return (x, txt)
    x, txt = _rec_inputs()

    def _L0_tok_setup():
        import jax, jax.numpy as jnp
        import numpy as np
        C = 1.0
        P = 16
        EMBED = 192
        key = jax.random.key(seed)
        k1, k2, k3 = jax.random.split(key, 3)
        B, Cin, H, W = (128, 3, 224, 224)
        x = jax.random.normal(k1, (B, Cin, H, W), dtype=jnp.float32)
        lin_in = Cin * P * P + 1
        weight = jax.random.normal(k2, (EMBED - 1, lin_in), dtype=jnp.float32) * (1.0 / np.sqrt(lin_in))
        bias = jax.random.normal(k3, (EMBED - 1,), dtype=jnp.float32) * 0.01
        return {'x': x, 'weight': weight, 'bias': bias}
    _L0_tok_all = _L0_tok_setup()
    _L0_tok_in = {k: v for k, v in _L0_tok_all.items() if k in ('weight', 'bias')}
    del _L0_tok_all

    def _L0_attn_setup():
        import jax, jax.numpy as jnp
        import numpy as np
        B, N, C = (32, 577, 192)
        H = 12
        D = C // H
        key = jax.random.key(seed)
        ks = jax.random.split(key, 4)
        x = jax.random.normal(ks[0], (B, N, C), dtype=jnp.float32)
        w_qkv = jax.random.normal(ks[1], (C, 3 * C), dtype=jnp.float32) * C ** (-0.5)
        b_qkv = jnp.zeros((3 * C,), dtype=jnp.float32)
        scale = jnp.ones((H,), dtype=jnp.float32) * D ** (-0.5)
        w_proj = jax.random.normal(ks[2], (C, C), dtype=jnp.float32) * C ** (-0.5)
        b_proj = jnp.zeros((C,), dtype=jnp.float32)
        return {'x': x, 'w_qkv': w_qkv, 'b_qkv': b_qkv, 'scale': scale, 'w_proj': w_proj, 'b_proj': b_proj}
    _L0_attn_all = _L0_attn_setup()
    _L0_attn_in = {k: v for k, v in _L0_attn_all.items() if k in ('w_qkv', 'b_qkv', 'scale', 'w_proj', 'b_proj')}
    del _L0_attn_all

    def _L0_ffn_setup():
        import jax, jax.numpy as jnp
        import numpy as np
        B, S, H, D, E = (4, 512, 192, 256, 8)
        TOP_K = 2
        EPS = 1e-08
        LN_EPS = 1e-05

        def _gelu(t):
            return jax.nn.gelu(t, approximate=False)

        def _layer_norm(t, gamma, beta):
            mu = jnp.mean(t, axis=-1, keepdims=True)
            var = jnp.mean(jnp.square(t - mu), axis=-1, keepdims=True)
            return (t - mu) * jax.lax.rsqrt(var + LN_EPS) * gamma + beta
        key = jax.random.key(seed)
        ks = jax.random.split(key, 8)
        x = jax.random.normal(ks[0], (B, S, H), dtype=jnp.float32)
        w1 = jax.random.normal(ks[1], (H, H // 2), dtype=jnp.float32) * 0.02
        b1 = jnp.zeros((H // 2,), dtype=jnp.float32)
        w2 = jax.random.normal(ks[2], (H // 2, E), dtype=jnp.float32) * 0.02
        b2 = jnp.zeros((E,), dtype=jnp.float32)
        a_dn = float(np.sqrt(6.0 / (H + D)))
        a_up = float(np.sqrt(6.0 / (D + H)))
        down_w = jax.random.uniform(ks[3], (E, H, D), dtype=jnp.float32, minval=-a_dn, maxval=a_dn)
        down_b = jnp.zeros((E, D), dtype=jnp.float32)
        up_w = jax.random.uniform(ks[4], (E, D, H), dtype=jnp.float32, minval=-a_up, maxval=a_up)
        gamma = jnp.ones((H,), dtype=jnp.float32)
        beta = jnp.zeros((H,), dtype=jnp.float32)
        return {'x': x, 'w1': w1, 'b1': b1, 'w2': w2, 'b2': b2, 'down_w': down_w, 'down_b': down_b, 'up_w': up_w, 'gamma': gamma, 'beta': beta}
    _L0_ffn_all = _L0_ffn_setup()
    _L0_ffn_in = {k: v for k, v in _L0_ffn_all.items() if k in ('w1', 'b1', 'w2', 'b2', 'down_w', 'down_b', 'up_w', 'gamma', 'beta')}
    del _L0_ffn_all
    return {'x': x, 'txt': txt, 'L0_tok_weight': _L0_tok_in['weight'], 'L0_tok_bias': _L0_tok_in['bias'], 'L0_attn_w_qkv': _L0_attn_in['w_qkv'], 'L0_attn_b_qkv': _L0_attn_in['b_qkv'], 'L0_attn_scale': _L0_attn_in['scale'], 'L0_attn_w_proj': _L0_attn_in['w_proj'], 'L0_attn_b_proj': _L0_attn_in['b_proj'], 'L0_ffn_w1': _L0_ffn_in['w1'], 'L0_ffn_b1': _L0_ffn_in['b1'], 'L0_ffn_w2': _L0_ffn_in['w2'], 'L0_ffn_b2': _L0_ffn_in['b2'], 'L0_ffn_down_w': _L0_ffn_in['down_w'], 'L0_ffn_down_b': _L0_ffn_in['down_b'], 'L0_ffn_up_w': _L0_ffn_in['up_w'], 'L0_ffn_gamma': _L0_ffn_in['gamma'], 'L0_ffn_beta': _L0_ffn_in['beta']}

def reference(x, txt, L0_tok_weight, L0_tok_bias, L0_attn_w_qkv, L0_attn_b_qkv, L0_attn_scale, L0_attn_w_proj, L0_attn_b_proj, L0_ffn_w1, L0_ffn_b1, L0_ffn_w2, L0_ffn_b2, L0_ffn_down_w, L0_ffn_down_b, L0_ffn_up_w, L0_ffn_gamma, L0_ffn_beta):
    import jax
    import jax.numpy as jnp

    def _L0_tok_ref(x, weight, bias):
        import jax, jax.numpy as jnp
        import numpy as np
        C = 1.0
        P = 16
        EMBED = 192
        B, Cin, H, W = x.shape
        xs = jnp.transpose(x, (0, 2, 3, 1))
        t = jnp.sqrt(jnp.maximum(jnp.sum(xs * xs, axis=-1, keepdims=True) + C, 1e-06))
        xl = jnp.concatenate([t, xs], axis=-1)
        Hp, Wp = (H // P, W // P)
        K = P * P
        p = xl.reshape(B, Hp, P, Wp, P, Cin + 1)
        p = jnp.transpose(p, (0, 1, 3, 5, 2, 4)).reshape(B, Hp, Wp, Cin + 1, K)
        pt = jnp.maximum(p[..., 0, :], jnp.sqrt(jnp.float32(C)))
        t_new = jnp.sqrt(jnp.sum(pt * pt, axis=-1, keepdims=True) - (K - 1) * C)
        ps = p[..., 1:, :].reshape(B, Hp, Wp, Cin * K)
        feat = jnp.concatenate([t_new, ps], axis=-1)
        z = jnp.einsum('bhwf,of->bhwo', feat, weight) + bias
        zt = jnp.sqrt(jnp.sum(z * z, axis=-1, keepdims=True) + C)
        out = jnp.concatenate([zt, z], axis=-1)
        return out.reshape(B, Hp * Wp, EMBED)

    def _L0_attn_ref(x, w_qkv, b_qkv, scale, w_proj, b_proj):
        import jax, jax.numpy as jnp
        import numpy as np
        B, N, C = (32, 577, 192)
        H = 12
        D = C // H
        b, n, c = x.shape
        h = scale.shape[0]
        d = c // h
        qkv = (x @ w_qkv + b_qkv).reshape(b, n, 3, h, d)
        q = qkv[:, :, 0]
        k = qkv[:, :, 1]
        v = qkv[:, :, 2]
        attn = jnp.einsum('bihd,bjhd->bhij', q, k) * scale[None, :, None, None]
        if n > 1:
            mask = jnp.zeros((n, n), dtype=bool).at[1:, 1:].set(jnp.eye(n - 1, dtype=bool))
            attn = jnp.where(mask[None, None], -jnp.inf, attn)
        attn = jax.nn.softmax(attn, axis=-1)
        out = jnp.einsum('bhij,bjhd->bihd', attn, v).reshape(b, n, c)
        return out @ w_proj + b_proj

    def _L0_ffn_ref(x, w1, b1, w2, b2, down_w, down_b, up_w, gamma, beta):
        import jax, jax.numpy as jnp
        import numpy as np
        B, S, H, D, E = (4, 512, 192, 256, 8)
        TOP_K = 2
        EPS = 1e-08
        LN_EPS = 1e-05

        def _gelu(t):
            return jax.nn.gelu(t, approximate=False)

        def _layer_norm(t, gamma, beta):
            mu = jnp.mean(t, axis=-1, keepdims=True)
            var = jnp.mean(jnp.square(t - mu), axis=-1, keepdims=True)
            return (t - mu) * jax.lax.rsqrt(var + LN_EPS) * gamma + beta
        logits = _gelu(x @ w1 + b1) @ w2 + b2
        routing = jax.nn.softmax(logits, axis=-1)
        topv, topi = jax.lax.top_k(routing, TOP_K)
        sparse = jnp.sum(jax.nn.one_hot(topi, E, dtype=routing.dtype) * topv[..., None], axis=-2)
        sparse = sparse / (jnp.sum(sparse, axis=-1, keepdims=True) + EPS)
        z = _gelu(jnp.einsum('bsh,ehd->bsed', x, down_w) + down_b)
        expert_out = jnp.einsum('bsed,edh->bseh', z, up_w)
        moe_out = jnp.einsum('bseh,bse->bsh', expert_out, sparse)
        return _layer_norm(x + moe_out, gamma, beta)
    h = _L0_tok_ref(x, L0_tok_weight, L0_tok_bias)
    h = jnp.concatenate([h, txt], axis=1)
    h = h + _L0_attn_ref(_layernorm(h, axis=-1), L0_attn_w_qkv, L0_attn_b_qkv, L0_attn_scale, L0_attn_w_proj, L0_attn_b_proj)
    h = h + _L0_ffn_ref(_layernorm(h, axis=-1), L0_ffn_w1, L0_ffn_b1, L0_ffn_w2, L0_ffn_b2, L0_ffn_down_w, L0_ffn_down_b, L0_ffn_up_w, L0_ffn_gamma, L0_ffn_beta)
    return h

_drawn_inputs = setup_inputs


def setup_inputs(seed=0):
    import zlib

    import numpy as np

    out = dict(_drawn_inputs(seed))
    spreads = {'L0_attn_b_qkv': (0.0, 0.1),
     'L0_attn_scale': (0.25, 0.6),
     'L0_attn_b_proj': (0.0, 0.1),
     'L0_ffn_b1': (0.0, 0.1),
     'L0_ffn_b2': (0.0, 0.1),
     'L0_ffn_down_b': (0.0, 0.563),
     'L0_ffn_gamma': (1.0, 0.2),
     'L0_ffn_beta': (0.0, 0.1)}
    factors = {'L0_tok_bias': 6.912}
    for name, (base, spread) in spreads.items():
        noise = np.random.default_rng([zlib.crc32(name.encode()), seed]).standard_normal(out[name].shape)
        drawn = base * np.exp(spread * noise) if base else spread * noise
        out[name] = jnp.asarray(drawn.astype(out[name].dtype))
    for name, factor in factors.items():
        out[name] = (out[name] * factor).astype(out[name].dtype)
    return out
```

```python
from contextlib import ExitStack

import concourse.bass as bass
from concourse import mybir

ALU = mybir.AluOpType
ACT = mybir.ActivationFunctionType
AX = mybir.AxisListType
F32 = mybir.dt.float32
BF16 = mybir.dt.bfloat16

LN_EPS = 1e-5
GATE_EPS = 1e-8
MASK = -1e30
BANK = 512


def settled(eng, sb_const):
    eng.sem_inc(sb_const["wait_carrier"], 1)


def constants(nc, ctx):
    ident = ctx.enter_context(nc.sbuf_tensor("ident", [128, 128], F32))
    ident_bf = ctx.enter_context(nc.sbuf_tensor("ident_bf", [96, 96], BF16))
    neg_diag = ctx.enter_context(nc.sbuf_tensor("neg_diag", [96, 2, 96], BF16))
    zeroed = ctx.enter_context(nc.semaphore("c_zeroed"))
    ready = ctx.enter_context(nc.semaphore("c_ready"))
    first = ctx.enter_context(nc.semaphore("c_first"))
    names = ("bias_scaled", "dve_cleared", "gates_ready", "wait_carrier")
    extra = {n: ctx.enter_context(nc.semaphore("c_" + n)) for n in names}
    with nc.Block() as block:

        @block.gpsimd
        def _(pool):
            for tile in (ident, ident_bf, neg_diag):
                nc.gpsimd.memset(tile[:], 0.0).then_inc(zeroed, 1)
            pool.wait_ge(zeroed, 3)
            for n, (view, size, fill) in enumerate(((ident[:], 128, 1.0), (ident_bf[:], 96, 1.0),
                                                    (neg_diag[:, 0, :], 96, MASK), (neg_diag[:, 1, :], 96, MASK))):
                nc.gpsimd.affine_select(out=view, in_=view, compare_op=ALU.not_equal, fill=fill, base=0,
                                        pattern=[[-1, size]], channel_multiplier=1).then_inc(first, 1)
            pool.wait_ge(first, 4)
            nc.gpsimd.memset(neg_diag[0:1, 0, 0:1], 0.0).then_inc(ready, 1)
    return {"ident": ident, "ident_bf": ident_bf, "neg_diag": neg_diag, "ident_ready": ready, **extra}


def tokenize(nc, ctx, sems, sb_const, x, tok_w, tok_bias, tokens):
    B, Cin, HW, _ = x.shape
    P16 = 16
    NP = HW // P16
    IMG = 8
    R = IMG * NP
    G = B // IMG
    ROW = P16 * HW
    E = tok_w.shape[1] + 1
    CH = Cin * 2
    LOADED = 8 * IMG
    assert R <= 128 and G % 2 == 0 and G >= 4 and P16 * P16 == 256
    ident = sb_const["ident"]

    def sb(name, shape, dt=F32):
        return ctx.enter_context(nc.sbuf_tensor(name, shape, dt))

    def sem(name):
        return sems.enter_context(nc.semaphore(name))

    pix = [sb(f"t_pix{p}", [R, Cin, ROW]) for p in range(2)]
    patch = [sb(f"t_patch{p}", [R, Cin * P16 * P16]) for p in range(2)]
    w_sb = sb("t_w", [128, CH, E - 1])
    w_time = sb("t_w_time", [R, E - 1])
    bias_bc = sb("t_bias", [R, E - 1])
    pixT = [sb(f"t_pixT{p}", [128, CH, R]) for p in range(2)]
    time_bias = [sb(f"t_tb{p}", [R, E - 1]) for p in range(2)]
    tok = [sb(f"t_tok{p}", [R, NP, E]) for p in range(2)]
    ssq = [sb(f"t_ssq{p}", [R, NP]) for p in range(2)]
    tnew = [sb(f"t_tnew{p}", [R, NP]) for p in range(2)]
    ssz = [sb(f"t_ssz{p}", [R, NP]) for p in range(2)]
    junk = sb("t_junk", [R, Cin, P16, P16])
    junk_z = sb("t_junk_z", [R, E - 1])
    turned = [ctx.enter_context(nc.psum_tensor(f"t_turned{n}", [128, BANK], F32)) for n in range(4)]
    prod = [ctx.enter_context(nc.psum_tensor(f"t_prod{n}", [128, BANK], F32)) for n in range(2)]

    weights_in = sem("t_weights_in")
    pix_in = [sem(f"t_pix_in{p}") for p in range(2)]
    gathered = sem("t_gathered")
    sq_done = sem("t_sq_done")
    tnew_ready = sem("t_tnew_ready")
    turned_ready = sem("t_turned_ready")
    left_copied = sem("t_left_copied")
    right_copied = sem("t_right_copied")
    prod_ready = sem("t_prod_ready")
    tb_done = sem("t_tb_done")
    z_done = sem("t_z_done")
    zsq_done = sem("t_zsq_done")
    stored = [sem(f"t_stored{p}") for p in range(2)]
    zt_done = sem("t_zt_done")

    out_rows = tokens.rearrange("b (hp wp) e -> (b hp) (wp e)", wp=NP)

    with nc.Block() as block:

        @block.sync
        def _(sp):
            sp.dma_start(w_sb[:], tok_w[1:, :].rearrange("(k p) o -> p k o", p=128)).then_inc(weights_in, 16)
            sp.dma_start(w_time[:], tok_w[0:1, :].to_broadcast([R, E - 1])).then_inc(weights_in, 16)
            sp.dma_start(bias_bc[:], tok_bias.rearrange("(a o) -> a o", a=1).to_broadcast([R, E - 1])
                         ).then_inc(weights_in, 16)

            def load_group(g, p):
                for i in range(IMG):
                    src = x[bass.ds(g * IMG + i, 1)].rearrange("a c (hp f) w -> hp (a c) (f w)", f=P16)
                    sp.dma_start(pix[p][i * NP:(i + 1) * NP], src).then_inc(pix_in[p], 16)

            load_group(0, 0)
            load_group(1, 1)
            with sp.Fori(1, G // 2) as pair:
                for p in range(2):
                    g = 2 * pair + p
                    sp.wait_ge(gathered, (g - 1) * NP)
                    sp.wait_ge(sq_done, (g - 1) * NP)
                    load_group(g, p)

        @block.tensor
        def _(pe):
            pe.wait_ge(weights_in, 48)
            pe.wait_ge(sb_const["ident_ready"], 1)

            def turn(g, p, w, first):
                n = g * NP + w
                pe.wait_ge(gathered, n + 1)
                for half in range(2):
                    bank = turned[2 * (w % 2) + half]
                    if not (first and w < 2):
                        pe.wait_ge(right_copied if half else left_copied, n - 1)
                    for k in range(3):
                        j = 3 * half + k
                        last = pe.transpose(bank[:, k * R:(k + 1) * R],
                                            patch[w % 2][:, j * 128:(j + 1) * 128], ident[0:R, 0:R])
                    last.then_inc(turned_ready, 1)
                return last

            def multiply(g, w, first):
                n = g * NP + w
                pe.wait_ge(left_copied, n + 1)
                pe.wait_ge(right_copied, n + 1)
                if not (first and w < 2):
                    pe.wait_ge(z_done, n - 1)
                for k in range(CH):
                    last = pe.matmul(prod[w % 2][0:R, 0:E - 1], pixT[w % 2][:, k, :], w_sb[:, k, :],
                                     start=(k == 0), stop=(k == CH - 1))
                last.then_inc(prod_ready, 1)

            def group(g, p, first):
                for w in range(NP):
                    turn(g, p, w, first)
                    if w > 0:
                        multiply(g, w - 1, first)
                multiply(g, NP - 1, first)

            group(0, 0, True)
            group(1, 1, False)
            with pe.Fori(1, G // 2) as pair:
                group(2 * pair, 0, False)
                group(2 * pair + 1, 1, False)

        @block.vector
        def _(dve):
            def gather(g, p, w):
                n = g * NP + w
                if w == 0:
                    dve.wait_ge(pix_in[p], LOADED * g + 2 * LOADED - LOADED * p)
                if not (isinstance(n, int) and n < 2):
                    dve.wait_ge(turned_ready, 2 * n - 2)
                view = pix[p][:].rearrange("r c (py q) -> r c py q", py=P16)
                nc.vector.tensor_copy(patch[w % 2][:].rearrange("r (c py q) -> r c py q", c=Cin, py=P16),
                                      view[:, :, :, w * P16:(w + 1) * P16]).then_inc(gathered, 1)

            def group(g, p, first, last):
                for w in range(NP + 1):
                    n = g * NP + w
                    if w < NP - 1:
                        gather(g, p, w + 1)
                    elif w == NP - 1 and not last:
                        gather(g + 1, 1 - p, 0)
                    if w < NP:
                        dve.wait_ge(turned_ready, 2 * n + 1)
                        if not (first and w < 2):
                            dve.wait_ge(prod_ready, n - 1)
                        nc.vector.tensor_copy(pixT[w % 2][:, 0:3, :].rearrange("p k r -> p (k r)"),
                                              turned[2 * (w % 2)][:, 0:3 * R]).then_inc(left_copied, 1)
                        if w == 0:
                            dve.wait_ge(tnew_ready, g + 1)
                        if not (first and w < 2):
                            dve.wait_ge(z_done, n - 1)
                        nc.vector.scalar_tensor_tensor(time_bias[w % 2][:], w_time[:], tnew[p][:, w:w + 1],
                                                       bias_bc[:], ALU.mult, ALU.add).then_inc(tb_done, 1)
                    if w > 0:
                        if w == 1 and not first:
                            dve.wait_ge(stored[p], 8 * g - 8 * p)
                        dve.wait_ge(prod_ready, n)
                        dve.wait_ge(tb_done, n)
                        nc.vector.tensor_tensor(tok[p][:, w - 1, 1:E], prod[(w - 1) % 2][0:R, 0:E - 1],
                                                time_bias[(w - 1) % 2][:], ALU.add).then_inc(z_done, 1)

            dve.wait_ge(weights_in, 48)
            gather(0, 0, 0)
            group(0, 0, True, False)
            group(1, 1, False, False)
            with dve.Fori(1, G // 2 - 1) as pair:
                group(2 * pair, 0, False, False)
                group(2 * pair + 1, 1, False, False)
            group(G - 2, 0, False, False)
            group(G - 1, 1, False, True)

        @block.scalar
        def _(act):
            def square(g, p, w):
                if not (isinstance(g, int) and g * NP + w == 0):
                    act.wait_ge(sq_done, g * NP + w)
                view = pix[p][:].rearrange("r c (py q) -> r c py q", py=P16)
                nc.scalar.activation(junk[:], view[:, :, :, w * P16:(w + 1) * P16], ACT.Square,
                                     accum_out=ssq[p][:, w:w + 1]).then_inc(sq_done, 1)

            def time_features(g, p):
                act.wait_ge(sq_done, (g + 1) * NP)
                nc.scalar.activation(tnew[p][:], ssq[p][:], ACT.Sqrt, bias=1.0).then_inc(tnew_ready, 1)

            def square_tokens(g, p, w):
                n = g * NP + w
                act.wait_ge(z_done, n + 1)
                if not (isinstance(n, int) and n == 0):
                    act.wait_ge(zsq_done, n)
                nc.scalar.activation(junk_z[:], tok[p][:, w, 1:E], ACT.Square,
                                     accum_out=ssz[p][:, w:w + 1]).then_inc(zsq_done, 1)

            def group(g, p, first, last):
                for w in range(NP):
                    n = g * NP + w
                    act.wait_ge(turned_ready, 2 * n + 2)
                    if not (first and w < 2):
                        act.wait_ge(prod_ready, n - 1)
                    nc.scalar.copy(pixT[w % 2][:, 3:6, :].rearrange("p k r -> p (k r)"),
                                   turned[2 * (w % 2) + 1][:, 0:3 * R]).then_inc(right_copied, 1)
                    if w > 0:
                        square_tokens(g, p, w - 1)
                    if not last and w >= NP // 2:
                        if w == NP // 2:
                            act.wait_ge(pix_in[1 - p], LOADED * g + LOADED + 2 * LOADED - LOADED * (1 - p))
                        square(g + 1, 1 - p, 2 * w - NP)
                        square(g + 1, 1 - p, 2 * w - NP + 1)
                if not last:
                    time_features(g + 1, 1 - p)
                square_tokens(g, p, NP - 1)
                act.wait_ge(zsq_done, (g + 1) * NP)
                nc.scalar.activation(tok[p][:, :, 0], ssz[p][:], ACT.Sqrt, bias=1.0).then_inc(zt_done, 1)
                act.wait_ge(zt_done, g + 1)
                rows = out_rows[bass.ds(g * R, R)]
                act.dma_start(rows, tok[p][:].rearrange("r w e -> r (w e)")).then_inc(stored[p], 16)

            act.wait_ge(pix_in[0], 2 * LOADED)
            for w in range(NP):
                square(0, 0, w)
            time_features(0, 0)
            group(0, 0, True, False)
            group(1, 1, False, False)
            with act.Fori(1, G // 2 - 1) as pair:
                group(2 * pair, 0, False, False)
                group(2 * pair + 1, 1, False, False)
            group(G - 2, 0, False, False)
            group(G - 1, 1, False, True)
            for p in range(2):
                act.wait_ge(stored[p], 8 * G)


def attend(nc, ctx, sems, sb_const, tokens, txt, w_qk, b_qk, w_v, b_v, scale, w_proj, b_proj, mixed):
    NI, NT, E = mixed.shape
    IMG_T = tokens.shape[1]
    H = scale.shape[0]
    D = E // H
    T = 3
    TP = 96
    LAST = NT - (T - 1) * TP
    PAD = T * TP
    F2 = E // 96
    HH = 96 // D
    QS = [0, 1, 2, 0, 1, 0]
    KS = [0, 0, 0, 1, 1, 2]
    KROWS = 6 * D
    SROWS = KROWS + 2
    STRIP = 32
    HG = 4
    NG = H // HG
    assert E == 192 and D == 16 and H == 12 and 0 < LAST <= TP and IMG_T == 2 * TP + 4 and NI % 3 == 1 and NI > 9
    ident, ident_bf, neg_diag = sb_const["ident"], sb_const["ident_bf"], sb_const["neg_diag"]

    def sb(name, shape, dt=F32):
        return ctx.enter_context(nc.sbuf_tensor(name, shape, dt))

    def sem(name):
        return sems.enter_context(nc.semaphore(name))

    def ps(name):
        return ctx.enter_context(nc.psum_tensor(name, [128, BANK], F32))

    w_qk_sb = sb("a_wqk", [96, F2, 2 * E])
    w_v_sb = sb("a_wv", [96, F2, E])
    w_p_sb = sb("a_wp", [96, F2, E])
    bqk = sb("a_bqk", [96, 4])
    bqk_s = sb("a_bqks", [96, 4])
    scl = sb("a_scl", [96, 2])
    bv = sb("a_bv", [96, F2])
    bp_bc = sb("a_bp", [96, T, E])
    minus_half = sb("a_mh", [96, T])
    h_front = [sb(f"a_hf{r}", [96, T, E]) for r in range(3)]
    h_res = [sb(f"a_hr{r}", [96, T, E]) for r in range(3)]
    h_out = [sb(f"a_ho{r}", [96, T, E]) for r in range(3)]
    bst = sb("a_bst", [96, T, 6])
    mv = sb("a_mv", [96, T, 2])
    veps = sb("a_veps", [96, T])
    rstd = sb("a_rstd", [96, T])
    hn = sb("a_hn", [96, T, E])
    hnT = sb("a_hnT", [96, F2, PAD])
    qk = sb("a_qk", [96, 4, NT])
    qk_rest = sb("a_qkr", [96, 4, NT])
    parts = sb("a_parts", [96, 3, 4, NT], BF16)
    q_st = [sb(f"a_qst{r}", [SROWS, H, PAD], BF16) for r in range(3)]
    k_st = [sb(f"a_kst{r}", [SROWS, H, PAD], BF16) for r in range(3)]
    v_st = [sb(f"a_vst{r}", [96, T, H, STRIP]) for r in range(3)]
    mx = sb("a_mx", [96, T, H])
    m_hi = [sb(f"a_mhi{a}", [H // 2, PAD], BF16) for a in range(2)]
    m_lo = [sb(f"a_mlo{a}", [H // 2, PAD], BF16) for a in range(2)]
    prob = [sb(f"a_p{a}", [96, T, NT]) for a in range(2)]
    oT = sb("a_oT", [128, NG, PAD])
    rden = sb("a_rden", [96, T, H])
    on = sb("a_on", [96, T, E])
    onT = sb("a_onT", [96, F2, PAD])

    st = ctx.enter_context(nc.psum_tensor("a_st", [128, T, BANK], F32))
    sm = ctx.enter_context(nc.psum_tensor("a_sm", [128, T, BANK], F32))
    ob = ps("a_ob")
    wb = ps("a_wb")

    weights_in = sem("a_weights_in")
    cleared = sem("a_cleared")
    hf_in = [sem(f"a_hf_in{r}") for r in range(3)]
    hr_in = [sem(f"a_hr_in{r}") for r in range(3)]
    stats = sem("a_stats")
    pool_own = sem("a_pool_own")
    hn_ready = sem("a_hn_ready")
    res_ready = sem("a_res_ready")
    work_ready = sem("a_work_ready")
    work_free = sem("a_work_free")
    split = sem("a_split")
    stack_in = [sem(f"a_stack_in{r}") for r in range(3)]
    sm_ready = sem("a_sm_ready")
    max_done = sem("a_max_done")
    m_split = sem("a_m_split")
    m_ready = sem("a_m_ready")
    m_in = [[sem(f"a_m_in{r}{a}") for a in range(2)] for r in range(3)]
    st_ready = sem("a_st_ready")
    exp_done = sem("a_exp_done")
    pv_done = sem("a_pv_done")
    o_free = sem("a_o_free")
    rd_done = sem("a_rd_done")
    h2_done = sem("a_h2_done")
    stored = [sem(f"a_stored{r}") for r in range(3)]

    FRONT = ["t0", "t1", "q0", "q1", "q2", "q3", "v0", "v1"]
    FINISH = ["o0", "o1", "o2", "n0", "n1", "p0", "p1"]
    BEFORE = {0: "t0", 1: "o0", 2: "o2", 3: "q1", 4: "q2", 5: "q3", 6: "m0", 7: "v0", 8: "v1"}
    AFTER = {0: "t1", 1: "o1", 2: "q0", 3: "n0", 4: "n1", 5: "p0", 6: "p1", 11: "m1"}
    ORDER = [u for s in range(H) for u in (BEFORE.get(s), AFTER.get(s)) if u]
    assert sorted(ORDER) == sorted(FRONT + FINISH + ["m0", "m1"])

    class Step:

        def __init__(self, k, r):
            self.s = 3 * k + r
            fixed = isinstance(k, int)
            self.front = self._img(k, r, 0) if not fixed or self.s < NI else None
            self.maxima = self._img(k, r, 1) if not fixed or 1 <= self.s <= NI else None
            self.core = self._img(k, r, 2) if not fixed or 2 <= self.s <= NI + 1 else None
            self.finish = self._img(k, r, 3) if not fixed or 3 <= self.s <= NI + 2 else None
            self.next = self._img(k, r, -1) if not fixed or self.s + 1 < NI else None
            self.next_finish = self._img(k, r, 2) if not fixed or 2 <= self.s <= NI + 1 else None
            if fixed:
                clip = lambda v: max(0, min(v, NI))
                self.base = 8 * clip(self.s) + 2 * clip(self.s - 1) + 7 * clip(self.s - 3)
            else:
                self.base = 17 * self.s - 23

        @staticmethod
        def _img(k, r, back):
            q, rr = divmod(r - back, 3)
            return 3 * k + r - back, k + q, rr

        def has(self, unit):
            return (self.front if unit in FRONT else self.finish if unit in FINISH else self.maxima) is not None

        def seq(self, unit):
            return self.base + sum(self.has(u) for u in ORDER[:ORDER.index(unit)])

    def steps(engine, do):
        for s in range(6):
            do(Step(s // 3, s % 3))
        with engine.Fori(2, (NI - 1) // 3) as k:
            for r in range(3):
                do(Step(k, r))
        for s in range(NI - 1, NI + 3):
            do(Step(s // 3, s % 3))

    def wait(eng, semaphore, value):
        if not (isinstance(value, int) and value <= 0):
            eng.wait_ge(semaphore, value)

    with nc.Block() as block:

        @block.sync
        def _(sp):
            def dma(out, in_, semaphore, **kw):
                sp.dma_start(out, in_, **kw).then_inc(semaphore, 16)

            dma(w_qk_sb[:], w_qk.rearrange("(f p) o -> p f o", p=96), weights_in)
            dma(w_v_sb[:], w_v.rearrange("(f p) o -> p f o", p=96), weights_in)
            dma(w_p_sb[:], w_proj.rearrange("(f p) o -> p f o", p=96), weights_in)
            dma(bqk[:], b_qk.rearrange("(m p) -> p m", p=96), weights_in, allow_slow_non_contiguous=True)
            dma(bv[:], b_v.rearrange("(f p) -> p f", p=96), weights_in, allow_slow_non_contiguous=True)
            for d in range(D):
                dma(scl[d * HH:(d + 1) * HH, :], scale.rearrange("(h m) -> h m", m=2), weights_in)
            for t in range(T):
                dma(bp_bc[:, t, :], b_proj.rearrange("(a o) -> a o", a=1).to_broadcast([96, E]), weights_in)

            def load_tokens(dst, n, semaphore):
                img = tokens[bass.ds(n, 1)].rearrange("a t e -> (a t) e")
                dma(dst[:, 0:2, :], img[0:2 * TP].rearrange("(t p) e -> p t e", p=TP), semaphore)
                dma(dst[0:IMG_T - 2 * TP, 2, :], img[2 * TP:IMG_T], semaphore)
                dma(dst[IMG_T - 2 * TP:LAST, 2, :], txt[bass.ds(n, 1)].rearrange("a t e -> (a t) e"), semaphore)

            def spread(stack, which, part, slots, r):
                for slot, p in enumerate(slots):
                    if p == part:
                        src = parts[:, part, 2 * which:2 * which + 2, :]
                        dma(stack[r][slot * D:(slot + 1) * D, :, 0:NT], src, stack_in[r])

            def step(st_):
                if st_.next is not None:
                    n, k, r = st_.next
                    wait(sp, hn_ready, T * (n - 2))
                    load_tokens(h_front[r], n, hf_in[r])
                if st_.next_finish is not None:
                    n, k, r = st_.next_finish
                    wait(sp, h2_done, 2 * (n - 2))
                    load_tokens(h_res[r], n, hr_in[r])
                if st_.maxima is not None:
                    minus_max(st_.maxima, 0)
                if st_.front is not None:
                    n, k, r = st_.front
                    wait(sp, st_ready, H * (n - 2))
                    for part, ops in ((0, 1), (1, 3), (2, 4)):
                        sp.wait_ge(split, 4 * n + ops)
                        spread(q_st, 0, part, QS, r)
                        spread(k_st, 1, part, KS, r)
                if st_.finish is not None:
                    n, k, r = st_.finish
                    sp.wait_ge(h2_done, 2 * n + 2)
                    img = mixed[bass.ds(n, 1)].rearrange("a t e -> (a t) e")
                    dma(img[0:2 * TP].rearrange("(t p) e -> p t e", p=TP), h_out[r][:, 0:2, :], stored[r])
                    dma(img[2 * TP:NT], h_out[r][0:LAST, 2, :], stored[r])
                if st_.maxima is not None:
                    minus_max(st_.maxima, 1)

            def minus_max(image, a):
                n, k, r = image
                sp.wait_ge(m_ready, 2 * n + a + 1)
                for row, m in ((KROWS, m_hi), (KROWS + 1, m_lo)):
                    dst = q_st[r][row:row + 1, a * H // 2:(a + 1) * H // 2, 0:NT]
                    dma(dst, m[a][:, 0:NT], m_in[r][a])

            sp.wait_ge(cleared, 2)
            load_tokens(h_front[0], 0, hf_in[0])
            steps(sp, step)
            for r in range(3):
                sp.wait_ge(stored[r], 32 * len(range(r, NI, 3)))

        @block.gpsimd
        def _(pool):
            nc.gpsimd.memset(minus_half[:], -0.5)
            for r in range(3):
                nc.gpsimd.memset(v_st[r][:], 0.0).then_inc(pool_own, 1)
            for r in range(3):
                pool.wait_ge(pool_own, 3)
                nc.gpsimd.memset(v_st[r][:, :, :, D:D + 1], 1.0).then_inc(pool_own, 1)
            for r in range(3):
                pool.wait_ge(pool_own, 6)
                ones = v_st[r][:, T - 1, :, D]
                last = nc.gpsimd.affine_select(out=ones, in_=ones, compare_op=ALU.is_ge, fill=0.0, base=LAST - 1,
                                               pattern=[[0, H]], channel_multiplier=-1)
                last.then_inc(pool_own, 1)
            pool.wait_ge(pool_own, 9)
            pool.nop().then_inc(cleared, 1)
            OWN = 9

            def normalise(image, st_):
                n, k, r = image
                pool.wait_ge(stats, 2 * T * (n + 1))
                settled(pool, sb_const)
                nc.gpsimd.tensor_scalar(veps[:], mv[:, :, 1], LN_EPS, None, ALU.add).then_inc(pool_own, 1)
                pool.wait_ge(pool_own, OWN + 2 * n + 1)
                nc.gpsimd.tensor_tensor(rstd[:], veps[:], minus_half[:], ALU.pow).then_inc(pool_own, 1)
                pool.wait_ge(pool_own, OWN + 2 * n + 2)
                if st_ is not None:
                    pool.wait_ge(work_ready, st_.seq("t1") + 1)
                settled(pool, sb_const)
                for t in range(T):
                    nc.gpsimd.tensor_scalar(hn[:, t, :], h_front[r][:, t, :], mv[:, t, 0:1], rstd[:, t:t + 1],
                                            ALU.subtract, ALU.mult).then_inc(hn_ready, 1)

            def step(st_):
                if st_.finish is not None:
                    n, k, r = st_.finish
                    pool.wait_ge(hr_in[r], 48 * (k + 1))
                    nc.gpsimd.tensor_tensor(h_res[r][:], h_res[r][:], bp_bc[:], ALU.add).then_inc(res_ready, 1)
                if st_.next is not None:
                    normalise(st_.next, st_)

            pool.wait_ge(weights_in, 16 * (5 + D + T))
            normalise((0, 0, 0), None)
            steps(pool, step)

        @block.tensor
        def _(pe):
            def unit(name, st_):
                if name is None or not st_.has(name):
                    return
                seq = st_.seq(name)
                wait(pe, work_free, seq)
                kind, j = name[0], int(name[1])
                if kind == "t":
                    if j == 0:
                        pe.wait_ge(hn_ready, T * (st_.front[0] + 1))
                    for t in range(T):
                        last = pe.transpose(wb[0:96, t * TP:(t + 1) * TP], hn[:, t, j * 96:(j + 1) * 96],
                                            ident[0:96, 0:96])
                elif kind == "q":
                    for f in range(F2):
                        last = pe.matmul(wb[0:96, 0:NT], w_qk_sb[:, f, j * 96:(j + 1) * 96], hnT[:, f, 0:NT],
                                         start=(f == 0), stop=(f == F2 - 1))
                elif kind == "m":
                    pe.wait_ge(max_done, H * st_.maxima[0] + (j + 1) * H // 2)
                    for t in range(T):
                        last = pe.transpose(wb[0:H // 2, t * TP:(t + 1) * TP],
                                            mx[:, t, j * H // 2:(j + 1) * H // 2], ident[0:96, 0:96])
                elif kind == "o":
                    if j == 0:
                        pe.wait_ge(o_free, NG * (st_.finish[0] + 1))
                    for g in range(NG):
                        last = pe.transpose(wb[0:96, g * 128:(g + 1) * 128], oT[:, g, j * TP:(j + 1) * TP],
                                            ident[:, :])
                elif kind == "n":
                    for t in range(T):
                        last = pe.transpose(wb[0:96, t * TP:(t + 1) * TP], on[:, t, j * 96:(j + 1) * 96],
                                            ident[0:96, 0:96])
                else:
                    left, w = (hnT, w_v_sb) if kind == "v" else (onT, w_p_sb)
                    for i, t in enumerate(([0, 1], [2])[j]):
                        for f in range(F2):
                            last = pe.matmul(wb[0:96, i * E:(i + 1) * E], left[:, f, t * TP:(t + 1) * TP], w[:, f, :],
                                             start=(f == 0), stop=(f == F2 - 1))
                last.then_inc(work_ready, 1)

            def scores(bank, left, right, rows, h, done):
                for t in range(T):
                    width = min(TP, NT - t * TP)
                    pe.matmul(bank[0:96, t, 0:NT], left[0:rows, h, t * TP:(t + 1) * TP], right[0:rows, h, 0:NT],
                              start=True, stop=False)
                    last = pe.matmul(bank[0:96, t, t * TP:t * TP + width], ident_bf[0:96, 0:96],
                                     neg_diag[0:96, 0 if t == 0 else 1, 0:width], start=False, stop=True)
                last.then_inc(done, 1)

            def values(h, st_):
                n, k, r = st_.core
                pe.wait_ge(exp_done, H * n + h + 1)
                if h % HG == 0:
                    wait(pe, o_free, NG * n + h // HG)
                j = (h % HG) * STRIP
                for t in range(T):
                    last = pe.matmul(ob[j:j + STRIP, 0:NT], v_st[r][:, t, h, :], prob[h % 2][:, t, :],
                                     start=(t == 0), stop=(t == T - 1))
                last.then_inc(pv_done, 1)

            def step(st_):
                for h in range(H):
                    if st_.core is not None:
                        n, k, r = st_.core
                        wait(pe, exp_done, H * n + h)
                        if h % (H // 2) == 0:
                            pe.wait_ge(m_in[r][h // (H // 2)], 32 * (k + 1))
                        scores(st, k_st[r], q_st[r], SROWS, h, st_ready)
                    unit(BEFORE.get(h), st_)
                    if st_.maxima is not None:
                        n, k, r = st_.maxima
                        if h == 0:
                            pe.wait_ge(stack_in[r], 16 * 12 * (k + 1))
                        wait(pe, max_done, H * n + h)
                        scores(sm, q_st[r], k_st[r], KROWS, h, sm_ready)
                    unit(AFTER.get(h), st_)
                    if st_.core is not None and h > 0:
                        values(h - 1, st_)
                if st_.core is not None:
                    values(H - 1, st_)

            pe.wait_ge(weights_in, 16 * (5 + D + T))
            pe.wait_ge(cleared, 2)
            steps(pe, step)

        @block.scalar
        def _(act):
            def unit(name, st_):
                if name is None or not st_.has(name) or name[0] not in "tqvn":
                    return
                act.wait_ge(work_ready, st_.seq(name) + 1)
                kind, j = name[0], int(name[1])
                if kind == "t":
                    ins = nc.scalar.copy(hnT[:, j, :], wb[0:96, 0:PAD])
                elif kind == "q":
                    wait(act, split, 4 * st_.front[0])
                    ins = nc.scalar.activation(qk[:, j, :], wb[0:96, 0:NT], ACT.Identity, bias=bqk_s[:, j:j + 1],
                                               scale=scl[:, j:j + 1] if j < 2 else 1.0)
                elif kind == "n":
                    ins = nc.scalar.activation(onT[:, j, :], wb[0:96, 0:PAD], ACT.Identity, bias=bv[:, j:j + 1])
                else:
                    t0, nt = ((0, 2), (2, 1))[j]
                    dst = v_st[st_.front[2]][:, t0:t0 + nt, :, 0:D]
                    ins = nc.scalar.copy(dst, wb[0:96, 0:nt * E].rearrange("p (t h d) -> p t h d", t=nt, d=D))
                ins.then_inc(work_free, 1)

            def outputs(g, st_):
                act.wait_ge(pv_done, H * st_.core[0] + HG * (g + 1))
                nc.scalar.copy(oT[:, g, 0:NT], ob[:, 0:NT]).then_inc(o_free, 1)

            def step(st_):
                for h in range(H):
                    if st_.core is not None:
                        n, k, r = st_.core
                        act.wait_ge(st_ready, H * n + h + 1)
                        wait(act, pv_done, H * n + h - 1)
                        nc.scalar.activation(prob[h % 2][:], st[0:96, :, 0:NT], ACT.Exp).then_inc(exp_done, 1)
                    unit(BEFORE.get(h), st_)
                    unit(AFTER.get(h), st_)
                    if st_.core is not None and h in (HG, 2 * HG):
                        outputs(h // HG - 1, st_)
                if st_.core is not None:
                    outputs(NG - 1, st_)

            act.wait_ge(weights_in, 16 * (5 + D + T))
            act.wait_ge(cleared, 2)
            nc.scalar.copy(bqk_s[:, 2:4], bqk[:, 2:4]).then_inc(sb_const["bias_scaled"], 1)
            for m in range(2):
                nc.scalar.activation(bqk_s[:, m:m + 1], bqk[:, m:m + 1], ACT.Identity,
                                     scale=scl[:, m:m + 1]).then_inc(sb_const["bias_scaled"], 1)
            act.wait_ge(sb_const["bias_scaled"], 3)
            steps(act, step)

        @block.vector
        def _(dve):
            for r in range(3):
                for tile in (h_front[r], h_res[r], q_st[r], k_st[r]):
                    nc.vector.memset(tile[:], 0.0).then_inc(sb_const["dve_cleared"], 1)
            nc.vector.memset(oT[:], 1.0).then_inc(sb_const["dve_cleared"], 1)
            for r in range(3):
                dve.wait_ge(sb_const["dve_cleared"], 13)
                last = nc.vector.memset(k_st[r][KROWS:SROWS, :, 0:NT], 1.0)
                if r == 2:
                    last.then_inc(cleared, 1)

            def statistics(image):
                n, k, r = image
                dve.wait_ge(hf_in[r], 48 * (k + 1))
                wait(dve, hn_ready, T * n)
                for t in range(T):
                    nc.vector.bn_stats(bst[:, t, :], h_front[r][:, t, :]).then_inc(stats, 1)
                dve.wait_ge(stats, 2 * T * n + T)
                settled(dve, sb_const)
                for t in range(T):
                    nc.vector.bn_aggr(mv[:, t, :], bst[:, t, :]).then_inc(stats, 1)

            def unit(name, st_):
                if name is None or not st_.has(name) or name[0] not in "mop":
                    return
                dve.wait_ge(work_ready, st_.seq(name) + 1)
                kind, j = name[0], int(name[1])
                if kind == "m":
                    n, k, r = st_.maxima
                    if not (isinstance(n, int) and n == 0):
                        rr, kk = (r - 1) % 3, (k if r > 0 else k - 1)
                        dve.wait_ge(m_in[rr][j], 32 * (kk + 1))
                    nc.vector.tensor_scalar(m_hi[j][:], wb[0:H // 2, 0:PAD], -1.0, None, ALU.mult).then_inc(m_split, 1)
                    dve.wait_ge(m_split, 2 * n + j + 1)
                    dve.wait_ge(m_split, 2 * n + j + 1)
                    nc.vector.scalar_tensor_tensor(m_lo[j][:], wb[0:H // 2, 0:PAD], -1.0, m_hi[j][:],
                                                   ALU.mult, ALU.subtract).then_inc(m_ready, 1)
                    dve.wait_ge(m_ready, 2 * n + j + 1)
                    dve.sem_inc(work_free, 1)
                elif kind == "o":
                    n, k, r = st_.finish
                    heads = wb[0:96, 0:H * STRIP].rearrange("p (h c) -> p h c", c=STRIP)
                    nc.vector.reciprocal(rden[:, j, :], heads[:, :, D]).then_inc(rd_done, 1)
                    dve.wait_ge(rd_done, T * n + j + 1)
                    nc.vector.tensor_tensor(on[:, j, :].rearrange("p (h d) -> p h d", d=D), heads[:, :, 0:D],
                                            rden[:, j, :].unsqueeze(2).to_broadcast([96, H, D]), ALU.mult
                                            ).then_inc(work_free, 1)
                else:
                    n, k, r = st_.finish
                    if j == 0:
                        dve.wait_ge(res_ready, n + 1)
                        wait(dve, stored[r], 32 * k)
                    t0, nt = ((0, 2), (2, 1))[j]
                    ins = nc.vector.tensor_tensor(h_out[r][:, t0:t0 + nt, :].rearrange("p t e -> p (t e)"),
                                                  wb[0:96, 0:nt * E],
                                                  h_res[r][:, t0:t0 + nt, :].rearrange("p t e -> p (t e)"), ALU.add)
                    ins.then_inc(h2_done, 1)
                    dve.wait_ge(h2_done, 2 * n + j + 1)
                    dve.sem_inc(work_free, 1)

            def split_part(i, st_):
                n, k, r = st_.front
                if i == 0:
                    dve.wait_ge(work_free, st_.seq("q3") + 1)
                    if not (isinstance(n, int) and n == 0):
                        rr, kk = (r - 1) % 3, (k if r > 0 else k - 1)
                        dve.wait_ge(stack_in[rr], 192 * (kk + 1))
                else:
                    dve.wait_ge(split, 4 * n + i)
                if i == 0:
                    ins = nc.vector.tensor_copy(parts[:, 0], qk[:])
                elif i == 1:
                    ins = nc.vector.tensor_tensor(qk_rest[:], qk[:], parts[:, 0], ALU.subtract)
                elif i == 2:
                    ins = nc.vector.tensor_copy(parts[:, 1], qk_rest[:])
                else:
                    ins = nc.vector.tensor_tensor(parts[:, 2], qk_rest[:], parts[:, 1], ALU.subtract)
                ins.then_inc(split, 1)

            def step(st_):
                for h in range(H):
                    unit(BEFORE.get(h), st_)
                    if st_.maxima is not None:
                        n, k, r = st_.maxima
                        dve.wait_ge(sm_ready, H * n + h + 1)
                        nc.vector.tensor_reduce(mx[:, :, h], sm[0:96, :, 0:NT], AX.X, ALU.max).then_inc(max_done, 1)
                    unit(AFTER.get(h), st_)
                    if st_.front is not None and 6 <= h < 10:
                        split_part(h - 6, st_)
                    if st_.next is not None and h == 10:
                        statistics(st_.next)

            dve.wait_ge(cleared, 2)
            statistics((0, 0, 0))
            steps(dve, step)


def mix_experts(nc, ctx, sems, sb_const, mixed, w1, b1, w2, b2, down_w, down_b, up_w, gamma, beta, out):
    NE, E, DH = down_w.shape
    RH = w1.shape[1]
    TP, T = 112, 4
    N = TP * T
    src = mixed.rearrange("b t e -> (b t) e")
    dst = out.rearrange("b t e -> (b t) e")
    NTILE = src.shape[0] // N
    F2, M2 = E // 96, DH // 128
    TOP_K = 2
    assert src.shape[0] == NTILE * N and NTILE >= 7 and E == 192 and RH == 96
    ident = sb_const["ident"]

    def sb(name, shape, dt=F32):
        return ctx.enter_context(nc.sbuf_tensor(name, shape, dt))

    def sem(name):
        return sems.enter_context(nc.semaphore(name))

    def ps(name):
        return ctx.enter_context(nc.psum_tensor(name, [128, BANK], F32))

    down_sb = sb("m_down", [96, NE, F2, DH])
    up_sb = sb("m_up", [128, NE, M2, E])
    down_b_sb = sb("m_downb", [128, NE, M2])
    w1_sb = sb("m_w1", [96, F2, RH])
    b1_sb = sb("m_b1", [RH, 1])
    w2_sb = sb("m_w2", [RH, NE])
    b2_bc = sb("m_b2", [TP, T, NE])
    gamma_bc = sb("m_gamma", [TP, T, E])
    beta_bc = sb("m_beta", [TP, T, E])
    minus_half = sb("m_mh", [TP, T])
    lower = sb("m_lower", [TP, NE, NE])
    h_in = [sb(f"m_h{p}", [TP, T, E]) for p in range(2)]
    h_beta = [sb(f"m_hb{p}", [TP, T, E]) for p in range(2)]
    xn = [sb(f"m_x{p}", [TP, T, E]) for p in range(2)]
    xT = [sb(f"m_xT{p}", [96, F2, N]) for p in range(2)]
    uT = sb("m_uT", [RH, N])
    bst = sb("m_bst", [TP, T, 6])
    mv = sb("m_mv", [TP, T, 2])
    rstd = sb("m_rstd", [TP, T, 2])
    fst = sb("m_fst", [TP, T, 6])
    fmv = sb("m_fmv", [TP, T, 2])
    frstd = sb("m_frstd", [TP, T, 2])
    logits = sb("m_logits", [TP, T, NE])
    lmax = sb("m_lmax", [TP, T])
    shifted = sb("m_shifted", [TP, T, NE])
    ex = sb("m_ex", [TP, T, NE])
    total = sb("m_total", [TP, T])
    rtotal = sb("m_rtotal", [TP, T])
    routing = sb("m_routing", [TP, T, NE])
    above = sb("m_above", [TP, T, NE, NE])
    equal = sb("m_equal", [TP, T, NE, NE])
    tie = sb("m_tie", [TP, T, NE, NE])
    ahead = sb("m_ahead", [TP, T, NE, NE])
    rank = sb("m_rank", [TP, T, NE])
    sparse = sb("m_sparse", [TP, T, NE])
    kept = sb("m_kept", [TP, T])
    kept_eps = sb("m_kept_eps", [TP, T])
    rkept = sb("m_rkept", [TP, T])
    gates = [sb(f"m_gates{p}", [TP, T, NE]) for p in range(2)]
    z = [sb(f"m_z{a}", [128, M2, N]) for a in range(2)]
    acc = [sb(f"m_acc{p}", [TP, T, E]) for p in range(2)]
    y = [sb(f"m_y{p}", [TP, T, E]) for p in range(2)]

    hid = [ps(f"m_hid{n}") for n in range(4)]
    upb = [ps(f"m_up{n}_ps") for n in range(2)]
    fb = [ps(f"m_front{n}") for n in range(2)]

    weights_in = sem("m_weights_in")
    lower_ready = sem("m_lower_ready")
    h_loaded = [sem(f"m_h_in{p}") for p in range(2)]
    stats = sem("m_stats")
    pool_own = sem("m_pool_own")
    xn_ready = sem("m_xn_ready")
    hb_ready = sem("m_hb_ready")
    front_ready = sem("m_front_ready")
    front_free = sem("m_front_free")
    gate_step = sem("m_gate_step")
    ex_ready = sem("m_ex_ready")
    hid_ready = sem("m_hid_ready")
    z_ready = sem("m_z_ready")
    up_ready = sem("m_up_ready")
    acc_done = sem("m_acc_done")
    fstats = sem("m_fstats")
    final = sem("m_final")
    stored = [sem(f"m_stored{p}") for p in range(2)]
    GATE_OPS = 15
    FINAL_OPS = 5

    class Step:

        def __init__(self, k, p):
            self.s = 2 * k + p
            fixed = isinstance(k, int)
            self.next = self._tile(k, p, -1) if not fixed or self.s + 1 < NTILE else None
            self.front = self._tile(k, p, 0) if not fixed or self.s < NTILE else None
            self.experts = self._tile(k, p, 1) if not fixed or 1 <= self.s <= NTILE else None
            self.end = self._tile(k, p, 2) if not fixed or 2 <= self.s <= NTILE + 1 else None

        @staticmethod
        def _tile(k, p, back):
            q, pp = divmod(p - back, 2)
            return 2 * k + p - back, k + q, pp

    LOOPS = (NTILE - 1) // 2

    def steps(engine, do):
        for s in range(4):
            do(Step(s // 2, s % 2))
        with engine.Fori(2, LOOPS) as k:
            for p in range(2):
                do(Step(k, p))
        for s in range(2 * LOOPS, NTILE + 2):
            do(Step(s // 2, s % 2))

    def wait(eng, semaphore, value):
        if not (isinstance(value, int) and value <= 0):
            eng.wait_ge(semaphore, value)

    N_WEIGHTS = 9 + 2 * T + T

    with nc.Block() as block:

        @block.sync
        def _(sp):
            def dma(o, i, semaphore, **kw):
                sp.dma_start(o, i, **kw).then_inc(semaphore, 16)

            def load(tile):
                n, k, p = tile
                rows = src[bass.ds(n * N, N)].rearrange("(t p) e -> p t e", p=TP)
                dma(h_in[p][:], rows, h_loaded[p])

            load((0, 0, 0))
            dma(w1_sb[:], w1.rearrange("(f p) o -> p f o", p=96), weights_in)
            dma(b1_sb[:], b1.rearrange("(p a) -> p a", a=1), weights_in)
            dma(w2_sb[:], w2, weights_in)
            for m in range(M2):
                dma(down_b_sb[:, :, m], down_b[:, m * 128:(m + 1) * 128].rearrange("n p -> p n"), weights_in,
                    allow_slow_non_contiguous=True)
            for f in range(F2):
                dma(down_sb[:, :, f, :], down_w[:, f * 96:(f + 1) * 96, :].rearrange("n p o -> p n o"), weights_in)
            for m in range(M2):
                dma(up_sb[:, :, m, :], up_w[:, m * 128:(m + 1) * 128, :].rearrange("n p o -> p n o"), weights_in)
            for t in range(T):
                for row, tile, size in ((gamma, gamma_bc, E), (beta, beta_bc, E), (b2, b2_bc, NE)):
                    dma(tile[:, t, :], row.rearrange("(a o) -> a o", a=1).to_broadcast([TP, size]), weights_in)

            def step(st):
                if st.next is not None:
                    n, k, p = st.next
                    wait(sp, xn_ready, T * (n - 1))
                    wait(sp, hb_ready, n - 1)
                    load(st.next)
                if st.end is not None:
                    n, k, p = st.end
                    sp.wait_ge(final, FINAL_OPS * (n + 1))
                    rows = dst[bass.ds(n * N, N)].rearrange("(t p) e -> p t e", p=TP)
                    dma(rows, y[p][:], stored[p])

            steps(sp, step)
            for p in range(2):
                sp.wait_ge(stored[p], 16 * len(range(p, NTILE, 2)))

        @block.gpsimd
        def _(pool):
            nc.gpsimd.memset(minus_half[:], -0.5).then_inc(lower_ready, 1)
            nc.gpsimd.memset(lower[:], 1.0).then_inc(lower_ready, 1)
            pool.wait_ge(lower_ready, 2)
            nc.gpsimd.affine_select(out=lower[:], in_=lower[:], compare_op=ALU.is_gt, fill=0.0, base=0,
                                    pattern=[[1, NE], [-1, NE]], channel_multiplier=0).then_inc(lower_ready, 1)

            def normalise(tile):
                n, k, p = tile
                pool.wait_ge(stats, 2 * T * (n + 1))
                settled(pool, sb_const)
                nc.gpsimd.tensor_scalar(rstd[:, :, 0], mv[:, :, 1], LN_EPS, None, ALU.add).then_inc(pool_own, 1)
                pool.wait_ge(pool_own, 2 * n + 1)
                nc.gpsimd.tensor_tensor(rstd[:, :, 1], rstd[:, :, 0], minus_half[:], ALU.pow).then_inc(pool_own, 1)
                pool.wait_ge(pool_own, 2 * n + 2)
                wait(pool, acc_done, T * NE * (n - 2) + T)
                settled(pool, sb_const)
                for t in range(T):
                    nc.gpsimd.tensor_scalar(xn[p][:, t, :], h_in[p][:, t, :], mv[:, t, 0:1], rstd[:, t, 1:2],
                                            ALU.subtract, ALU.mult).then_inc(xn_ready, 1)

            def residual(tile):
                n, k, p = tile
                wait(pool, final, FINAL_OPS * (n - 1))
                nc.gpsimd.tensor_tensor(h_beta[p][:], h_in[p][:], beta_bc[:], ALU.add).then_inc(hb_ready, 1)

            def finish(tile):
                n, k, p = tile
                pool.wait_ge(fstats, 2 * T * (n + 1))
                settled(pool, sb_const)
                nc.gpsimd.tensor_scalar(frstd[:, :, 0], fmv[:, :, 1], LN_EPS, None, ALU.add).then_inc(final, 1)
                pool.wait_ge(final, FINAL_OPS * n + 1)
                nc.gpsimd.tensor_tensor(frstd[:, :, 1], frstd[:, :, 0], minus_half[:], ALU.pow).then_inc(final, 1)
                pool.wait_ge(final, FINAL_OPS * n + 2)
                wait(pool, stored[p], 16 * k)
                settled(pool, sb_const)
                for t in range(T):
                    last = nc.gpsimd.tensor_scalar(y[p][:, t, :], acc[p][:, t, :], fmv[:, t, 0:1], frstd[:, t, 1:2],
                                                   ALU.subtract, ALU.mult)
                last.then_inc(final, 1)
                pool.wait_ge(final, FINAL_OPS * n + 3)
                nc.gpsimd.tensor_tensor(y[p][:], y[p][:], gamma_bc[:], ALU.mult).then_inc(final, 1)
                pool.wait_ge(final, FINAL_OPS * n + 4)
                pool.wait_ge(hb_ready, n + 1)
                nc.gpsimd.tensor_tensor(y[p][:], y[p][:], h_beta[p][:], ALU.add).then_inc(final, 1)

            def step(st):
                if st.end is not None:
                    finish(st.end)
                if st.front is not None:
                    residual(st.front)
                if st.next is not None:
                    normalise(st.next)

            pool.wait_ge(weights_in, 16 * N_WEIGHTS)
            normalise((0, 0, 0))
            steps(pool, step)

        @block.tensor
        def _(pe):
            def front(u, st):
                n, k, p = st.front
                bank = fb[u % 2]
                wait(pe, front_free, 4 * n + u)
                if u < 2:
                    if u == 0:
                        pe.wait_ge(xn_ready, T * (n + 1))
                    for t in range(T):
                        last = pe.transpose(bank[0:96, t * TP:(t + 1) * TP], xn[p][:, t, u * 96:(u + 1) * 96],
                                            ident[0:TP, 0:TP])
                elif u == 2:
                    for f in range(F2):
                        last = pe.matmul(bank[0:RH, 0:N], w1_sb[:, f, :], xT[p][:, f, :],
                                         start=(f == 0), stop=(f == F2 - 1))
                else:
                    for t in range(T):
                        last = pe.matmul(bank[0:TP, t * NE:(t + 1) * NE], uT[:, t * TP:(t + 1) * TP], w2_sb[:],
                                         start=True, stop=True)
                last.then_inc(front_ready, 1)

            def down(e, st):
                n, k, p = st.experts
                for m in range(M2):
                    wait(pe, z_ready, M2 * (NE * n + e - 2) + m + 1)
                    for f in range(F2):
                        last = pe.matmul(hid[M2 * (e % 2) + m][:, 0:N], down_sb[:, e, f, m * 128:(m + 1) * 128],
                                         xT[p][:, f, :], start=(f == 0), stop=(f == F2 - 1))
                    last.then_inc(hid_ready, 1)

            def up(e, st):
                n, k, p = st.experts
                pe.wait_ge(z_ready, M2 * (NE * n + e + 1))
                for j in range(T // 2):
                    wait(pe, acc_done, T * (NE * n + e - 1) + 2 * j + 2)
                    for i in range(2):
                        t = 2 * j + i
                        for m in range(M2):
                            last = pe.matmul(upb[j][0:TP, i * E:(i + 1) * E], z[e % 2][:, m, t * TP:(t + 1) * TP],
                                             up_sb[:, e, m, :], start=(m == 0), stop=(m == M2 - 1))
                    last.then_inc(up_ready, 1)

            def step(st):
                for e in range(NE):
                    if st.experts is not None:
                        down(e, st)
                    if st.front is not None and e in (0, 1, 3, 4):
                        front((0, 1, 3, 4).index(e), st)
                    if st.experts is not None and e > 0:
                        up(e - 1, st)
                if st.experts is not None:
                    up(NE - 1, st)

            pe.wait_ge(weights_in, 16 * N_WEIGHTS)
            steps(pe, step)

        @block.scalar
        def _(act):
            def front(u, st):
                n, k, p = st.front
                if u == 3:
                    act.wait_ge(gate_step, GATE_OPS * n + 3)
                    nc.scalar.activation(ex[:], shifted[:], ACT.Exp).then_inc(ex_ready, 1)
                    return
                act.wait_ge(front_ready, 4 * n + u + 1)
                if u < 2:
                    ins = nc.scalar.copy(xT[p][:, u, :], fb[u % 2][0:96, 0:N])
                else:
                    ins = nc.scalar.activation(uT[:], fb[u % 2][0:RH, 0:N], ACT.Gelu, bias=b1_sb[:, 0:1])
                ins.then_inc(front_free, 1)

            def gelu(e, st):
                n, k, p = st.experts
                for m in range(M2):
                    act.wait_ge(hid_ready, M2 * (NE * n + e) + m + 1)
                    if m == 0:
                        wait(act, up_ready, 2 * (NE * n + e - 1))
                    nc.scalar.activation(z[e % 2][:, m, :], hid[M2 * (e % 2) + m][:, 0:N], ACT.Gelu,
                                         bias=down_b_sb[:, e, m:m + 1]).then_inc(z_ready, 1)

            def step(st):
                for e in range(NE):
                    if st.experts is not None:
                        gelu(e, st)
                    if st.front is not None and e in (0, 1, 3, 5):
                        front((0, 1, 3, 5).index(e), st)

            act.wait_ge(weights_in, 16 * N_WEIGHTS)
            steps(act, step)

        @block.vector
        def _(dve):
            def statistics(tile):
                n, k, p = tile
                dve.wait_ge(h_loaded[p], 16 * (k + 1))
                wait(dve, xn_ready, T * n)
                for t in range(T):
                    nc.vector.bn_stats(bst[:, t, :], h_in[p][:, t, :]).then_inc(stats, 1)
                dve.wait_ge(stats, 2 * T * n + T)
                settled(dve, sb_const)
                for t in range(T):
                    nc.vector.bn_aggr(mv[:, t, :], bst[:, t, :]).then_inc(stats, 1)

            def final_statistics(tile):
                n, k, p = tile
                wait(dve, final, FINAL_OPS * n)
                dve.wait_ge(acc_done, T * NE * (n + 1))
                for t in range(T):
                    nc.vector.bn_stats(fst[:, t, :], acc[p][:, t, :]).then_inc(fstats, 1)
                dve.wait_ge(fstats, 2 * T * n + T)
                settled(dve, sb_const)
                for t in range(T):
                    nc.vector.bn_aggr(fmv[:, t, :], fst[:, t, :]).then_inc(fstats, 1)

            def gate(tile):
                n, k, p = tile
                count = [0]

                def chain(ins):
                    count[0] += 1
                    ins.then_inc(gate_step, 1)
                    dve.wait_ge(gate_step, GATE_OPS * n + count[0])

                def wide(tile_, shape=(TP, T, NE)):
                    return tile_[:].unsqueeze(2).to_broadcast(list(shape))

                others = routing[:].unsqueeze(2).to_broadcast([TP, T, NE, NE])
                own = routing[:].unsqueeze(3).to_broadcast([TP, T, NE, NE])
                dve.wait_ge(front_ready, 4 * n + 4)
                chain(nc.vector.tensor_tensor(logits[:].rearrange("p t e -> p (t e)"), fb[1][0:TP, 0:T * NE],
                                              b2_bc[:].rearrange("p t e -> p (t e)"), ALU.add))
                dve.sem_inc(front_free, 1)
                chain(nc.vector.tensor_reduce(lmax[:], logits[:], AX.X, ALU.max))
                chain(nc.vector.tensor_tensor(shifted[:], logits[:], wide(lmax), ALU.subtract))
                dve.wait_ge(ex_ready, n + 1)
                chain(nc.vector.tensor_reduce(total[:], ex[:], AX.X, ALU.add))
                chain(nc.vector.reciprocal(rtotal[:], total[:]))
                chain(nc.vector.tensor_tensor(routing[:], ex[:], wide(rtotal), ALU.mult))
                chain(nc.vector.tensor_tensor(above[:], others, own, ALU.is_gt))
                chain(nc.vector.tensor_tensor(equal[:], others, own, ALU.is_equal))
                chain(nc.vector.tensor_tensor(tie[:].rearrange("p t e j -> p t (e j)"),
                                              equal[:].rearrange("p t e j -> p t (e j)"),
                                              lower[:].rearrange("p e j -> p (e j)").unsqueeze(1)
                                              .to_broadcast([TP, T, NE * NE]), ALU.mult))
                chain(nc.vector.tensor_tensor(ahead[:], above[:], tie[:], ALU.add))
                chain(nc.vector.tensor_reduce(rank[:], ahead[:], AX.X, ALU.add))
                chain(nc.vector.scalar_tensor_tensor(sparse[:], rank[:], float(TOP_K), routing[:],
                                                     ALU.is_lt, ALU.mult))
                chain(nc.vector.tensor_reduce(kept[:], sparse[:], AX.X, ALU.add))
                chain(nc.vector.tensor_scalar(kept_eps[:], kept[:], GATE_EPS, None, ALU.add))
                chain(nc.vector.reciprocal(rkept[:], kept_eps[:]))
                assert count[0] == GATE_OPS
                nc.vector.tensor_tensor(gates[p][:], sparse[:], wide(rkept), ALU.mult).then_inc(gates_ready, 1)

            def sums(e, st):
                n, k, p = st.experts
                if e == 0:
                    dve.wait_ge(gates_ready, n + 1)
                    wait(dve, final, FINAL_OPS * (n - 2) + 3)
                for t in range(T):
                    if t % 2 == 0:
                        dve.wait_ge(up_ready, 2 * (NE * n + e) + t // 2 + 1)
                    if e > 0:
                        dve.wait_ge(acc_done, T * (NE * n + e - 1) + t + 1)
                    before = xn[p] if e == 0 else acc[p]
                    nc.vector.scalar_tensor_tensor(acc[p][:, t, :], upb[t // 2][0:TP, (t % 2) * E:(t % 2 + 1) * E],
                                                   gates[p][:, t, e:e + 1], before[:, t, :], ALU.mult, ALU.add
                                                   ).then_inc(acc_done, 1)

            def step(st):
                for e in range(NE):
                    if st.experts is not None and e > 0:
                        sums(e - 1, st)
                    if st.next is not None and e == 2:
                        statistics(st.next)
                    if st.front is not None and e == 5:
                        gate(st.front)
                if st.experts is not None:
                    sums(NE - 1, st)
                    final_statistics(st.experts)

            gates_ready = sb_const["gates_ready"]
            dve.wait_ge(weights_in, 16 * N_WEIGHTS)
            dve.wait_ge(lower_ready, 3)
            statistics((0, 0, 0))
            steps(dve, step)


def early_fusion(nc, x, txt, tok_w, tok_bias, w_qk, b_qk, w_v, b_v, scale, w_proj, b_proj,
                 w1, b1, w2, b2, down_w, down_b, up_w, gamma, beta, out):
    B, NT, E = out.shape
    tokens = nc.dram_tensor("tokens_scratch", (B, NT - txt.shape[1], E), F32).ap()
    mixed = nc.dram_tensor("mixed_scratch", (B, NT, E), F32).ap()
    with ExitStack() as sems:
        sb_const = constants(nc, sems)
        with ExitStack() as ctx:
            tokenize(nc, ctx, sems, sb_const, x, tok_w, tok_bias, tokens)
        with ExitStack() as ctx:
            attend(nc, ctx, sems, sb_const, tokens, txt, w_qk, b_qk, w_v, b_v, scale, w_proj, b_proj, mixed)
        with ExitStack() as ctx:
            mix_experts(nc, ctx, sems, sb_const, mixed, w1, b1, w2, b2, down_w, down_b, up_w, gamma, beta, out)




def by_head_pair(a, E=192, H=12):
    a = a[..., :2 * E]
    lead = a.shape[:-1]
    n = len(lead)
    a = a.reshape(lead + (2, H // 2, 2, E // H))
    return a.transpose(tuple(range(n)) + (n, n + 2, n + 3, n + 1)).reshape(lead + (2 * E,))


def kernel(x, txt, L0_tok_weight, L0_tok_bias, L0_attn_w_qkv, L0_attn_b_qkv, L0_attn_scale, L0_attn_w_proj,
           L0_attn_b_proj, L0_ffn_w1, L0_ffn_b1, L0_ffn_w2, L0_ffn_b2, L0_ffn_down_w, L0_ffn_down_b, L0_ffn_up_w,
           L0_ffn_gamma, L0_ffn_beta):
    import numpy as np
    import concourse.bacc as bacc
    from concourse.bass_utils import run_bass_kernel_spmd

    w_qkv, b_qkv = np.asarray(L0_attn_w_qkv), np.asarray(L0_attn_b_qkv)
    E = w_qkv.shape[0]
    arrays = {
        "x": x, "txt": txt, "tok_w": np.asarray(L0_tok_weight).T, "tok_bias": L0_tok_bias,
        "w_qk": by_head_pair(w_qkv), "b_qk": by_head_pair(b_qkv), "w_v": w_qkv[:, 2 * E:], "b_v": b_qkv[2 * E:],
        "scale": L0_attn_scale, "w_proj": L0_attn_w_proj, "b_proj": L0_attn_b_proj, "w1": L0_ffn_w1,
        "b1": L0_ffn_b1, "w2": L0_ffn_w2, "b2": L0_ffn_b2, "down_w": L0_ffn_down_w, "down_b": L0_ffn_down_b,
        "up_w": L0_ffn_up_w, "gamma": L0_ffn_gamma, "beta": L0_ffn_beta,
    }
    arrays = {name: np.ascontiguousarray(a) for name, a in arrays.items()}
    B, IMG_T = x.shape[0], (x.shape[2] // 16) ** 2
    nc = bacc.Bacc("TRN2", target_bir_lowering=False, num_devices=1)
    aps = [nc.dram_tensor(name, a.shape, mybir.dt.from_np(a.dtype), kind="ExternalInput").ap()
           for name, a in arrays.items()]
    out = nc.dram_tensor("out", (B, IMG_T + txt.shape[1], E), F32, kind="ExternalOutput").ap()
    early_fusion(nc, *aps, out)
    r = run_bass_kernel_spmd(nc, [arrays], core_ids=[0])
    return r.results[0]["out"]
```

```python
from contextlib import ExitStack

import concourse.bass as bass
from concourse import mybir

ALU = mybir.AluOpType
ACT = mybir.ActivationFunctionType
AX = mybir.AxisListType
F32 = mybir.dt.float32
BF16 = mybir.dt.bfloat16
F32R = mybir.dt.float32r

LN_EPS = 1e-5
GATE_EPS = 1e-8
MASK = -1e30
BANK = 512


def settled(eng, sb_const):
    eng.sem_inc(sb_const["wait_carrier"], 1)


def constants(nc, ctx):
    ident = ctx.enter_context(nc.sbuf_tensor("ident", [128, 128], F32))
    ident_bf = ctx.enter_context(nc.sbuf_tensor("ident_bf", [96, 96], BF16))
    neg_diag = ctx.enter_context(nc.sbuf_tensor("neg_diag", [96, 2, 96], BF16))
    zeroed = ctx.enter_context(nc.semaphore("c_zeroed"))
    ready = ctx.enter_context(nc.semaphore("c_ready"))
    first = ctx.enter_context(nc.semaphore("c_first"))
    names = ("bias_scaled", "dve_cleared", "gates_ready", "wait_carrier")
    extra = {n: ctx.enter_context(nc.semaphore("c_" + n)) for n in names}
    with nc.Block() as block:

        @block.gpsimd
        def _(pool):
            for tile in (ident, ident_bf, neg_diag):
                nc.gpsimd.memset(tile[:], 0.0).then_inc(zeroed, 1)
            pool.wait_ge(zeroed, 3)
            for n, (view, size, fill) in enumerate(((ident[:], 128, 1.0), (ident_bf[:], 96, 1.0),
                                                    (neg_diag[:, 0, :], 96, MASK), (neg_diag[:, 1, :], 96, MASK))):
                nc.gpsimd.affine_select(out=view, in_=view, compare_op=ALU.not_equal, fill=fill, base=0,
                                        pattern=[[-1, size]], channel_multiplier=1).then_inc(first, 1)
            pool.wait_ge(first, 4)
            nc.gpsimd.memset(neg_diag[0:1, 0, 0:1], 0.0).then_inc(ready, 1)
    return {"ident": ident, "ident_bf": ident_bf, "neg_diag": neg_diag, "ident_ready": ready, **extra}


def tokenize(nc, ctx, sems, sb_const, x, tok_w, tok_bias, tokens):
    B, Cin, HW, _ = x.shape
    P16 = 16
    NP = HW // P16
    IMG = 8
    R = IMG * NP
    G = B // IMG
    ROW = P16 * HW
    E = tok_w.shape[1] + 1
    CH = Cin * 2
    LOADED = 8 * IMG
    assert R <= 128 and G % 2 == 0 and G >= 4 and P16 * P16 == 256
    ident = sb_const["ident"]

    def sb(name, shape, dt=F32):
        return ctx.enter_context(nc.sbuf_tensor(name, shape, dt))

    def sem(name):
        return sems.enter_context(nc.semaphore(name))

    pix = [sb(f"t_pix{p}", [R, Cin, ROW]) for p in range(2)]
    patch = [sb(f"t_patch{p}", [R, Cin * P16 * P16]) for p in range(2)]
    w_sb = sb("t_w", [128, CH, E - 1])
    w_time = sb("t_w_time", [R, E - 1])
    bias_bc = sb("t_bias", [R, E - 1])
    pixT = [sb(f"t_pixT{p}", [128, CH, R]) for p in range(2)]
    time_bias = [sb(f"t_tb{p}", [R, E - 1]) for p in range(2)]
    tok = [sb(f"t_tok{p}", [R, NP, E]) for p in range(2)]
    ssq = [sb(f"t_ssq{p}", [R, NP]) for p in range(2)]
    tnew = [sb(f"t_tnew{p}", [R, NP]) for p in range(2)]
    ssz = [sb(f"t_ssz{p}", [R, NP]) for p in range(2)]
    junk = sb("t_junk", [R, Cin, P16, P16])
    junk_z = sb("t_junk_z", [R, E - 1])
    turned = [ctx.enter_context(nc.psum_tensor(f"t_turned{n}", [128, BANK], F32)) for n in range(4)]
    prod = [ctx.enter_context(nc.psum_tensor(f"t_prod{n}", [128, BANK], F32)) for n in range(2)]

    weights_in = sem("t_weights_in")
    pix_in = [sem(f"t_pix_in{p}") for p in range(2)]
    gathered = sem("t_gathered")
    sq_done = sem("t_sq_done")
    tnew_ready = sem("t_tnew_ready")
    turned_ready = sem("t_turned_ready")
    left_copied = sem("t_left_copied")
    right_copied = sem("t_right_copied")
    prod_ready = sem("t_prod_ready")
    tb_done = sem("t_tb_done")
    z_done = sem("t_z_done")
    zsq_done = sem("t_zsq_done")
    stored = [sem(f"t_stored{p}") for p in range(2)]
    zt_done = sem("t_zt_done")

    out_rows = tokens.rearrange("b (hp wp) e -> (b hp) (wp e)", wp=NP)

    with nc.Block() as block:

        @block.sync
        def _(sp):
            sp.dma_start(w_sb[:], tok_w[1:, :].rearrange("(k p) o -> p k o", p=128)).then_inc(weights_in, 16)
            sp.dma_start(w_time[:], tok_w[0:1, :].to_broadcast([R, E - 1])).then_inc(weights_in, 16)
            sp.dma_start(bias_bc[:], tok_bias.rearrange("(a o) -> a o", a=1).to_broadcast([R, E - 1])
                         ).then_inc(weights_in, 16)

            def load_group(g, p):
                for i in range(IMG):
                    src = x[bass.ds(g * IMG + i, 1)].rearrange("a c (hp f) w -> hp (a c) (f w)", f=P16)
                    sp.dma_start(pix[p][i * NP:(i + 1) * NP], src).then_inc(pix_in[p], 16)

            load_group(0, 0)
            load_group(1, 1)
            with sp.Fori(1, G // 2) as pair:
                for p in range(2):
                    g = 2 * pair + p
                    sp.wait_ge(gathered, (g - 1) * NP)
                    sp.wait_ge(sq_done, (g - 1) * NP)
                    load_group(g, p)

        @block.tensor
        def _(pe):
            pe.wait_ge(weights_in, 48)
            pe.wait_ge(sb_const["ident_ready"], 1)

            def turn(g, p, w, first):
                n = g * NP + w
                pe.wait_ge(gathered, n + 1)
                for half in range(2):
                    bank = turned[2 * (w % 2) + half]
                    if not (first and w < 2):
                        pe.wait_ge(right_copied if half else left_copied, n - 1)
                    for k in range(3):
                        j = 3 * half + k
                        last = pe.transpose(bank[:, k * R:(k + 1) * R],
                                            patch[w % 2][:, j * 128:(j + 1) * 128], ident[0:R, 0:R])
                    last.then_inc(turned_ready, 1)
                return last

            def multiply(g, w, first):
                n = g * NP + w
                pe.wait_ge(left_copied, n + 1)
                pe.wait_ge(right_copied, n + 1)
                if not (first and w < 2):
                    pe.wait_ge(z_done, n - 1)
                for k in range(CH):
                    last = pe.matmul(prod[w % 2][0:R, 0:E - 1], pixT[w % 2][:, k, :], w_sb[:, k, :],
                                     start=(k == 0), stop=(k == CH - 1))
                last.then_inc(prod_ready, 1)

            def group(g, p, first):
                for w in range(NP):
                    turn(g, p, w, first)
                    if w > 0:
                        multiply(g, w - 1, first)
                multiply(g, NP - 1, first)

            group(0, 0, True)
            group(1, 1, False)
            with pe.Fori(1, G // 2) as pair:
                group(2 * pair, 0, False)
                group(2 * pair + 1, 1, False)

        @block.vector
        def _(dve):
            def gather(g, p, w):
                n = g * NP + w
                if w == 0:
                    dve.wait_ge(pix_in[p], LOADED * g + 2 * LOADED - LOADED * p)
                if not (isinstance(n, int) and n < 2):
                    dve.wait_ge(turned_ready, 2 * n - 2)
                view = pix[p][:].rearrange("r c (py q) -> r c py q", py=P16)
                nc.vector.tensor_copy(patch[w % 2][:].rearrange("r (c py q) -> r c py q", c=Cin, py=P16),
                                      view[:, :, :, w * P16:(w + 1) * P16]).then_inc(gathered, 1)

            def group(g, p, first, last):
                for w in range(NP + 1):
                    n = g * NP + w
                    if w < NP - 1:
                        gather(g, p, w + 1)
                    elif w == NP - 1 and not last:
                        gather(g + 1, 1 - p, 0)
                    if w < NP:
                        dve.wait_ge(turned_ready, 2 * n + 1)
                        if not (first and w < 2):
                            dve.wait_ge(prod_ready, n - 1)
                        nc.vector.tensor_copy(pixT[w % 2][:, 0:3, :].rearrange("p k r -> p (k r)"),
                                              turned[2 * (w % 2)][:, 0:3 * R]).then_inc(left_copied, 1)
                        if w == 0:
                            dve.wait_ge(tnew_ready, g + 1)
                        if not (first and w < 2):
                            dve.wait_ge(z_done, n - 1)
                        nc.vector.scalar_tensor_tensor(time_bias[w % 2][:], w_time[:], tnew[p][:, w:w + 1],
                                                       bias_bc[:], ALU.mult, ALU.add).then_inc(tb_done, 1)
                    if w > 0:
                        if w == 1 and not first:
                            dve.wait_ge(stored[p], 8 * g - 8 * p)
                        dve.wait_ge(prod_ready, n)
                        dve.wait_ge(tb_done, n)
                        nc.vector.tensor_tensor(tok[p][:, w - 1, 1:E], prod[(w - 1) % 2][0:R, 0:E - 1],
                                                time_bias[(w - 1) % 2][:], ALU.add).then_inc(z_done, 1)

            dve.wait_ge(weights_in, 48)
            gather(0, 0, 0)
            group(0, 0, True, False)
            group(1, 1, False, False)
            with dve.Fori(1, G // 2 - 1) as pair:
                group(2 * pair, 0, False, False)
                group(2 * pair + 1, 1, False, False)
            group(G - 2, 0, False, False)
            group(G - 1, 1, False, True)

        @block.scalar
        def _(act):
            def square(g, p, w):
                if not (isinstance(g, int) and g * NP + w == 0):
                    act.wait_ge(sq_done, g * NP + w)
                view = pix[p][:].rearrange("r c (py q) -> r c py q", py=P16)
                nc.scalar.activation(junk[:], view[:, :, :, w * P16:(w + 1) * P16], ACT.Square,
                                     accum_out=ssq[p][:, w:w + 1]).then_inc(sq_done, 1)

            def time_features(g, p):
                act.wait_ge(sq_done, (g + 1) * NP)
                nc.scalar.activation(tnew[p][:], ssq[p][:], ACT.Sqrt, bias=1.0).then_inc(tnew_ready, 1)

            def square_tokens(g, p, w):
                n = g * NP + w
                act.wait_ge(z_done, n + 1)
                if not (isinstance(n, int) and n == 0):
                    act.wait_ge(zsq_done, n)
                nc.scalar.activation(junk_z[:], tok[p][:, w, 1:E], ACT.Square,
                                     accum_out=ssz[p][:, w:w + 1]).then_inc(zsq_done, 1)

            def group(g, p, first, last):
                for w in range(NP):
                    n = g * NP + w
                    act.wait_ge(turned_ready, 2 * n + 2)
                    if not (first and w < 2):
                        act.wait_ge(prod_ready, n - 1)
                    nc.scalar.copy(pixT[w % 2][:, 3:6, :].rearrange("p k r -> p (k r)"),
                                   turned[2 * (w % 2) + 1][:, 0:3 * R]).then_inc(right_copied, 1)
                    if w > 0:
                        square_tokens(g, p, w - 1)
                    if not last and w >= NP // 2:
                        if w == NP // 2:
                            act.wait_ge(pix_in[1 - p], LOADED * g + LOADED + 2 * LOADED - LOADED * (1 - p))
                        square(g + 1, 1 - p, 2 * w - NP)
                        square(g + 1, 1 - p, 2 * w - NP + 1)
                if not last:
                    time_features(g + 1, 1 - p)
                square_tokens(g, p, NP - 1)
                act.wait_ge(zsq_done, (g + 1) * NP)
                nc.scalar.activation(tok[p][:, :, 0], ssz[p][:], ACT.Sqrt, bias=1.0).then_inc(zt_done, 1)
                act.wait_ge(zt_done, g + 1)
                rows = out_rows[bass.ds(g * R, R)]
                act.dma_start(rows, tok[p][:].rearrange("r w e -> r (w e)")).then_inc(stored[p], 16)

            act.wait_ge(pix_in[0], 2 * LOADED)
            for w in range(NP):
                square(0, 0, w)
            time_features(0, 0)
            group(0, 0, True, False)
            group(1, 1, False, False)
            with act.Fori(1, G // 2 - 1) as pair:
                group(2 * pair, 0, False, False)
                group(2 * pair + 1, 1, False, False)
            group(G - 2, 0, False, False)
            group(G - 1, 1, False, True)
            for p in range(2):
                act.wait_ge(stored[p], 8 * G)


def attend(nc, ctx, sems, sb_const, tokens, txt, w_qk, b_qk, w_v, b_v, scale, w_proj, b_proj, mixed):
    NI, NT, E = mixed.shape
    IMG_T = tokens.shape[1]
    H = scale.shape[0]
    D = E // H
    T = 3
    TP = 96
    LAST = NT - (T - 1) * TP
    PAD = T * TP
    F2 = E // 96
    HH = 96 // D
    QS = [0, 1, 2, 0, 1, 0]
    KS = [0, 0, 0, 1, 1, 2]
    KROWS = 6 * D
    SROWS = KROWS + 2
    STRIP = 32
    HG = 4
    NG = H // HG
    assert E == 192 and D == 16 and H == 12 and 0 < LAST <= TP and IMG_T == 2 * TP + 4 and NI % 3 == 1 and NI > 9
    ident, ident_bf, neg_diag = sb_const["ident"], sb_const["ident_bf"], sb_const["neg_diag"]

    def sb(name, shape, dt=F32):
        return ctx.enter_context(nc.sbuf_tensor(name, shape, dt))

    def sem(name):
        return sems.enter_context(nc.semaphore(name))

    def ps(name):
        return ctx.enter_context(nc.psum_tensor(name, [128, BANK], F32))

    w_qk_sb = sb("a_wqk", [96, F2, 2 * E])
    w_v_sb = sb("a_wv", [96, F2, E])
    w_p_sb = sb("a_wp", [96, F2, E])
    bqk = sb("a_bqk", [96, 4])
    bqk_s = sb("a_bqks", [96, 4])
    scl = sb("a_scl", [96, 2])
    bv = sb("a_bv", [96, F2])
    bp_bc = sb("a_bp", [96, T, E])
    minus_half = sb("a_mh", [96, T])
    h_front = [sb(f"a_hf{r}", [96, T, E]) for r in range(3)]
    h_res = [sb(f"a_hr{r}", [96, T, E]) for r in range(3)]
    h_out = [sb(f"a_ho{r}", [96, T, E]) for r in range(3)]
    bst = sb("a_bst", [96, T, 6])
    mv = sb("a_mv", [96, T, 2])
    veps = sb("a_veps", [96, T])
    rstd = sb("a_rstd", [96, T])
    hn = sb("a_hn", [96, T, E])
    hnT = sb("a_hnT", [96, F2, PAD])
    qk = sb("a_qk", [96, 4, NT])
    qk_rest = sb("a_qkr", [96, 4, NT])
    parts = sb("a_parts", [96, 3, 4, NT], BF16)
    q_st = [sb(f"a_qst{r}", [SROWS, H, PAD], BF16) for r in range(3)]
    k_st = [sb(f"a_kst{r}", [SROWS, H, PAD], BF16) for r in range(3)]
    v_st = [sb(f"a_vst{r}", [96, T, H, STRIP]) for r in range(3)]
    mx = sb("a_mx", [96, T, H])
    m_hi = [sb(f"a_mhi{a}", [H // 2, PAD], BF16) for a in range(2)]
    m_lo = [sb(f"a_mlo{a}", [H // 2, PAD], BF16) for a in range(2)]
    prob = [sb(f"a_p{g}", [96, HG, T, NT]) for g in range(NG)]
    oT = sb("a_oT", [128, NG, PAD])
    rden = sb("a_rden", [96, T, H])
    on = sb("a_on", [96, T, E])
    onT = sb("a_onT", [96, F2, PAD])

    st = ctx.enter_context(nc.psum_tensor("a_st", [128, T, BANK], F32))
    sm = ctx.enter_context(nc.psum_tensor("a_sm", [128, T, BANK], F32))
    work = [ps(f"a_work{b}") for b in range(2)]

    weights_in = sem("a_weights_in")
    cleared = sem("a_cleared")
    hf_in = [sem(f"a_hf_in{r}") for r in range(3)]
    hr_in = [sem(f"a_hr_in{r}") for r in range(3)]
    stats = sem("a_stats")
    pool_own = sem("a_pool_own")
    hn_ready = sem("a_hn_ready")
    res_ready = sem("a_res_ready")
    work_ready = sem("a_work_ready")
    work_free = [sem(f"a_work_free{b}") for b in range(2)]
    split = sem("a_split")
    stack_in = [sem(f"a_stack_in{r}") for r in range(3)]
    sm_ready = sem("a_sm_ready")
    max_done = sem("a_max_done")
    m_split = [sem(f"a_m_split{a}") for a in range(2)]
    m_ready = [sem(f"a_m_ready{a}") for a in range(2)]
    m_in = [[sem(f"a_m_in{r}{a}") for a in range(2)] for r in range(3)]
    st_ready = sem("a_st_ready")
    exp_done = sem("a_exp_done")
    rd_done = sem("a_rd_done")
    h2_done = sem("a_h2_done")
    stored = [sem(f"a_stored{r}") for r in range(3)]

    FRONT = ["t0", "t1", "q0", "q1", "q2", "q3", "v0", "v1"]
    CORE = ["m1", "x0", "x1"]
    FINISH = ["x2", "o0", "o1", "o2", "n0", "n1", "p0", "p1"]
    BEFORE = ["t0", "q0", "q1", "q2", "q3", "o2", "n0", "v0", "v1", "p1", None, None]
    AFTER = ["t1", "x2", "m1", "o0", "o1", "x0", "n1", "m0", "p0", "x1", None, None]
    ORDER = [u for pair in zip(BEFORE, AFTER) for u in pair if u]
    assert sorted(ORDER) == sorted(FRONT + CORE + FINISH + ["m0"]) and len(ORDER) % 2 == 0
    NEEDS = {"q0": "t1", "q1": "t1", "q2": "t1", "q3": "t1", "v0": "t1", "v1": "t1", "o0": "x2", "o1": "x2",
             "o2": "x2", "n0": "o2", "n1": "o2", "p0": "n1", "p1": "n1"}

    class Step:

        def __init__(self, k, r):
            self.s = 3 * k + r
            fixed = isinstance(k, int)
            self.front = self._img(k, r, 0) if not fixed or self.s < NI else None
            self.maxima = self._img(k, r, 1) if not fixed or 1 <= self.s <= NI else None
            self.core = self._img(k, r, 2) if not fixed or 2 <= self.s <= NI + 1 else None
            self.finish = self._img(k, r, 3) if not fixed or 3 <= self.s <= NI + 2 else None
            self.next = self._img(k, r, -1) if not fixed or self.s + 1 < NI else None
            self.next_finish = self._img(k, r, 2) if not fixed or 2 <= self.s <= NI + 1 else None
            if fixed:
                clip = lambda v: max(0, min(v, NI))
                self.base = (8 * clip(self.s) + clip(self.s - 1) + 3 * clip(self.s - 2) + 8 * clip(self.s - 3), 0)
            else:
                self.base = (-31, 20)

        @staticmethod
        def _img(k, r, back):
            q, rr = divmod(r - back, 3)
            return 3 * k + r - back, k + q, rr

        def has(self, unit):
            stage = (self.front if unit in FRONT else self.finish if unit in FINISH
                     else self.core if unit in CORE else self.maxima)
            return stage is not None

        def at(self, unit):
            return self.base[0] + sum(self.has(u) for u in ORDER[:ORDER.index(unit)])

        def seq(self, unit):
            return self.at(unit) + self.base[1] * self.s

        def bank(self, unit):
            return self.at(unit) % 2

        def turns(self, unit):
            return self.at(unit) // 2 + self.base[1] // 2 * self.s

    def steps(engine, do):
        for s in range(6):
            do(Step(s // 3, s % 3))
        with engine.Fori(2, (NI - 1) // 3) as k:
            for r in range(3):
                do(Step(k, r))
        for s in range(NI - 1, NI + 3):
            do(Step(s // 3, s % 3))

    def wait(eng, semaphore, value):
        if not (isinstance(value, int) and value <= 0):
            eng.wait_ge(semaphore, value)

    with nc.Block() as block:

        @block.sync
        def _(sp):
            def dma(out, in_, semaphore, **kw):
                sp.dma_start(out, in_, **kw).then_inc(semaphore, 16)

            dma(w_qk_sb[:], w_qk.rearrange("(f p) o -> p f o", p=96), weights_in)
            dma(w_v_sb[:], w_v.rearrange("(f p) o -> p f o", p=96), weights_in)
            dma(w_p_sb[:], w_proj.rearrange("(f p) o -> p f o", p=96), weights_in)
            dma(bqk[:], b_qk.rearrange("(m p) -> p m", p=96), weights_in, allow_slow_non_contiguous=True)
            dma(bv[:], b_v.rearrange("(f p) -> p f", p=96), weights_in, allow_slow_non_contiguous=True)
            for d in range(D):
                dma(scl[d * HH:(d + 1) * HH, :], scale.rearrange("(h m) -> h m", m=2), weights_in)
            for t in range(T):
                dma(bp_bc[:, t, :], b_proj.rearrange("(a o) -> a o", a=1).to_broadcast([96, E]), weights_in)

            def load_tokens(dst, n, semaphore):
                img = tokens[bass.ds(n, 1)].rearrange("a t e -> (a t) e")
                dma(dst[:, 0:2, :], img[0:2 * TP].rearrange("(t p) e -> p t e", p=TP), semaphore)
                dma(dst[0:IMG_T - 2 * TP, 2, :], img[2 * TP:IMG_T], semaphore)
                dma(dst[IMG_T - 2 * TP:LAST, 2, :], txt[bass.ds(n, 1)].rearrange("a t e -> (a t) e"), semaphore)

            def spread(stack, which, part, slots, r):
                for slot, p in enumerate(slots):
                    if p == part:
                        src = parts[:, part, 2 * which:2 * which + 2, :]
                        dma(stack[r][slot * D:(slot + 1) * D, :, 0:NT], src, stack_in[r])

            def step(st_):
                if st_.next is not None:
                    n, k, r = st_.next
                    wait(sp, hn_ready, T * (n - 2))
                    load_tokens(h_front[r], n, hf_in[r])
                if st_.next_finish is not None:
                    n, k, r = st_.next_finish
                    wait(sp, h2_done, 2 * (n - 2))
                    load_tokens(h_res[r], n, hr_in[r])
                if st_.core is not None:
                    minus_max(st_.core, 1)
                if st_.front is not None:
                    n, k, r = st_.front
                    wait(sp, st_ready, H * (n - 2))
                    for part, ops in ((0, 1), (1, 3), (2, 4)):
                        if part == 2 and st_.maxima is not None:
                            minus_max(st_.maxima, 0)
                        sp.wait_ge(split, 4 * n + ops)
                        spread(q_st, 0, part, QS, r)
                        spread(k_st, 1, part, KS, r)
                elif st_.maxima is not None:
                    minus_max(st_.maxima, 0)
                if st_.finish is not None:
                    n, k, r = st_.finish
                    sp.wait_ge(h2_done, 2 * n + 2)
                    img = mixed[bass.ds(n, 1)].rearrange("a t e -> (a t) e")
                    dma(img[0:2 * TP].rearrange("(t p) e -> p t e", p=TP), h_out[r][:, 0:2, :], stored[r])
                    dma(img[2 * TP:NT], h_out[r][0:LAST, 2, :], stored[r])

            def minus_max(image, a):
                n, k, r = image
                sp.wait_ge(m_ready[a], n + 1)
                for row, m in ((KROWS, m_hi), (KROWS + 1, m_lo)):
                    dst = q_st[r][row:row + 1, a * H // 2:(a + 1) * H // 2, 0:NT]
                    dma(dst, m[a][:, 0:NT], m_in[r][a])

            sp.wait_ge(cleared, 2)
            load_tokens(h_front[0], 0, hf_in[0])
            steps(sp, step)
            for r in range(3):
                sp.wait_ge(stored[r], 32 * len(range(r, NI, 3)))

        @block.gpsimd
        def _(pool):
            nc.gpsimd.memset(minus_half[:], -0.5)
            for r in range(3):
                nc.gpsimd.memset(v_st[r][:], 0.0).then_inc(pool_own, 1)
            for r in range(3):
                pool.wait_ge(pool_own, 3)
                nc.gpsimd.memset(v_st[r][:, :, :, D:D + 1], 1.0).then_inc(pool_own, 1)
            for r in range(3):
                pool.wait_ge(pool_own, 6)
                ones = v_st[r][:, T - 1, :, D]
                last = nc.gpsimd.affine_select(out=ones, in_=ones, compare_op=ALU.is_ge, fill=0.0, base=LAST - 1,
                                               pattern=[[0, H]], channel_multiplier=-1)
                last.then_inc(pool_own, 1)
            pool.wait_ge(pool_own, 9)
            pool.nop().then_inc(cleared, 1)
            OWN = 9

            def normalise(image, st_):
                n, k, r = image
                pool.wait_ge(stats, 2 * T * (n + 1))
                settled(pool, sb_const)
                nc.gpsimd.tensor_scalar(veps[:], mv[:, :, 1], LN_EPS, None, ALU.add).then_inc(pool_own, 1)
                pool.wait_ge(pool_own, OWN + 2 * n + 1)
                nc.gpsimd.tensor_tensor(rstd[:], veps[:], minus_half[:], ALU.pow).then_inc(pool_own, 1)
                pool.wait_ge(pool_own, OWN + 2 * n + 2)
                if st_ is not None:
                    pool.wait_ge(work_ready, st_.seq("t1") + 1)
                settled(pool, sb_const)
                for t in range(T):
                    nc.gpsimd.tensor_scalar(hn[:, t, :], h_front[r][:, t, :], mv[:, t, 0:1], rstd[:, t:t + 1],
                                            ALU.subtract, ALU.mult).then_inc(hn_ready, 1)

            def step(st_):
                if st_.finish is not None:
                    n, k, r = st_.finish
                    pool.wait_ge(hr_in[r], 48 * (k + 1))
                    nc.gpsimd.tensor_tensor(h_res[r][:], h_res[r][:], bp_bc[:], ALU.add).then_inc(res_ready, 1)
                if st_.next is not None:
                    normalise(st_.next, st_)

            pool.wait_ge(weights_in, 16 * (5 + D + T))
            normalise((0, 0, 0), None)
            steps(pool, step)

        @block.tensor
        def _(pe):
            def unit(name, st_):
                if name is None or not st_.has(name):
                    return
                wb = work[st_.bank(name)]
                wait(pe, work_free[st_.bank(name)], st_.turns(name))
                if name in NEEDS:
                    made_from = NEEDS[name]
                    pe.wait_ge(work_free[st_.bank(made_from)], st_.turns(made_from) + 1)
                kind, j = name[0], int(name[1])
                if kind == "t":
                    if j == 0:
                        pe.wait_ge(hn_ready, T * (st_.front[0] + 1))
                    for t in range(T):
                        last = pe.transpose(wb[0:96, t * TP:(t + 1) * TP], hn[:, t, j * 96:(j + 1) * 96],
                                            ident[0:96, 0:96])
                elif kind == "q":
                    for f in range(F2):
                        last = pe.matmul(wb[0:96, 0:NT], w_qk_sb[:, f, j * 96:(j + 1) * 96], hnT[:, f, 0:NT],
                                         start=(f == 0), stop=(f == F2 - 1))
                elif kind == "m":
                    n = (st_.core if j else st_.maxima)[0]
                    pe.wait_ge(max_done, H * n + (j + 1) * H // 2)
                    for t in range(T):
                        last = pe.transpose(wb[0:H // 2, t * TP:(t + 1) * TP],
                                            mx[:, t, j * H // 2:(j + 1) * H // 2], ident[0:96, 0:96])
                elif kind == "x":
                    n, k, r = st_.finish if j == 2 else st_.core
                    pe.wait_ge(exp_done, H * n + HG * (j + 1))
                    for t in range(T):
                        for i in range(HG):
                            last = pe.matmul(wb[i * STRIP:(i + 1) * STRIP, 0:NT], v_st[r][:, t, HG * j + i, :],
                                             prob[j][:, i, t, :], start=(t == 0), stop=(t == T - 1))
                elif kind == "o":
                    for g in range(NG):
                        last = pe.transpose(wb[0:96, g * 128:(g + 1) * 128], oT[:, g, j * TP:(j + 1) * TP],
                                            ident[:, :])
                elif kind == "n":
                    for t in range(T):
                        last = pe.transpose(wb[0:96, t * TP:(t + 1) * TP], on[:, t, j * 96:(j + 1) * 96],
                                            ident[0:96, 0:96])
                else:
                    left, w = (hnT, w_v_sb) if kind == "v" else (onT, w_p_sb)
                    for i, t in enumerate(([0, 1], [2])[j]):
                        for f in range(F2):
                            last = pe.matmul(wb[0:96, i * E:(i + 1) * E], left[:, f, t * TP:(t + 1) * TP], w[:, f, :],
                                             start=(f == 0), stop=(f == F2 - 1))
                last.then_inc(work_ready, 1)

            def scores(bank, left, right, rows, h, done):
                for t in range(T):
                    width = min(TP, NT - t * TP)
                    pe.matmul(bank[0:96, t, 0:NT], left[0:rows, h, t * TP:(t + 1) * TP], right[0:rows, h, 0:NT],
                              start=True, stop=False)
                    last = pe.matmul(bank[0:96, t, t * TP:t * TP + width], ident_bf[0:96, 0:96],
                                     neg_diag[0:96, 0 if t == 0 else 1, 0:width], start=False, stop=True)
                last.then_inc(done, 1)

            def step(st_):
                for h in range(H):
                    if st_.core is not None:
                        n, k, r = st_.core
                        wait(pe, exp_done, H * n + h)
                        if h % (H // 2) == 0:
                            pe.wait_ge(m_in[r][h // (H // 2)], 32 * (k + 1))
                        scores(st, k_st[r], q_st[r], SROWS, h, st_ready)
                    unit(BEFORE[h], st_)
                    if st_.maxima is not None:
                        n, k, r = st_.maxima
                        if h == 0:
                            pe.wait_ge(stack_in[r], 16 * 12 * (k + 1))
                        wait(pe, max_done, H * n + h)
                        scores(sm, q_st[r], k_st[r], KROWS, h, sm_ready)
                    unit(AFTER[h], st_)

            pe.wait_ge(weights_in, 16 * (5 + D + T))
            pe.wait_ge(cleared, 2)
            steps(pe, step)

        @block.scalar
        def _(act):
            def unit(name, st_):
                if name is None or not st_.has(name) or name[0] not in "tqvnx":
                    return
                act.wait_ge(work_ready, st_.seq(name) + 1)
                kind, j = name[0], int(name[1])
                wb = work[st_.bank(name)]
                if kind == "x":
                    ins = nc.scalar.copy(oT[:, j, 0:NT], wb[:, 0:NT])
                elif kind == "t":
                    ins = nc.scalar.copy(hnT[:, j, :], wb[0:96, 0:PAD])
                elif kind == "q":
                    wait(act, split, 4 * st_.front[0])
                    ins = nc.scalar.activation(qk[:, j, :], wb[0:96, 0:NT], ACT.Identity, bias=bqk_s[:, j:j + 1],
                                               scale=scl[:, j:j + 1] if j < 2 else 1.0)
                elif kind == "n":
                    ins = nc.scalar.activation(onT[:, j, :], wb[0:96, 0:PAD], ACT.Identity, bias=bv[:, j:j + 1])
                else:
                    t0, nt = ((0, 2), (2, 1))[j]
                    dst = v_st[st_.front[2]][:, t0:t0 + nt, :, 0:D]
                    ins = nc.scalar.copy(dst, wb[0:96, 0:nt * E].rearrange("p (t h d) -> p t h d", t=nt, d=D))
                ins.then_inc(work_free[st_.bank(name)], 1)

            def head_exp(h, st_):
                n, k, r = st_.core
                act.wait_ge(st_ready, H * n + h + 1)
                nc.scalar.activation(prob[h // HG][:, h % HG], st[0:96, :, 0:NT], ACT.Exp).then_inc(exp_done, 1)

            def step(st_):
                for h in range(H):
                    if st_.core is not None:
                        head_exp(h, st_)
                    unit(BEFORE[h], st_)
                    unit(AFTER[h], st_)

            act.wait_ge(weights_in, 16 * (5 + D + T))
            act.wait_ge(cleared, 2)
            nc.scalar.copy(bqk_s[:, 2:4], bqk[:, 2:4]).then_inc(sb_const["bias_scaled"], 1)
            for m in range(2):
                nc.scalar.activation(bqk_s[:, m:m + 1], bqk[:, m:m + 1], ACT.Identity,
                                     scale=scl[:, m:m + 1]).then_inc(sb_const["bias_scaled"], 1)
            act.wait_ge(sb_const["bias_scaled"], 3)
            steps(act, step)

        @block.vector
        def _(dve):
            for r in range(3):
                for tile in (h_front[r], h_res[r], q_st[r], k_st[r]):
                    nc.vector.memset(tile[:], 0.0).then_inc(sb_const["dve_cleared"], 1)
            nc.vector.memset(oT[:], 1.0).then_inc(sb_const["dve_cleared"], 1)
            for r in range(3):
                dve.wait_ge(sb_const["dve_cleared"], 13)
                last = nc.vector.memset(k_st[r][KROWS:SROWS, :, 0:NT], 1.0)
                if r == 2:
                    last.then_inc(cleared, 1)

            def statistics(image):
                n, k, r = image
                dve.wait_ge(hf_in[r], 48 * (k + 1))
                wait(dve, hn_ready, T * n)
                for t in range(T):
                    nc.vector.bn_stats(bst[:, t, :], h_front[r][:, t, :]).then_inc(stats, 1)
                dve.wait_ge(stats, 2 * T * n + T)
                settled(dve, sb_const)
                for t in range(T):
                    nc.vector.bn_aggr(mv[:, t, :], bst[:, t, :]).then_inc(stats, 1)

            def unit(name, st_):
                if name is None or not st_.has(name) or name[0] not in "mop":
                    return
                dve.wait_ge(work_ready, st_.seq(name) + 1)
                kind, j = name[0], int(name[1])
                wb, free = work[st_.bank(name)], work_free[st_.bank(name)]
                if kind == "m":
                    n, k, r = st_.core if j else st_.maxima
                    if not (isinstance(n, int) and n == 0):
                        rr, kk = (r - 1) % 3, (k if r > 0 else k - 1)
                        dve.wait_ge(m_in[rr][j], 32 * (kk + 1))
                    nc.vector.tensor_scalar(m_hi[j][:], wb[0:H // 2, 0:PAD], -1.0, None, ALU.mult
                                            ).then_inc(m_split[j], 1)
                    dve.wait_ge(m_split[j], n + 1)
                    nc.vector.scalar_tensor_tensor(m_lo[j][:], wb[0:H // 2, 0:PAD], -1.0, m_hi[j][:],
                                                   ALU.mult, ALU.subtract).then_inc(m_ready[j], 1)
                    dve.wait_ge(m_ready[j], n + 1)
                    dve.sem_inc(free, 1)
                elif kind == "o":
                    n, k, r = st_.finish
                    heads = wb[0:96, 0:H * STRIP].rearrange("p (h c) -> p h c", c=STRIP)
                    nc.vector.reciprocal(rden[:, j, :], heads[:, :, D]).then_inc(rd_done, 1)
                    dve.wait_ge(rd_done, T * n + j + 1)
                    nc.vector.tensor_tensor(on[:, j, :].rearrange("p (h d) -> p h d", d=D), heads[:, :, 0:D],
                                            rden[:, j, :].unsqueeze(2).to_broadcast([96, H, D]), ALU.mult
                                            ).then_inc(free, 1)
                else:
                    n, k, r = st_.finish
                    if j == 0:
                        dve.wait_ge(res_ready, n + 1)
                        wait(dve, stored[r], 32 * k)
                    t0, nt = ((0, 2), (2, 1))[j]
                    ins = nc.vector.tensor_tensor(h_out[r][:, t0:t0 + nt, :].rearrange("p t e -> p (t e)"),
                                                  wb[0:96, 0:nt * E],
                                                  h_res[r][:, t0:t0 + nt, :].rearrange("p t e -> p (t e)"), ALU.add)
                    ins.then_inc(h2_done, 1)
                    dve.wait_ge(h2_done, 2 * n + j + 1)
                    dve.sem_inc(free, 1)

            def split_part(i, st_):
                n, k, r = st_.front
                if i == 0:
                    for q in ("q2", "q3"):
                        dve.wait_ge(work_free[st_.bank(q)], st_.turns(q) + 1)
                    if not (isinstance(n, int) and n == 0):
                        rr, kk = (r - 1) % 3, (k if r > 0 else k - 1)
                        dve.wait_ge(stack_in[rr], 192 * (kk + 1))
                else:
                    dve.wait_ge(split, 4 * n + i)
                if i == 0:
                    ins = nc.vector.tensor_copy(parts[:, 0], qk[:])
                elif i == 1:
                    ins = nc.vector.tensor_tensor(qk_rest[:], qk[:], parts[:, 0], ALU.subtract)
                elif i == 2:
                    ins = nc.vector.tensor_copy(parts[:, 1], qk_rest[:])
                else:
                    ins = nc.vector.tensor_tensor(parts[:, 2], qk_rest[:], parts[:, 1], ALU.subtract)
                ins.then_inc(split, 1)

            def step(st_):
                for h in range(H):
                    unit(BEFORE[h], st_)
                    if st_.maxima is not None:
                        n, k, r = st_.maxima
                        dve.wait_ge(sm_ready, H * n + h + 1)
                        nc.vector.tensor_reduce(mx[:, :, h], sm[0:96, :, 0:NT], AX.X, ALU.max).then_inc(max_done, 1)
                    unit(AFTER[h], st_)
                    if st_.front is not None and 5 <= h < 9:
                        split_part(h - 5, st_)
                    if st_.next is not None and h == 3:
                        statistics(st_.next)

            dve.wait_ge(cleared, 2)
            statistics((0, 0, 0))
            steps(dve, step)


def mix_experts(nc, ctx, sems, sb_const, mixed, w1, b1, w2, b2, down_w, down_b, up_w, gamma, beta, out):
    NE, E, DH = down_w.shape
    RH = w1.shape[1]
    TP, T = 112, 4
    N = TP * T
    src = mixed.rearrange("b t e -> (b t) e")
    dst = out.rearrange("b t e -> (b t) e")
    NTILE = src.shape[0] // N
    F2, M2 = E // 96, DH // 128
    TOP_K = 2
    assert src.shape[0] == NTILE * N and NTILE >= 7 and E == 192 and RH == 96
    ident = sb_const["ident"]

    def sb(name, shape, dt=F32):
        return ctx.enter_context(nc.sbuf_tensor(name, shape, dt))

    def sem(name):
        return sems.enter_context(nc.semaphore(name))

    def ps(name):
        return ctx.enter_context(nc.psum_tensor(name, [128, BANK], F32))

    raw = sb("m_raw", [128, NE * F2 * DH])
    w_top = [sb(f"m_w_top{a}", [128, F2 * DH]) for a in range(2)]
    down_high = sb("m_down_high", [96, NE, F2, DH], F32R)
    down_low = sb("m_down_low", [96, NE, F2, DH], F32R)
    up_high = sb("m_up_high", [128, NE, M2, E], F32R)
    up_low = sb("m_up_low", [128, NE, M2, E], F32R)
    down_b_sb = sb("m_downb", [128, NE, M2])
    w1_sb = sb("m_w1", [96, F2, RH])
    b1_sb = sb("m_b1", [RH, 1])
    w2_sb = sb("m_w2", [RH, NE])
    b2_bc = sb("m_b2", [TP, T, NE])
    gamma_bc = sb("m_gamma", [TP, T, E])
    beta_bc = sb("m_beta", [TP, T, E])
    minus_half = sb("m_mh", [TP, T])
    lower = sb("m_lower", [TP, NE, NE])
    h_in = [sb(f"m_h{p}", [TP, T, E]) for p in range(2)]
    h_beta = [sb(f"m_hb{p}", [TP, T, E]) for p in range(2)]
    xn = [sb(f"m_x{p}", [TP, T, E]) for p in range(2)]
    xT = [sb(f"m_xT{p}", [96, F2, N]) for p in range(2)]
    x_top = sb("m_x_top", [96, F2, N])
    xT_high = [sb(f"m_xTh{p}", [96, F2, N], F32R) for p in range(2)]
    xT_low = [sb(f"m_xTl{p}", [96, F2, N], F32R) for p in range(2)]
    uT = sb("m_uT", [RH, N])
    bst = sb("m_bst", [TP, T, 6])
    mv = sb("m_mv", [TP, T, 2])
    rstd = sb("m_rstd", [TP, T, 2])
    fst = sb("m_fst", [TP, T, 6])
    fmv = sb("m_fmv", [TP, T, 2])
    frstd = sb("m_frstd", [TP, T, 2])
    logits = sb("m_logits", [TP, T, NE])
    lmax = sb("m_lmax", [TP, T])
    shifted = sb("m_shifted", [TP, T, NE])
    ex = sb("m_ex", [TP, T, NE])
    total = sb("m_total", [TP, T])
    rtotal = sb("m_rtotal", [TP, T])
    routing = sb("m_routing", [TP, T, NE])
    above = sb("m_above", [TP, T, NE, NE])
    equal = sb("m_equal", [TP, T, NE, NE])
    tie = sb("m_tie", [TP, T, NE, NE])
    ahead = sb("m_ahead", [TP, T, NE, NE])
    rank = sb("m_rank", [TP, T, NE])
    sparse = sb("m_sparse", [TP, T, NE])
    kept = sb("m_kept", [TP, T])
    kept_eps = sb("m_kept_eps", [TP, T])
    rkept = sb("m_rkept", [TP, T])
    gates = [sb(f"m_gates{p}", [TP, T, NE]) for p in range(2)]
    z = [sb(f"m_z{a}", [128, M2, N]) for a in range(2)]
    z_top = [sb(f"m_z_top{a}", [128, M2, N]) for a in range(2)]
    z_high = [sb(f"m_zh{a}", [128, M2, N], F32R) for a in range(2)]
    z_low = [sb(f"m_zl{a}", [128, M2, N], F32R) for a in range(2)]
    acc = [sb(f"m_acc{p}", [TP, T, E]) for p in range(2)]
    y = [sb(f"m_y{p}", [TP, T, E]) for p in range(2)]

    hid = [ps(f"m_hid{n}") for n in range(4)]
    upb = [ps(f"m_up{n}_ps") for n in range(2)]
    fb = [ps(f"m_front{n}") for n in range(2)]

    weights_in = sem("m_weights_in")
    lower_ready = sem("m_lower_ready")
    h_loaded = [sem(f"m_h_in{p}") for p in range(2)]
    stats = sem("m_stats")
    pool_own = sem("m_pool_own")
    xn_ready = sem("m_xn_ready")
    hb_ready = sem("m_hb_ready")
    front_ready = sem("m_front_ready")
    front_free = sem("m_front_free")
    gate_step = sem("m_gate_step")
    ex_ready = sem("m_ex_ready")
    hid_ready = sem("m_hid_ready")
    z_ready = sem("m_z_ready")
    z_top_ready = sem("m_z_top_ready")
    z_high_ready = sem("m_z_high_ready")
    z_low_ready = sem("m_z_low_ready")
    z_low_rest = sem("m_z_low_rest")
    x_top_ready = sem("m_x_top_ready")
    x_high_ready = sem("m_x_high_ready")
    x_low_ready = sem("m_x_low_ready")
    raw_in = [sem("m_raw_in_down"), sem("m_raw_in_up")]
    w_top_ready = sem("m_w_top_ready")
    w_high = sem("m_w_high")
    w_low = sem("m_w_low")
    up_ready = sem("m_up_ready")
    acc_done = sem("m_acc_done")
    fstats = sem("m_fstats")
    final = sem("m_final")
    stored = [sem(f"m_stored{p}") for p in range(2)]
    GATE_OPS = 15
    FINAL_OPS = 5

    class Step:

        def __init__(self, k, p):
            self.s = 2 * k + p
            self.first = isinstance(self.s, int) and self.s == 0
            fixed = isinstance(k, int)
            self.next = self._tile(k, p, -1) if not fixed or self.s + 1 < NTILE else None
            self.front = self._tile(k, p, 0) if not fixed or self.s < NTILE else None
            self.experts = self._tile(k, p, 1) if not fixed or 1 <= self.s <= NTILE else None
            self.end = self._tile(k, p, 2) if not fixed or 2 <= self.s <= NTILE + 1 else None

        @staticmethod
        def _tile(k, p, back):
            q, pp = divmod(p - back, 2)
            return 2 * k + p - back, k + q, pp

    LOOPS = (NTILE - 1) // 2

    def steps(engine, do):
        for s in range(4):
            do(Step(s // 2, s % 2))
        with engine.Fori(2, LOOPS) as k:
            for p in range(2):
                do(Step(k, p))
        for s in range(2 * LOOPS, NTILE + 2):
            do(Step(s // 2, s % 2))

    def wait(eng, semaphore, value):
        if not (isinstance(value, int) and value <= 0):
            eng.wait_ge(semaphore, value)

    N_WEIGHTS = 5 + 2 * T + T
    RAW_PARTS = 2

    raw_down = raw[0:96].rearrange("p (n f o) -> p n f o", n=NE, f=F2)
    raw_up = raw[:, 0:NE * M2 * E].rearrange("p (n m o) -> p n m o", n=NE, m=M2)

    def weight_parts(i):
        which, e = divmod(i, NE)
        raw_w, high, low = ((raw_down, down_high, down_low), (raw_up, up_high, up_low))[which]
        rows, size = high.shape[0], high.shape[2] * high.shape[3]
        top = w_top[i % 2][0:rows, 0:size].rearrange("p (a o) -> p a o", a=2)
        return which, raw_w[:, e], top, high[:, e], low[:, e]

    def high_bits(engine, o, i):
        return engine.tensor_scalar(o.bitcast(mybir.dt.uint32), i.bitcast(mybir.dt.uint32), 0xFFFFF000, None,
                                    ALU.bitwise_and)

    def three_passes(pe, o, left, right, chunks):
        pairs = [(k, a, b) for a, b in ((0, 1), (1, 0), (0, 0)) for k in range(chunks)]
        for i, (k, a, b) in enumerate(pairs):
            last = pe.matmul(o, left[a](k), right[b](k),
                             start=(i == 0), stop=(i == len(pairs) - 1))
        return last

    with nc.Block() as block:

        @block.sync
        def _(sp):
            def dma(o, i, semaphore, **kw):
                sp.dma_start(o, i, **kw).then_inc(semaphore, 16)

            def load(tile):
                n, k, p = tile
                rows = src[bass.ds(n * N, N)].rearrange("(t p) e -> p t e", p=TP)
                dma(h_in[p][:], rows, h_loaded[p])

            load((0, 0, 0))
            for f in range(F2):
                dma(raw_down[:, :, f, :], down_w[:, f * 96:(f + 1) * 96, :].rearrange("n p o -> p n o"), raw_in[0])
            dma(w1_sb[:], w1.rearrange("(f p) o -> p f o", p=96), weights_in)
            dma(b1_sb[:], b1.rearrange("(p a) -> p a", a=1), weights_in)
            dma(w2_sb[:], w2, weights_in)
            for m in range(M2):
                dma(down_b_sb[:, :, m], down_b[:, m * 128:(m + 1) * 128].rearrange("n p -> p n"), weights_in,
                    allow_slow_non_contiguous=True)
            for t in range(T):
                for row, tile, size in ((gamma, gamma_bc, E), (beta, beta_bc, E), (b2, b2_bc, NE)):
                    dma(tile[:, t, :], row.rearrange("(a o) -> a o", a=1).to_broadcast([TP, size]), weights_in)

            sp.wait_ge(w_low, NE)
            for m in range(M2):
                dma(raw_up[:, :, m, :], up_w[:, m * 128:(m + 1) * 128, :].rearrange("n p o -> p n o"), raw_in[1])

            def step(st):
                if st.next is not None:
                    n, k, p = st.next
                    wait(sp, xn_ready, T * (n - 1))
                    wait(sp, hb_ready, n - 1)
                    load(st.next)
                if st.end is not None:
                    n, k, p = st.end
                    sp.wait_ge(final, FINAL_OPS * (n + 1))
                    rows = dst[bass.ds(n * N, N)].rearrange("(t p) e -> p t e", p=TP)
                    dma(rows, y[p][:], stored[p])

            steps(sp, step)
            for p in range(2):
                sp.wait_ge(stored[p], 16 * len(range(p, NTILE, 2)))

        @block.gpsimd
        def _(pool):
            nc.gpsimd.memset(minus_half[:], -0.5).then_inc(lower_ready, 1)
            nc.gpsimd.memset(lower[:], 1.0).then_inc(lower_ready, 1)
            pool.wait_ge(lower_ready, 2)
            nc.gpsimd.affine_select(out=lower[:], in_=lower[:], compare_op=ALU.is_gt, fill=0.0, base=0,
                                    pattern=[[1, NE], [-1, NE]], channel_multiplier=0).then_inc(lower_ready, 1)

            def deviation(tile):
                n, k, p = tile
                pool.wait_ge(stats, 2 * T * (n + 1))
                settled(pool, sb_const)
                nc.gpsimd.tensor_scalar(rstd[:, :, 0], mv[:, :, 1], LN_EPS, None, ALU.add).then_inc(pool_own, 1)
                pool.wait_ge(pool_own, 2 * n + 1)
                nc.gpsimd.tensor_tensor(rstd[:, :, 1], rstd[:, :, 0], minus_half[:], ALU.pow).then_inc(pool_own, 1)

            def residual(tile):
                n, k, p = tile
                wait(pool, final, FINAL_OPS * (n - 1))
                nc.gpsimd.tensor_tensor(h_beta[p][:], h_in[p][:], beta_bc[:], ALU.add).then_inc(hb_ready, 1)

            def finish(tile, part):
                n, k, p = tile
                if part == 0:
                    pool.wait_ge(fstats, 2 * T * (n + 1))
                    settled(pool, sb_const)
                    nc.gpsimd.tensor_scalar(frstd[:, :, 0], fmv[:, :, 1], LN_EPS, None, ALU.add).then_inc(final, 1)
                    pool.wait_ge(final, FINAL_OPS * n + 1)
                    nc.gpsimd.tensor_tensor(frstd[:, :, 1], frstd[:, :, 0], minus_half[:], ALU.pow).then_inc(final, 1)
                elif part == 1:
                    pool.wait_ge(final, FINAL_OPS * n + 3)
                    nc.gpsimd.tensor_tensor(y[p][:], y[p][:], gamma_bc[:], ALU.mult).then_inc(final, 1)
                else:
                    pool.wait_ge(final, FINAL_OPS * n + 4)
                    pool.wait_ge(hb_ready, n + 1)
                    nc.gpsimd.tensor_tensor(y[p][:], y[p][:], h_beta[p][:], ALU.add).then_inc(final, 1)

            def low_x(tile):
                n, k, p = tile
                pool.wait_ge(x_top_ready, n + 1)
                nc.gpsimd.tensor_tensor(xT_low[p][:], xT[p][:], x_top[:], ALU.subtract).then_inc(x_low_ready, 1)

            def low_z(e, st):
                n, k, p = st.experts
                pool.wait_ge(z_top_ready, NE * n + e + 1)
                wait(pool, up_ready, 2 * (NE * n + e - 1))
                nc.gpsimd.tensor_tensor(z_low[e % 2][:, 1, :], z[e % 2][:, 1, :], z_top[e % 2][:, 1, :],
                                        ALU.subtract).then_inc(z_low_rest, 1)

            def step(st):
                for e in range(NE):
                    if st.experts is not None:
                        low_z(e, st)
                    if st.next is not None and e == 3:
                        deviation(st.next)
                    if st.end is not None and e in (1, 3, 4):
                        finish(st.end, (1, 3, 4).index(e))
                    if st.front is not None and e == 5:
                        low_x(st.front)
                    if st.front is not None and e == 6:
                        residual(st.front)

            pool.wait_ge(weights_in, 16 * N_WEIGHTS)
            deviation((0, 0, 0))
            steps(pool, step)

        @block.tensor
        def _(pe):
            def front(u, st):
                n, k, p = st.front
                bank = fb[u % 2]
                wait(pe, front_free, 4 * n + u)
                if u < 2:
                    if u == 0:
                        pe.wait_ge(xn_ready, T * (n + 1))
                    for t in range(T):
                        last = pe.transpose(bank[0:96, t * TP:(t + 1) * TP], xn[p][:, t, u * 96:(u + 1) * 96],
                                            ident[0:TP, 0:TP])
                elif u == 2:
                    for f in range(F2):
                        last = pe.matmul(bank[0:RH, 0:N], w1_sb[:, f, :], xT[p][:, f, :],
                                         start=(f == 0), stop=(f == F2 - 1))
                else:
                    for t in range(T):
                        last = pe.matmul(bank[0:TP, t * NE:(t + 1) * NE], uT[:, t * TP:(t + 1) * TP], w2_sb[:],
                                         start=True, stop=True)
                last.then_inc(front_ready, 1)

            def down(e, st):
                n, k, p = st.experts
                if isinstance(n, int) and n == 0:
                    pe.wait_ge(w_high, e + 1)
                    pe.wait_ge(w_low, e + 1)
                if e == 0:
                    pe.wait_ge(x_high_ready, n + 1)
                    pe.wait_ge(x_low_ready, n + 1)
                for m in range(M2):
                    wait(pe, z_ready, M2 * (NE * n + e - 2) + m + 1)
                    columns = slice(m * 128, (m + 1) * 128)
                    three_passes(pe, hid[M2 * (e % 2) + m][:, 0:N],
                                 (lambda f: down_high[:, e, f, columns], lambda f: down_low[:, e, f, columns]),
                                 (lambda f: xT_high[p][:, f, :], lambda f: xT_low[p][:, f, :]), F2
                                 ).then_inc(hid_ready, 1)

            def up(e, tile):
                n, k, p = tile
                if isinstance(n, int) and n == 0:
                    pe.wait_ge(w_high, NE + e + 1)
                    pe.wait_ge(w_low, NE + e + 1)
                pe.wait_ge(z_high_ready, NE * n + e + 1)
                pe.wait_ge(z_low_ready, NE * n + e + 1)
                pe.wait_ge(z_low_rest, NE * n + e + 1)
                for j in range(T // 2):
                    wait(pe, acc_done, T * (NE * n + e - 1) + 2 * j + 2)
                    for i in range(2):
                        rows = slice((2 * j + i) * TP, (2 * j + i + 1) * TP)
                        last = three_passes(pe, upb[j][0:TP, i * E:(i + 1) * E],
                                            (lambda m: z_high[e % 2][:, m, rows], lambda m: z_low[e % 2][:, m, rows]),
                                            (lambda m: up_high[:, e, m, :], lambda m: up_low[:, e, m, :]), M2)
                    last.then_inc(up_ready, 1)

            def step(st):
                for e in range(NE):
                    if st.experts is not None:
                        down(e, st)
                    if st.front is not None and e in (0, 1, 3, 4):
                        front((0, 1, 3, 4).index(e), st)
                    if e == 0 and st.end is not None:
                        up(NE - 1, st.end)
                    if e > 0 and st.experts is not None:
                        up(e - 1, st.experts)

            pe.wait_ge(weights_in, 16 * N_WEIGHTS)
            steps(pe, step)

        @block.scalar
        def _(act):
            def front(u, st):
                n, k, p = st.front
                if u == 3:
                    act.wait_ge(gate_step, GATE_OPS * n + 3)
                    nc.scalar.activation(ex[:], shifted[:], ACT.Exp).then_inc(ex_ready, 1)
                    return
                act.wait_ge(front_ready, 4 * n + u + 1)
                if u < 2:
                    ins = nc.scalar.copy(xT[p][:, u, :], fb[u % 2][0:96, 0:N])
                else:
                    ins = nc.scalar.activation(uT[:], fb[u % 2][0:RH, 0:N], ACT.Gelu, bias=b1_sb[:, 0:1])
                ins.then_inc(front_free, 1)

            def gelu(e, st):
                n, k, p = st.experts
                for m in range(M2):
                    act.wait_ge(hid_ready, M2 * (NE * n + e) + m + 1)
                    if m == 0:
                        wait(act, z_low_ready, NE * n + e - 1)
                        wait(act, z_low_rest, NE * n + e - 1)
                    nc.scalar.activation(z[e % 2][:, m, :], hid[M2 * (e % 2) + m][:, 0:N], ACT.Gelu,
                                         bias=down_b_sb[:, e, m:m + 1]).then_inc(z_ready, 1)

            def high_z(e, st):
                n, k, p = st.experts
                act.wait_ge(z_top_ready, NE * n + e + 1)
                wait(act, up_ready, 2 * (NE * n + e - 1))
                nc.scalar.copy(z_high[e % 2][:], z_top[e % 2][:]).then_inc(z_high_ready, 1)

            def high_x(tile):
                n, k, p = tile
                act.wait_ge(x_top_ready, n + 1)
                nc.scalar.copy(xT_high[p][:], x_top[:]).then_inc(x_high_ready, 1)

            def high_weights():
                for i in range(2 * NE):
                    _, _, top, high, _ = weight_parts(i)
                    act.wait_ge(w_top_ready, i + 1)
                    nc.scalar.copy(high, top).then_inc(w_high, 1)

            def step(st):
                if st.first:
                    front(0, st)
                    front(1, st)
                    high_weights()
                    high_x(st.front)
                    front(2, st)
                    front(3, st)
                    return
                for e in range(NE):
                    if st.experts is not None:
                        gelu(e, st)
                        high_z(e, st)
                    if st.front is not None and e == 4:
                        high_x(st.front)
                    if st.front is not None and e in (0, 1, 3, 5):
                        front((0, 1, 3, 5).index(e), st)

            act.wait_ge(weights_in, 16 * N_WEIGHTS)
            steps(act, step)

        @block.vector
        def _(dve):
            def statistics(tile):
                n, k, p = tile
                dve.wait_ge(h_loaded[p], 16 * (k + 1))
                wait(dve, xn_ready, T * n)
                for t in range(T):
                    nc.vector.bn_stats(bst[:, t, :], h_in[p][:, t, :]).then_inc(stats, 1)
                dve.wait_ge(stats, 2 * T * n + T)
                settled(dve, sb_const)
                for t in range(T):
                    nc.vector.bn_aggr(mv[:, t, :], bst[:, t, :]).then_inc(stats, 1)

            def normalise(tile):
                n, k, p = tile
                dve.wait_ge(pool_own, 2 * n + 2)
                wait(dve, acc_done, T * NE * (n - 2) + T)
                for t in range(T):
                    nc.vector.tensor_scalar(xn[p][:, t, :], h_in[p][:, t, :], mv[:, t, 0:1], rstd[:, t, 1:2],
                                            ALU.subtract, ALU.mult).then_inc(xn_ready, 1)

            def final_normalise(tile):
                n, k, p = tile
                dve.wait_ge(final, FINAL_OPS * n + 2)
                wait(dve, stored[p], 16 * k)
                for t in range(T):
                    last = nc.vector.tensor_scalar(y[p][:, t, :], acc[p][:, t, :], fmv[:, t, 0:1],
                                                   frstd[:, t, 1:2], ALU.subtract, ALU.mult)
                last.then_inc(final, 1)

            def final_statistics(tile):
                n, k, p = tile
                wait(dve, final, FINAL_OPS * n)
                dve.wait_ge(acc_done, T * NE * (n + 1))
                for t in range(T):
                    nc.vector.bn_stats(fst[:, t, :], acc[p][:, t, :]).then_inc(fstats, 1)
                dve.wait_ge(fstats, 2 * T * n + T)
                settled(dve, sb_const)
                for t in range(T):
                    nc.vector.bn_aggr(fmv[:, t, :], fst[:, t, :]).then_inc(fstats, 1)

            def gate(tile, part):
                n, k, p = tile
                count = [(0, 3, 7, 11)[part]]

                def chain(ins):
                    count[0] += 1
                    ins.then_inc(gate_step, 1)
                    dve.wait_ge(gate_step, GATE_OPS * n + count[0])

                def wide(tile_, shape=(TP, T, NE)):
                    return tile_[:].unsqueeze(2).to_broadcast(list(shape))

                others = routing[:].unsqueeze(2).to_broadcast([TP, T, NE, NE])
                own = routing[:].unsqueeze(3).to_broadcast([TP, T, NE, NE])
                if part == 0:
                    dve.wait_ge(front_ready, 4 * n + 4)
                    chain(nc.vector.tensor_tensor(logits[:].rearrange("p t e -> p (t e)"), fb[1][0:TP, 0:T * NE],
                                                  b2_bc[:].rearrange("p t e -> p (t e)"), ALU.add))
                    dve.sem_inc(front_free, 1)
                    chain(nc.vector.tensor_reduce(lmax[:], logits[:], AX.X, ALU.max))
                    chain(nc.vector.tensor_tensor(shifted[:], logits[:], wide(lmax), ALU.subtract))
                elif part == 1:
                    dve.wait_ge(ex_ready, n + 1)
                    chain(nc.vector.tensor_reduce(total[:], ex[:], AX.X, ALU.add))
                    chain(nc.vector.reciprocal(rtotal[:], total[:]))
                    chain(nc.vector.tensor_tensor(routing[:], ex[:], wide(rtotal), ALU.mult))
                    chain(nc.vector.tensor_tensor(above[:], others, own, ALU.is_gt))
                elif part == 2:
                    chain(nc.vector.tensor_tensor(equal[:], others, own, ALU.is_equal))
                    chain(nc.vector.tensor_tensor(tie[:].rearrange("p t e j -> p t (e j)"),
                                                  equal[:].rearrange("p t e j -> p t (e j)"),
                                                  lower[:].rearrange("p e j -> p (e j)").unsqueeze(1)
                                                  .to_broadcast([TP, T, NE * NE]), ALU.mult))
                    chain(nc.vector.tensor_tensor(ahead[:], above[:], tie[:], ALU.add))
                    chain(nc.vector.tensor_reduce(rank[:], ahead[:], AX.X, ALU.add))
                else:
                    chain(nc.vector.scalar_tensor_tensor(sparse[:], rank[:], float(TOP_K), routing[:],
                                                         ALU.is_lt, ALU.mult))
                    chain(nc.vector.tensor_reduce(kept[:], sparse[:], AX.X, ALU.add))
                    chain(nc.vector.tensor_scalar(kept_eps[:], kept[:], GATE_EPS, None, ALU.add))
                    chain(nc.vector.reciprocal(rkept[:], kept_eps[:]))
                    assert count[0] == GATE_OPS
                    nc.vector.tensor_tensor(gates[p][:], sparse[:], wide(rkept), ALU.mult).then_inc(gates_ready, 1)

            def split_x(tile):
                n, k, p = tile
                dve.wait_ge(front_free, 4 * n + 2)
                wait(dve, x_high_ready, n)
                wait(dve, x_low_ready, n)
                high_bits(nc.vector, x_top[:], xT[p][:]).then_inc(x_top_ready, 1)

            def split_z(e, st):
                n, k, p = st.experts
                dve.wait_ge(z_ready, M2 * (NE * n + e + 1))
                wait(dve, z_high_ready, NE * n + e - 1)
                wait(dve, z_low_rest, NE * n + e - 1)
                high_bits(nc.vector, z_top[e % 2][:], z[e % 2][:]).then_inc(z_top_ready, 1)
                dve.wait_ge(z_top_ready, NE * n + e + 1)
                wait(dve, up_ready, 2 * (NE * n + e - 1))
                nc.vector.tensor_tensor(z_low[e % 2][:, 0, :], z[e % 2][:, 0, :], z_top[e % 2][:, 0, :],
                                        ALU.subtract).then_inc(z_low_ready, 1)

            def split_weights():
                for i in range(2 * NE):
                    which, raw_w, top, high, low = weight_parts(i)
                    if i % NE == 0:
                        dve.wait_ge(raw_in[which], 16 * RAW_PARTS)
                    if i >= 2:
                        dve.wait_ge(w_high, i - 1)
                        dve.wait_ge(w_low, i - 1)
                    high_bits(nc.vector, top, raw_w).then_inc(w_top_ready, 1)
                    dve.wait_ge(w_top_ready, i + 1)
                    nc.vector.tensor_tensor(low, raw_w, top, ALU.subtract).then_inc(w_low, 1)

            def sums(e, tile):
                n, k, p = tile
                if e == 0:
                    dve.wait_ge(gates_ready, n + 1)
                    wait(dve, final, FINAL_OPS * (n - 2) + 3)
                for t in range(T):
                    if t % 2 == 0:
                        dve.wait_ge(up_ready, 2 * (NE * n + e) + t // 2 + 1)
                    if e > 0:
                        dve.wait_ge(acc_done, T * (NE * n + e - 1) + t + 1)
                    before = xn[p] if e == 0 else acc[p]
                    nc.vector.scalar_tensor_tensor(acc[p][:, t, :], upb[t // 2][0:TP, (t % 2) * E:(t % 2 + 1) * E],
                                                   gates[p][:, t, e:e + 1], before[:, t, :], ALU.mult, ALU.add
                                                   ).then_inc(acc_done, 1)

            def step(st):
                if st.first:
                    split_weights()
                for e in range(NE):
                    if st.experts is not None:
                        split_z(e, st)
                        if e > 0:
                            sums(e - 1, st.experts)
                    if st.end is not None and e == 0:
                        sums(NE - 1, st.end)
                        final_statistics(st.end)
                    if st.end is not None and e == 2:
                        final_normalise(st.end)
                    if st.next is not None and e == 3:
                        statistics(st.next)
                    if st.next is not None and e == 4:
                        normalise(st.next)
                    if st.front is not None and e == 3:
                        split_x(st.front)
                    if st.front is not None and e >= 5:
                        gate(st.front, e - 5)
                if st.front is not None:
                    gate(st.front, 3)

            gates_ready = sb_const["gates_ready"]
            dve.wait_ge(lower_ready, 3)
            statistics((0, 0, 0))
            normalise((0, 0, 0))
            dve.wait_ge(weights_in, 16 * N_WEIGHTS)
            steps(dve, step)


def early_fusion(nc, x, txt, tok_w, tok_bias, w_qk, b_qk, w_v, b_v, scale, w_proj, b_proj,
                 w1, b1, w2, b2, down_w, down_b, up_w, gamma, beta, out):
    B, NT, E = out.shape
    tokens = nc.dram_tensor("tokens_scratch", (B, NT - txt.shape[1], E), F32).ap()
    mixed = nc.dram_tensor("mixed_scratch", (B, NT, E), F32).ap()
    with ExitStack() as sems:
        sb_const = constants(nc, sems)
        with ExitStack() as ctx:
            tokenize(nc, ctx, sems, sb_const, x, tok_w, tok_bias, tokens)
        with ExitStack() as ctx:
            attend(nc, ctx, sems, sb_const, tokens, txt, w_qk, b_qk, w_v, b_v, scale, w_proj, b_proj, mixed)
        with ExitStack() as ctx:
            mix_experts(nc, ctx, sems, sb_const, mixed, w1, b1, w2, b2, down_w, down_b, up_w, gamma, beta, out)




def by_head_pair(a, E=192, H=12):
    a = a[..., :2 * E]
    lead = a.shape[:-1]
    n = len(lead)
    a = a.reshape(lead + (2, H // 2, 2, E // H))
    return a.transpose(tuple(range(n)) + (n, n + 2, n + 3, n + 1)).reshape(lead + (2 * E,))


def kernel(x, txt, L0_tok_weight, L0_tok_bias, L0_attn_w_qkv, L0_attn_b_qkv, L0_attn_scale, L0_attn_w_proj,
           L0_attn_b_proj, L0_ffn_w1, L0_ffn_b1, L0_ffn_w2, L0_ffn_b2, L0_ffn_down_w, L0_ffn_down_b, L0_ffn_up_w,
           L0_ffn_gamma, L0_ffn_beta):
    import numpy as np
    import concourse.bacc as bacc
    from concourse.bass_utils import run_bass_kernel_spmd

    w_qkv, b_qkv = np.asarray(L0_attn_w_qkv), np.asarray(L0_attn_b_qkv)
    E = w_qkv.shape[0]
    arrays = {
        "x": x, "txt": txt, "tok_w": np.asarray(L0_tok_weight).T, "tok_bias": L0_tok_bias,
        "w_qk": by_head_pair(w_qkv), "b_qk": by_head_pair(b_qkv), "w_v": w_qkv[:, 2 * E:], "b_v": b_qkv[2 * E:],
        "scale": L0_attn_scale, "w_proj": L0_attn_w_proj, "b_proj": L0_attn_b_proj, "w1": L0_ffn_w1,
        "b1": L0_ffn_b1, "w2": L0_ffn_w2, "b2": L0_ffn_b2, "down_w": L0_ffn_down_w, "down_b": L0_ffn_down_b,
        "up_w": L0_ffn_up_w, "gamma": L0_ffn_gamma, "beta": L0_ffn_beta,
    }
    arrays = {name: np.ascontiguousarray(a) for name, a in arrays.items()}
    B, IMG_T = x.shape[0], (x.shape[2] // 16) ** 2
    nc = bacc.Bacc("TRN2", target_bir_lowering=False, num_devices=1)
    aps = [nc.dram_tensor(name, a.shape, mybir.dt.from_np(a.dtype), kind="ExternalInput").ap()
           for name, a in arrays.items()]
    out = nc.dram_tensor("out", (B, IMG_T + txt.shape[1], E), F32, kind="ExternalOutput").ap()
    early_fusion(nc, *aps, out)
    r = run_bass_kernel_spmd(nc, [arrays], core_ids=[0])
    return r.results[0]["out"]
```

```python
from contextlib import ExitStack

import concourse.bass as bass
from concourse import mybir

ALU = mybir.AluOpType
ACT = mybir.ActivationFunctionType
AX = mybir.AxisListType
F32 = mybir.dt.float32
BF16 = mybir.dt.bfloat16
F32R = mybir.dt.float32r

LN_EPS = 1e-5
GATE_EPS = 1e-8
MASK = -1e30
BANK = 512


def settled(eng, sb_const):
    eng.sem_inc(sb_const["wait_carrier"], 1)


THIRD = 64
PAIRS = [(0, 1), (2, 0), (1, 2)]
STARTS = [0, 2 * THIRD, THIRD]
RIGHT = [0, 1, 2, 0, 1]
NL = len(RIGHT)


def high_bits(engine, o, i):
    return engine.tensor_scalar(o.bitcast(mybir.dt.uint32), i.bitcast(mybir.dt.uint32), 0xFFFFF000, None,
                                ALU.bitwise_and)


def thirds(pair):
    u, v = pair
    if v == u + 1:
        return [(slice(0, 128), slice(u * THIRD, (v + 1) * THIRD))]
    return [(slice(k * THIRD, (k + 1) * THIRD), slice(w * THIRD, (w + 1) * THIRD)) for k, w in enumerate(pair)]


def stack_parts(raw_w, top, stack):
    a, b = slice(0, THIRD), slice(THIRD, 128)
    high = [(stack[b, 1], top[b, 1]), (stack[:, 2], top[:, 2]), (stack[:, 3], top[:, 0]), (stack[a, 4], top[a, 1])]
    low = [(stack[:, 0], raw_w[:, 0], top[:, 0]), (stack[a, 1], raw_w[a, 1], top[a, 1])]
    return high, low


def constants(nc, ctx):
    ident = ctx.enter_context(nc.sbuf_tensor("ident", [128, 128], F32))
    ident_bf = ctx.enter_context(nc.sbuf_tensor("ident_bf", [96, 96], BF16))
    neg_diag = ctx.enter_context(nc.sbuf_tensor("neg_diag", [96, 2, 96], BF16))
    zeroed = ctx.enter_context(nc.semaphore("c_zeroed"))
    ready = ctx.enter_context(nc.semaphore("c_ready"))
    first = ctx.enter_context(nc.semaphore("c_first"))
    names = ("bias_scaled", "dve_cleared", "gates_ready", "wait_carrier")
    extra = {n: ctx.enter_context(nc.semaphore("c_" + n)) for n in names}
    with nc.Block() as block:

        @block.gpsimd
        def _(pool):
            for tile in (ident, ident_bf, neg_diag):
                nc.gpsimd.memset(tile[:], 0.0).then_inc(zeroed, 1)
            pool.wait_ge(zeroed, 3)
            for n, (view, size, fill) in enumerate(((ident[:], 128, 1.0), (ident_bf[:], 96, 1.0),
                                                    (neg_diag[:, 0, :], 96, MASK), (neg_diag[:, 1, :], 96, MASK))):
                nc.gpsimd.affine_select(out=view, in_=view, compare_op=ALU.not_equal, fill=fill, base=0,
                                        pattern=[[-1, size]], channel_multiplier=1).then_inc(first, 1)
            pool.wait_ge(first, 4)
            nc.gpsimd.memset(neg_diag[0:1, 0, 0:1], 0.0).then_inc(ready, 1)
    return {"ident": ident, "ident_bf": ident_bf, "neg_diag": neg_diag, "ident_ready": ready, **extra}


def tokenize(nc, ctx, sems, sb_const, x, tok_w, tok_bias, tokens):
    B, Cin, HW, _ = x.shape
    P16 = 16
    NP = HW // P16
    IMG = 8
    R = IMG * NP
    G = B // IMG
    ROW = P16 * HW
    E = tok_w.shape[1] + 1
    CH = Cin * 2
    LOADED = 8 * IMG
    assert R <= 128 and G % 2 == 0 and G >= 4 and P16 * P16 == 256
    ident = sb_const["ident"]

    def sb(name, shape, dt=F32):
        return ctx.enter_context(nc.sbuf_tensor(name, shape, dt))

    def sem(name):
        return sems.enter_context(nc.semaphore(name))

    pix = [sb(f"t_pix{p}", [R, Cin, ROW]) for p in range(2)]
    patch = [sb(f"t_patch{p}", [R, Cin * P16 * P16]) for p in range(2)]
    w_sb = sb("t_w", [128, CH, E - 1])
    w_time = sb("t_w_time", [R, E - 1])
    bias_bc = sb("t_bias", [R, E - 1])
    pixT = [sb(f"t_pixT{p}", [128, CH, R]) for p in range(2)]
    time_bias = [sb(f"t_tb{p}", [R, E - 1]) for p in range(2)]
    tok = [sb(f"t_tok{p}", [R, NP, E]) for p in range(2)]
    ssq = [sb(f"t_ssq{p}", [R, NP]) for p in range(2)]
    tnew = [sb(f"t_tnew{p}", [R, NP]) for p in range(2)]
    ssz = [sb(f"t_ssz{p}", [R, NP]) for p in range(2)]
    junk = sb("t_junk", [R, Cin, P16, P16])
    junk_z = sb("t_junk_z", [R, E - 1])
    turned = [ctx.enter_context(nc.psum_tensor(f"t_turned{n}", [128, BANK], F32)) for n in range(4)]
    prod = [ctx.enter_context(nc.psum_tensor(f"t_prod{n}", [128, BANK], F32)) for n in range(2)]

    weights_in = sem("t_weights_in")
    pix_in = [sem(f"t_pix_in{p}") for p in range(2)]
    gathered = sem("t_gathered")
    sq_done = sem("t_sq_done")
    tnew_ready = sem("t_tnew_ready")
    turned_ready = sem("t_turned_ready")
    left_copied = sem("t_left_copied")
    right_copied = sem("t_right_copied")
    prod_ready = sem("t_prod_ready")
    tb_done = sem("t_tb_done")
    z_done = sem("t_z_done")
    zsq_done = sem("t_zsq_done")
    stored = [sem(f"t_stored{p}") for p in range(2)]
    zt_done = sem("t_zt_done")

    out_rows = tokens.rearrange("b (hp wp) e -> (b hp) (wp e)", wp=NP)

    with nc.Block() as block:

        @block.sync
        def _(sp):
            sp.dma_start(w_sb[:], tok_w[1:, :].rearrange("(k p) o -> p k o", p=128)).then_inc(weights_in, 16)
            sp.dma_start(w_time[:], tok_w[0:1, :].to_broadcast([R, E - 1])).then_inc(weights_in, 16)
            sp.dma_start(bias_bc[:], tok_bias.rearrange("(a o) -> a o", a=1).to_broadcast([R, E - 1])
                         ).then_inc(weights_in, 16)

            def load_group(g, p):
                for i in range(IMG):
                    src = x[bass.ds(g * IMG + i, 1)].rearrange("a c (hp f) w -> hp (a c) (f w)", f=P16)
                    sp.dma_start(pix[p][i * NP:(i + 1) * NP], src).then_inc(pix_in[p], 16)

            load_group(0, 0)
            load_group(1, 1)
            with sp.Fori(1, G // 2) as pair:
                for p in range(2):
                    g = 2 * pair + p
                    sp.wait_ge(gathered, (g - 1) * NP)
                    sp.wait_ge(sq_done, (g - 1) * NP)
                    load_group(g, p)

        @block.tensor
        def _(pe):
            pe.wait_ge(weights_in, 48)
            pe.wait_ge(sb_const["ident_ready"], 1)

            def turn(g, p, w, first):
                n = g * NP + w
                pe.wait_ge(gathered, n + 1)
                for half in range(2):
                    bank = turned[2 * (w % 2) + half]
                    if not (first and w < 2):
                        pe.wait_ge(right_copied if half else left_copied, n - 1)
                    for k in range(3):
                        j = 3 * half + k
                        last = pe.transpose(bank[:, k * R:(k + 1) * R],
                                            patch[w % 2][:, j * 128:(j + 1) * 128], ident[0:R, 0:R])
                    last.then_inc(turned_ready, 1)
                return last

            def multiply(g, w, first):
                n = g * NP + w
                pe.wait_ge(left_copied, n + 1)
                pe.wait_ge(right_copied, n + 1)
                if not (first and w < 2):
                    pe.wait_ge(z_done, n - 1)
                for k in range(CH):
                    last = pe.matmul(prod[w % 2][0:R, 0:E - 1], pixT[w % 2][:, k, :], w_sb[:, k, :],
                                     start=(k == 0), stop=(k == CH - 1))
                last.then_inc(prod_ready, 1)

            def group(g, p, first):
                for w in range(NP):
                    turn(g, p, w, first)
                    if w > 0:
                        multiply(g, w - 1, first)
                multiply(g, NP - 1, first)

            group(0, 0, True)
            group(1, 1, False)
            with pe.Fori(1, G // 2) as pair:
                group(2 * pair, 0, False)
                group(2 * pair + 1, 1, False)

        @block.vector
        def _(dve):
            def gather(g, p, w):
                n = g * NP + w
                if w == 0:
                    dve.wait_ge(pix_in[p], LOADED * g + 2 * LOADED - LOADED * p)
                if not (isinstance(n, int) and n < 2):
                    dve.wait_ge(turned_ready, 2 * n - 2)
                view = pix[p][:].rearrange("r c (py q) -> r c py q", py=P16)
                nc.vector.tensor_copy(patch[w % 2][:].rearrange("r (c py q) -> r c py q", c=Cin, py=P16),
                                      view[:, :, :, w * P16:(w + 1) * P16]).then_inc(gathered, 1)

            def group(g, p, first, last):
                for w in range(NP + 1):
                    n = g * NP + w
                    if w < NP - 1:
                        gather(g, p, w + 1)
                    elif w == NP - 1 and not last:
                        gather(g + 1, 1 - p, 0)
                    if w < NP:
                        dve.wait_ge(turned_ready, 2 * n + 1)
                        if not (first and w < 2):
                            dve.wait_ge(prod_ready, n - 1)
                        nc.vector.tensor_copy(pixT[w % 2][:, 0:3, :].rearrange("p k r -> p (k r)"),
                                              turned[2 * (w % 2)][:, 0:3 * R]).then_inc(left_copied, 1)
                        if w == 0:
                            dve.wait_ge(tnew_ready, g + 1)
                        if not (first and w < 2):
                            dve.wait_ge(z_done, n - 1)
                        nc.vector.scalar_tensor_tensor(time_bias[w % 2][:], w_time[:], tnew[p][:, w:w + 1],
                                                       bias_bc[:], ALU.mult, ALU.add).then_inc(tb_done, 1)
                    if w > 0:
                        if w == 1 and not first:
                            dve.wait_ge(stored[p], 8 * g - 8 * p)
                        dve.wait_ge(prod_ready, n)
                        dve.wait_ge(tb_done, n)
                        nc.vector.tensor_tensor(tok[p][:, w - 1, 1:E], prod[(w - 1) % 2][0:R, 0:E - 1],
                                                time_bias[(w - 1) % 2][:], ALU.add).then_inc(z_done, 1)

            dve.wait_ge(weights_in, 48)
            gather(0, 0, 0)
            group(0, 0, True, False)
            group(1, 1, False, False)
            with dve.Fori(1, G // 2 - 1) as pair:
                group(2 * pair, 0, False, False)
                group(2 * pair + 1, 1, False, False)
            group(G - 2, 0, False, False)
            group(G - 1, 1, False, True)

        @block.scalar
        def _(act):
            def square(g, p, w):
                if not (isinstance(g, int) and g * NP + w == 0):
                    act.wait_ge(sq_done, g * NP + w)
                view = pix[p][:].rearrange("r c (py q) -> r c py q", py=P16)
                nc.scalar.activation(junk[:], view[:, :, :, w * P16:(w + 1) * P16], ACT.Square,
                                     accum_out=ssq[p][:, w:w + 1]).then_inc(sq_done, 1)

            def time_features(g, p):
                act.wait_ge(sq_done, (g + 1) * NP)
                nc.scalar.activation(tnew[p][:], ssq[p][:], ACT.Sqrt, bias=1.0).then_inc(tnew_ready, 1)

            def square_tokens(g, p, w):
                n = g * NP + w
                act.wait_ge(z_done, n + 1)
                if not (isinstance(n, int) and n == 0):
                    act.wait_ge(zsq_done, n)
                nc.scalar.activation(junk_z[:], tok[p][:, w, 1:E], ACT.Square,
                                     accum_out=ssz[p][:, w:w + 1]).then_inc(zsq_done, 1)

            def group(g, p, first, last):
                for w in range(NP):
                    n = g * NP + w
                    act.wait_ge(turned_ready, 2 * n + 2)
                    if not (first and w < 2):
                        act.wait_ge(prod_ready, n - 1)
                    nc.scalar.copy(pixT[w % 2][:, 3:6, :].rearrange("p k r -> p (k r)"),
                                   turned[2 * (w % 2) + 1][:, 0:3 * R]).then_inc(right_copied, 1)
                    if w > 0:
                        square_tokens(g, p, w - 1)
                    if not last and w >= NP // 2:
                        if w == NP // 2:
                            act.wait_ge(pix_in[1 - p], LOADED * g + LOADED + 2 * LOADED - LOADED * (1 - p))
                        square(g + 1, 1 - p, 2 * w - NP)
                        square(g + 1, 1 - p, 2 * w - NP + 1)
                if not last:
                    time_features(g + 1, 1 - p)
                square_tokens(g, p, NP - 1)
                act.wait_ge(zsq_done, (g + 1) * NP)
                nc.scalar.activation(tok[p][:, :, 0], ssz[p][:], ACT.Sqrt, bias=1.0).then_inc(zt_done, 1)
                act.wait_ge(zt_done, g + 1)
                rows = out_rows[bass.ds(g * R, R)]
                act.dma_start(rows, tok[p][:].rearrange("r w e -> r (w e)")).then_inc(stored[p], 16)

            act.wait_ge(pix_in[0], 2 * LOADED)
            for w in range(NP):
                square(0, 0, w)
            time_features(0, 0)
            group(0, 0, True, False)
            group(1, 1, False, False)
            with act.Fori(1, G // 2 - 1) as pair:
                group(2 * pair, 0, False, False)
                group(2 * pair + 1, 1, False, False)
            group(G - 2, 0, False, False)
            group(G - 1, 1, False, True)
            for p in range(2):
                act.wait_ge(stored[p], 8 * G)


def attend(nc, ctx, sems, sb_const, tokens, txt, w_qk, b_qk, w_v, b_v, scale, w_proj, b_proj, mixed):
    NI, NT, E = mixed.shape
    IMG_T = tokens.shape[1]
    H = scale.shape[0]
    D = E // H
    T = 3
    TP = 96
    LAST = NT - (T - 1) * TP
    PAD = T * TP
    EVEN = NT + NT % 2
    F2 = E // 96
    HH = 96 // D
    QS = [0, 1, 2, 0, 1, 0]
    KS = [0, 0, 0, 1, 1, 2]
    KROWS = 6 * D
    SROWS = KROWS + 2
    STRIP = 32
    HG = 4
    NG = H // HG
    assert E == 192 and D == 16 and H == 12 and 0 < LAST <= TP and IMG_T == 2 * TP + 4 and NI % 3 == 1 and NI > 9
    ident, ident_bf, neg_diag = sb_const["ident"], sb_const["ident_bf"], sb_const["neg_diag"]

    def sb(name, shape, dt=F32):
        return ctx.enter_context(nc.sbuf_tensor(name, shape, dt))

    def sem(name):
        return sems.enter_context(nc.semaphore(name))

    def ps(name):
        return ctx.enter_context(nc.psum_tensor(name, [128, BANK], F32))

    raw_qkv = sb("a_raw_qkv", [128, 3, 3 * E])
    w_top = sb("a_w_top", [128, 3, 3 * E])
    w_st = sb("a_w_st", [128, NL, 3 * E], F32R)
    w_p_sb = sb("a_wp", [96, F2, E])
    bqk = sb("a_bqk", [96, 4])
    bqk_s = sb("a_bqks", [96, 4])
    scl = sb("a_scl", [96, 2])
    bv = sb("a_bv", [96, F2])
    bp_bc = sb("a_bp", [96, T, E])
    minus_half = sb("a_mh", [96, T])
    h_front = [sb(f"a_hf{r}", [96, T, E]) for r in range(3)]
    h_res = [sb(f"a_hr{r}", [96, T, E]) for r in range(3)]
    h_out = [sb(f"a_ho{r}", [96, T, E]) for r in range(3)]
    bst = sb("a_bst", [96, T, 6])
    mv = sb("a_mv", [96, T, 2])
    veps = sb("a_veps", [96, T])
    rstd = sb("a_rstd", [96, T])
    hn = sb("a_hn", [96, T, E + THIRD])
    hnT = sb("a_hnT", [128, 3 * PAD])
    hn_top = sb("a_hn_top", [128, 3 * PAD])
    hn_st = sb("a_hn_st", [128, 3, PAD], F32R)
    qk = sb("a_qk", [96, 4, NT])
    qk_rest = sb("a_qkr", [96, 4, NT])
    parts = sb("a_parts", [96, 3, 4, NT], BF16)
    q_st = [sb(f"a_qst{r}", [SROWS, H, PAD], BF16) for r in range(3)]
    k_st = [sb(f"a_kst{r}", [SROWS, H, PAD], BF16) for r in range(3)]
    v_st = [sb(f"a_vst{r}", [96, T, H, STRIP]) for r in range(3)]
    mx = sb("a_mx", [96, T, H])
    m_hi = [sb(f"a_mhi{a}", [H // 2, PAD], BF16) for a in range(2)]
    m_lo = [sb(f"a_mlo{a}", [H // 2, PAD], BF16) for a in range(2)]
    prob = [sb(f"a_p{g}", [96, HG, T, NT]) for g in range(NG)]
    oT = sb("a_oT", [128, NG, PAD])
    rden = sb("a_rden", [96, T, H])
    on = sb("a_on", [96, T, E])
    onT = sb("a_onT", [96, F2, PAD])

    st = ctx.enter_context(nc.psum_tensor("a_st", [128, T, BANK], F32))
    sm = ctx.enter_context(nc.psum_tensor("a_sm", [128, T, BANK], F32))
    work = [ps(f"a_work{b}") for b in range(2)]

    weights_in = sem("a_weights_in")
    cleared = sem("a_cleared")
    hf_in = [sem(f"a_hf_in{r}") for r in range(3)]
    hr_in = [sem(f"a_hr_in{r}") for r in range(3)]
    stats = sem("a_stats")
    pool_own = sem("a_pool_own")
    hn_ready = sem("a_hn_ready")
    w_top_ready = sem("a_w_top_ready")
    w_parts = sem("a_w_parts")
    hn_turned = sem("a_hn_turned")
    hn_top_ready = sem("a_hn_top_ready")
    hn_high = sem("a_hn_high")
    hn_low_third = sem("a_hn_low_third")
    hn_low = sem("a_hn_low")
    res_ready = sem("a_res_ready")
    work_ready = sem("a_work_ready")
    work_free = [sem(f"a_work_free{b}") for b in range(2)]
    split = sem("a_split")
    stack_in = [sem(f"a_stack_in{r}") for r in range(3)]
    sm_ready = sem("a_sm_ready")
    max_done = sem("a_max_done")
    m_split = [sem(f"a_m_split{a}") for a in range(2)]
    m_ready = [sem(f"a_m_ready{a}") for a in range(2)]
    m_in = [[sem(f"a_m_in{r}{a}") for a in range(2)] for r in range(3)]
    st_ready = sem("a_st_ready")
    exp_done = sem("a_exp_done")
    masked = sem("a_masked")
    rd_done = sem("a_rd_done")
    h2_done = sem("a_h2_done")
    stored = [sem(f"a_stored{r}") for r in range(3)]

    FRONT = ["t0", "t1", "q0", "q1", "q2", "q3", "v0", "v1"]
    CORE = ["m1", "x0", "x1"]
    FINISH = ["x2", "o0", "o1", "o2", "n0", "n1", "p0", "p1"]
    BEFORE = ["t0", "t1", "x2", "q0", "q1", "q2", "q3", "v1", "n1", "p0", "x1", "v0"]
    AFTER = ["m1", None, "o0", None, "o1", "o2", "x0", "n0", "m0", None, None, "p1"]
    ORDER = [u for pair in zip(BEFORE, AFTER) for u in pair if u]
    assert sorted(ORDER) == sorted(FRONT + CORE + FINISH + ["m0"]) and len(ORDER) % 2 == 0
    NEEDS = {"o0": "x2", "o1": "x2", "o2": "x2", "n0": "o2", "n1": "o2", "p0": "n1", "p1": "n1"}
    SLOTS = [u for pair in zip(BEFORE, AFTER) for u in pair]
    SPLIT_AT = SLOTS.index("t1") + 1
    TURNS = {"t0": range(5), "t1": range(5, 3 * T)}

    class Step:

        def __init__(self, k, r):
            self.s = 3 * k + r
            fixed = isinstance(k, int)
            self.front = self._img(k, r, 0) if not fixed or self.s < NI else None
            self.maxima = self._img(k, r, 1) if not fixed or 1 <= self.s <= NI else None
            self.core = self._img(k, r, 2) if not fixed or 2 <= self.s <= NI + 1 else None
            self.finish = self._img(k, r, 3) if not fixed or 3 <= self.s <= NI + 2 else None
            self.next = self._img(k, r, -1) if not fixed or self.s + 1 < NI else None
            self.next_finish = self._img(k, r, 2) if not fixed or 2 <= self.s <= NI + 1 else None
            if fixed:
                clip = lambda v: max(0, min(v, NI))
                self.base = (8 * clip(self.s) + clip(self.s - 1) + 3 * clip(self.s - 2) + 8 * clip(self.s - 3), 0)
            else:
                self.base = (-31, 20)

        @staticmethod
        def _img(k, r, back):
            q, rr = divmod(r - back, 3)
            return 3 * k + r - back, k + q, rr

        def has(self, unit):
            stage = (self.front if unit in FRONT else self.finish if unit in FINISH
                     else self.core if unit in CORE else self.maxima)
            return stage is not None

        def at(self, unit):
            return self.base[0] + sum(self.has(u) for u in ORDER[:ORDER.index(unit)])

        def seq(self, unit):
            return self.at(unit) + self.base[1] * self.s

        def bank(self, unit):
            return self.at(unit) % 2

        def turns(self, unit):
            return self.at(unit) // 2 + self.base[1] // 2 * self.s

    def steps(engine, do):
        for s in range(6):
            do(Step(s // 3, s % 3))
        with engine.Fori(2, (NI - 1) // 3) as k:
            for r in range(3):
                do(Step(k, r))
        for s in range(NI - 1, NI + 3):
            do(Step(s // 3, s % 3))

    def wait(eng, semaphore, value):
        if not (isinstance(value, int) and value <= 0):
            eng.wait_ge(semaphore, value)

    N_WEIGHTS = 13

    with nc.Block() as block:

        @block.sync
        def _(sp):
            def dma(out, in_, semaphore, **kw):
                sp.dma_start(out, in_, **kw).then_inc(semaphore, 16)

            for j, pair in enumerate(PAIRS):
                for o, i in thirds(pair):
                    dma(raw_qkv[o, j, 0:2 * E], w_qk[i], weights_in)
                    dma(raw_qkv[o, j, 2 * E:3 * E], w_v[i], weights_in)
            dma(w_p_sb[:], w_proj.rearrange("(f p) o -> p f o", p=96), weights_in)
            dma(bqk[:], b_qk.rearrange("(m p) -> p m", p=96), weights_in, allow_slow_non_contiguous=True)
            dma(bv[:], b_v.rearrange("(f p) -> p f", p=96), weights_in, allow_slow_non_contiguous=True)
            dma(scl[:], scale.rearrange("(a h m) -> a h m", a=1, m=2).to_broadcast([D, HH, 2]), weights_in,
                allow_slow_non_contiguous=True)
            dma(bp_bc[:], b_proj.rearrange("(a b o) -> a b o", a=1, b=1).to_broadcast([96, T, E]), weights_in)

            def load_tokens(dst, n, semaphore):
                img = tokens[bass.ds(n, 1)].rearrange("a t e -> (a t) e")
                dma(dst[:, 0:2, :], img[0:2 * TP].rearrange("(t p) e -> p t e", p=TP), semaphore)
                dma(dst[0:IMG_T - 2 * TP, 2, :], img[2 * TP:IMG_T], semaphore)
                dma(dst[IMG_T - 2 * TP:LAST, 2, :], txt[bass.ds(n, 1)].rearrange("a t e -> (a t) e"), semaphore)

            def spread(stack, which, part, slots, r):
                for slot, p in enumerate(slots):
                    if p == part:
                        src = parts[:, part, 2 * which:2 * which + 2, :]
                        dma(stack[r][slot * D:(slot + 1) * D, :, 0:NT], src, stack_in[r])

            def step(st_):
                if st_.next is not None:
                    n, k, r = st_.next
                    wait(sp, hn_ready, T * (n - 2))
                    load_tokens(h_front[r], n, hf_in[r])
                if st_.next_finish is not None:
                    n, k, r = st_.next_finish
                    wait(sp, h2_done, 2 * (n - 2))
                    load_tokens(h_res[r], n, hr_in[r])
                if st_.core is not None:
                    minus_max(st_.core, 1)
                if st_.front is not None:
                    n, k, r = st_.front
                    wait(sp, st_ready, H * (n - 2))
                    for part, ops in ((0, 1), (1, 3), (2, 4)):
                        if part == 2 and st_.maxima is not None:
                            minus_max(st_.maxima, 0)
                        sp.wait_ge(split, 4 * n + ops)
                        spread(q_st, 0, part, QS, r)
                        spread(k_st, 1, part, KS, r)
                elif st_.maxima is not None:
                    minus_max(st_.maxima, 0)
                if st_.finish is not None:
                    n, k, r = st_.finish
                    sp.wait_ge(h2_done, 2 * n + 2)
                    img = mixed[bass.ds(n, 1)].rearrange("a t e -> (a t) e")
                    dma(img[0:2 * TP].rearrange("(t p) e -> p t e", p=TP), h_out[r][:, 0:2, :], stored[r])
                    dma(img[2 * TP:NT], h_out[r][0:LAST, 2, :], stored[r])

            def minus_max(image, a):
                n, k, r = image
                sp.wait_ge(m_ready[a], n + 1)
                for row, m in ((KROWS, m_hi), (KROWS + 1, m_lo)):
                    dst = q_st[r][row:row + 1, a * H // 2:(a + 1) * H // 2, 0:NT]
                    dma(dst, m[a][:, 0:NT], m_in[r][a])

            sp.wait_ge(sb_const["dve_cleared"], 6)
            load_tokens(h_front[0], 0, hf_in[0])
            steps(sp, step)
            for r in range(3):
                sp.wait_ge(stored[r], 32 * len(range(r, NI, 3)))

        @block.gpsimd
        def _(pool):
            nc.gpsimd.memset(minus_half[:], -0.5)
            for r in range(3):
                nc.gpsimd.memset(v_st[r][:], 0.0).then_inc(pool_own, 1)
            for r in range(3):
                pool.wait_ge(pool_own, 3)
                nc.gpsimd.memset(v_st[r][:, :, :, D:D + 1], 1.0).then_inc(pool_own, 1)
            for r in range(3):
                pool.wait_ge(pool_own, 6)
                ones = v_st[r][:, T - 1, :, D]
                last = nc.gpsimd.affine_select(out=ones, in_=ones, compare_op=ALU.is_ge, fill=0.0, base=LAST - 1,
                                               pattern=[[0, H]], channel_multiplier=-1)
                last.then_inc(pool_own, 1)
            pool.wait_ge(pool_own, 9)
            pool.nop().then_inc(cleared, 1)
            OWN = 9

            def normalise(image, st_):
                n, k, r = image
                pool.wait_ge(stats, 2 * T * (n + 1))
                settled(pool, sb_const)
                nc.gpsimd.tensor_scalar(veps[:], mv[:, :, 1], LN_EPS, None, ALU.add).then_inc(pool_own, 1)
                pool.wait_ge(pool_own, OWN + 2 * n + 1)
                nc.gpsimd.tensor_tensor(rstd[:], veps[:], minus_half[:], ALU.pow).then_inc(pool_own, 1)
                pool.wait_ge(pool_own, OWN + 2 * n + 2)
                if st_ is not None:
                    pool.wait_ge(work_ready, st_.seq("t1") + 1)
                settled(pool, sb_const)
                for t in range(T):
                    for o, size in ((E, THIRD), (0, E)):
                        last = nc.gpsimd.tensor_scalar(hn[:, t, o:o + size], h_front[r][:, t, 0:size], mv[:, t, 0:1],
                                                       rstd[:, t:t + 1], ALU.subtract, ALU.mult)
                    last.then_inc(hn_ready, 1)

            def mask_self(g, image):
                n, k, r = image
                pool.wait_ge(exp_done, H * n + HG * (g + 1))
                settled(pool, sb_const)
                for t in range(T):
                    skip = 1 if t == 0 else 0
                    width = min(TP, NT - t * TP) - skip
                    own = prob[g][:, :, t, t * TP + skip:t * TP + skip + width]
                    nc.gpsimd.affine_select(out=own, in_=own, compare_op=ALU.not_equal, fill=0.0, base=-skip,
                                            pattern=[[0, HG], [-1, width]], channel_multiplier=1
                                            ).then_inc(masked, 1)

            def step(st_):
                if st_.finish is not None:
                    n, k, r = st_.finish
                    pool.wait_ge(hr_in[r], 48 * (k + 1))
                    nc.gpsimd.tensor_tensor(h_res[r][:], h_res[r][:], bp_bc[:], ALU.add).then_inc(res_ready, 1)
                if st_.front is not None:
                    pool.wait_ge(hn_top_ready, st_.front[0] + 1)
                    nc.gpsimd.tensor_tensor(hn_st[:, 2, :], hnT[:, 2 * PAD:], hn_top[:, 2 * PAD:], ALU.subtract
                                            ).then_inc(hn_low, 1)
                if st_.core is not None:
                    mask_self(0, st_.core)
                if st_.next is not None:
                    normalise(st_.next, st_)
                if st_.core is not None:
                    mask_self(1, st_.core)
                if st_.front is not None:
                    pool.wait_ge(split, 4 * st_.front[0] + 3)
                    nc.gpsimd.tensor_tensor(parts[:, 2], qk_rest[:], parts[:, 1], ALU.subtract).then_inc(split, 1)
                if st_.core is not None:
                    mask_self(2, st_.core)

            pool.wait_ge(weights_in, 16 * N_WEIGHTS)
            normalise((0, 0, 0), None)
            steps(pool, step)

        @block.tensor
        def _(pe):
            def unit(name, st_):
                if name is None or not st_.has(name):
                    return
                wb = work[st_.bank(name)]
                wait(pe, work_free[st_.bank(name)], st_.turns(name))
                if name in NEEDS:
                    made_from = NEEDS[name]
                    pe.wait_ge(work_free[st_.bank(made_from)], st_.turns(made_from) + 1)
                kind, j = name[0], int(name[1])
                if kind == "t":
                    if j == 0:
                        pe.wait_ge(hn_ready, T * (st_.front[0] + 1))
                    for place, i in enumerate(TURNS[name]):
                        start, t = STARTS[i // T], i % T
                        last = pe.transpose(wb[:, place * TP:(place + 1) * TP], hn[:, t, start:start + 128],
                                            ident[0:96, 0:96])
                elif kind == "q":
                    if j == 0:
                        for parts_in in (hn_high, hn_low_third, hn_low):
                            pe.wait_ge(parts_in, st_.front[0] + 1)
                    for i, pair in enumerate(RIGHT):
                        last = pe.matmul(wb[0:96, 0:EVEN], w_st[:, i, j * 96:(j + 1) * 96], hn_st[:, pair, 0:EVEN],
                                         start=(i == 0), stop=(i == NL - 1))
                elif kind == "v":
                    for place, t in enumerate(([0, 1], [2])[j]):
                        for i, pair in enumerate(RIGHT):
                            last = pe.matmul(wb[0:96, place * E:(place + 1) * E], hn_st[:, pair, t * TP:(t + 1) * TP],
                                             w_st[:, i, 2 * E:3 * E], start=(i == 0), stop=(i == NL - 1))
                elif kind == "m":
                    n = (st_.core if j else st_.maxima)[0]
                    pe.wait_ge(max_done, H * n + (j + 1) * H // 2)
                    for t in range(T):
                        last = pe.transpose(wb[0:H // 2, t * TP:(t + 1) * TP],
                                            mx[:, t, j * H // 2:(j + 1) * H // 2], ident[0:96, 0:96])
                elif kind == "x":
                    n, k, r = st_.finish if j == 2 else st_.core
                    pe.wait_ge(masked, NG * T * n + T * (j + 1))
                    for t in range(T):
                        for i in range(HG):
                            last = pe.matmul(wb[i * STRIP:(i + 1) * STRIP, 0:NT], v_st[r][:, t, HG * j + i, :],
                                             prob[j][:, i, t, :], start=(t == 0), stop=(t == T - 1))
                elif kind == "o":
                    for g in range(NG):
                        last = pe.transpose(wb[0:96, g * 128:(g + 1) * 128], oT[:, g, j * TP:(j + 1) * TP],
                                            ident[:, :])
                elif kind == "n":
                    for t in range(T):
                        last = pe.transpose(wb[0:96, t * TP:(t + 1) * TP], on[:, t, j * 96:(j + 1) * 96],
                                            ident[0:96, 0:96])
                else:
                    for i, t in enumerate(([0, 1], [2])[j]):
                        for f in range(F2):
                            last = pe.matmul(wb[0:96, i * E:(i + 1) * E], onT[:, f, t * TP:(t + 1) * TP], w_p_sb[:, f, :],
                                             start=(f == 0), stop=(f == F2 - 1))
                last.then_inc(work_ready, 1)

            def scores(bank, left, right, rows, h, done, mask):
                for t in range(T):
                    width = min(TP, NT - t * TP)
                    last = pe.matmul(bank[0:96, t, 0:NT], left[0:rows, h, t * TP:(t + 1) * TP], right[0:rows, h, 0:NT],
                              start=True, stop=not mask)
                    if mask:
                        last = pe.matmul(bank[0:96, t, t * TP:t * TP + width], ident_bf[0:96, 0:96],
                                         neg_diag[0:96, 0 if t == 0 else 1, 0:width], start=False, stop=True)
                last.then_inc(done, 1)

            def step(st_):
                for h in range(H):
                    if st_.core is not None:
                        n, k, r = st_.core
                        wait(pe, exp_done, H * n + h)
                        if h % (H // 2) == 0:
                            pe.wait_ge(m_in[r][h // (H // 2)], 32 * (k + 1))
                        scores(st, k_st[r], q_st[r], SROWS, h, st_ready, False)
                    unit(BEFORE[h], st_)
                    if st_.maxima is not None:
                        n, k, r = st_.maxima
                        if h == 0:
                            pe.wait_ge(stack_in[r], 16 * 12 * (k + 1))
                        wait(pe, max_done, H * n + h)
                        scores(sm, q_st[r], k_st[r], KROWS, h, sm_ready, True)
                    unit(AFTER[h], st_)

            pe.wait_ge(weights_in, 16 * N_WEIGHTS)
            pe.wait_ge(cleared, 2)
            pe.wait_ge(w_parts, 2)
            steps(pe, step)

        @block.scalar
        def _(act):
            def unit(name, st_):
                if name is None or not st_.has(name) or name[0] not in "tqvnx":
                    return
                act.wait_ge(work_ready, st_.seq(name) + 1)
                kind, j = name[0], int(name[1])
                wb = work[st_.bank(name)]
                if kind == "x":
                    ins = nc.scalar.copy(oT[:, j, 0:NT], wb[:, 0:NT])
                elif kind == "t":
                    n = st_.front[0]
                    if j == 0:
                        wait(act, hn_low_third, n)
                        wait(act, hn_low, n)
                    units = TURNS[name]
                    nc.scalar.copy(hnT[:, units[0] * TP:(units[-1] + 1) * TP], wb[:, 0:len(units) * TP]
                                   ).then_inc(hn_turned, 1)
                    act.wait_ge(hn_turned, 2 * n + j + 1)
                    act.sem_inc(work_free[st_.bank(name)], 1)
                    return
                elif kind == "q":
                    wait(act, split, 4 * st_.front[0])
                    ins = nc.scalar.activation(qk[:, j, :], wb[0:96, 0:NT], ACT.Identity, bias=bqk_s[:, j:j + 1],
                                               scale=scl[:, j:j + 1] if j < 2 else 1.0)
                elif kind == "n":
                    ins = nc.scalar.activation(onT[:, j, :], wb[0:96, 0:PAD], ACT.Identity, bias=bv[:, j:j + 1])
                else:
                    t0, nt = ((0, 2), (2, 1))[j]
                    dst = v_st[st_.front[2]][:, t0:t0 + nt, :, 0:D]
                    ins = nc.scalar.copy(dst, wb[0:96, 0:nt * E].rearrange("p (t h d) -> p t h d", t=nt, d=D))
                ins.then_inc(work_free[st_.bank(name)], 1)

            def head_exp(h, st_):
                n, k, r = st_.core
                act.wait_ge(st_ready, H * n + h + 1)
                nc.scalar.activation(prob[h // HG][:, h % HG], st[0:96, :, 0:NT], ACT.Exp).then_inc(exp_done, 1)

            def high_parts(image):
                act.wait_ge(hn_top_ready, image[0] + 1)
                for rows, j in ((slice(0, 128), 0), (slice(0, THIRD), 1)):
                    last = nc.scalar.copy(hn_st[rows, j, :], hn_top[rows, j * PAD:(j + 1) * PAD])
                last.then_inc(hn_high, 1)

            def step(st_):
                for slot, name in enumerate(SLOTS):
                    if slot % 2 == 0 and st_.core is not None:
                        head_exp(slot // 2, st_)
                    unit(name, st_)
                    if slot == SPLIT_AT + 1 and st_.front is not None:
                        high_parts(st_.front)

            act.wait_ge(weights_in, 16 * N_WEIGHTS)
            act.wait_ge(cleared, 2)
            nc.scalar.copy(bqk_s[:, 2:4], bqk[:, 2:4]).then_inc(sb_const["bias_scaled"], 1)
            for m in range(2):
                nc.scalar.activation(bqk_s[:, m:m + 1], bqk[:, m:m + 1], ACT.Identity,
                                     scale=scl[:, m:m + 1]).then_inc(sb_const["bias_scaled"], 1)
            act.wait_ge(sb_const["bias_scaled"], 3)
            act.wait_ge(w_top_ready, 2)
            for o, top in stack_parts(raw_qkv[:], w_top[:], w_st[:])[0]:
                last = nc.scalar.copy(o, top)
            last.then_inc(w_parts, 1)
            steps(act, step)

        @block.vector
        def _(dve):
            def clear(view, value=0.0):
                nc.vector.memset(view, value).then_inc(sb_const["dve_cleared"], 1)

            for r in range(3):
                clear(h_front[r][64:96, T - 1, :])
                clear(h_res[r][64:96, T - 1, :])
            for r in range(3):
                clear(q_st[r][:, :, NT:PAD])
                clear(k_st[r][:, :, NT:PAD])
            clear(oT[:, :, NT:PAD], 1.0)
            for r in range(3):
                ones = k_st[r][KROWS:SROWS, :, 0:NT - 1].bitcast(mybir.dt.uint32)
                nc.vector.memset(ones, 0x3F803F80).then_inc(sb_const["dve_cleared"], 1)
                nc.vector.memset(k_st[r][KROWS:SROWS, :, NT - 1:NT], 1.0).then_inc(sb_const["dve_cleared"], 1)
            dve.wait_ge(sb_const["dve_cleared"], 19)
            dve.sem_inc(cleared, 1)

            def statistics(image):
                n, k, r = image
                dve.wait_ge(hf_in[r], 48 * (k + 1))
                wait(dve, hn_ready, T * n)
                for t in range(T):
                    nc.vector.bn_stats(bst[:, t, :], h_front[r][:, t, :]).then_inc(stats, 1)
                dve.wait_ge(stats, 2 * T * n + T)
                settled(dve, sb_const)
                for t in range(T):
                    nc.vector.bn_aggr(mv[:, t, :], bst[:, t, :]).then_inc(stats, 1)

            def unit(name, st_):
                if name is None or not st_.has(name) or name[0] not in "mop":
                    return
                dve.wait_ge(work_ready, st_.seq(name) + 1)
                kind, j = name[0], int(name[1])
                wb, free = work[st_.bank(name)], work_free[st_.bank(name)]
                if kind == "m":
                    n, k, r = st_.core if j else st_.maxima
                    if not (isinstance(n, int) and n == 0):
                        rr, kk = (r - 1) % 3, (k if r > 0 else k - 1)
                        dve.wait_ge(m_in[rr][j], 32 * (kk + 1))
                    nc.vector.tensor_scalar(m_hi[j][:], wb[0:H // 2, 0:PAD], -1.0, None, ALU.mult
                                            ).then_inc(m_split[j], 1)
                    dve.wait_ge(m_split[j], n + 1)
                    nc.vector.scalar_tensor_tensor(m_lo[j][:], wb[0:H // 2, 0:PAD], -1.0, m_hi[j][:],
                                                   ALU.mult, ALU.subtract).then_inc(m_ready[j], 1)
                    dve.wait_ge(m_ready[j], n + 1)
                    dve.sem_inc(free, 1)
                elif kind == "o":
                    n, k, r = st_.finish
                    heads = wb[0:96, 0:H * STRIP].rearrange("p (h c) -> p h c", c=STRIP)
                    nc.vector.reciprocal(rden[:, j, :], heads[:, :, D]).then_inc(rd_done, 1)
                    dve.wait_ge(rd_done, T * n + j + 1)
                    nc.vector.tensor_tensor(on[:, j, :].rearrange("p (h d) -> p h d", d=D), heads[:, :, 0:D],
                                            rden[:, j, :].unsqueeze(2).to_broadcast([96, H, D]), ALU.mult
                                            ).then_inc(free, 1)
                else:
                    n, k, r = st_.finish
                    if j == 0:
                        dve.wait_ge(res_ready, n + 1)
                        wait(dve, stored[r], 32 * k)
                    t0, nt = ((0, 2), (2, 1))[j]
                    ins = nc.vector.tensor_tensor(h_out[r][:, t0:t0 + nt, :].rearrange("p t e -> p (t e)"),
                                                  wb[0:96, 0:nt * E],
                                                  h_res[r][:, t0:t0 + nt, :].rearrange("p t e -> p (t e)"), ALU.add)
                    ins.then_inc(h2_done, 1)
                    dve.wait_ge(h2_done, 2 * n + j + 1)
                    dve.sem_inc(free, 1)

            def split_part(i, st_):
                n, k, r = st_.front
                if i == 0:
                    for q in ("q2", "q3"):
                        dve.wait_ge(work_free[st_.bank(q)], st_.turns(q) + 1)
                    if not (isinstance(n, int) and n == 0):
                        rr, kk = (r - 1) % 3, (k if r > 0 else k - 1)
                        dve.wait_ge(stack_in[rr], 192 * (kk + 1))
                else:
                    dve.wait_ge(split, 4 * n + i)
                if i == 0:
                    ins = nc.vector.tensor_copy(parts[:, 0], qk[:])
                elif i == 1:
                    ins = nc.vector.tensor_tensor(qk_rest[:], qk[:], parts[:, 0], ALU.subtract)
                else:
                    ins = nc.vector.tensor_copy(parts[:, 1], qk_rest[:])
                ins.then_inc(split, 1)

            def take_parts(image):
                n = image[0]
                dve.wait_ge(hn_turned, 2 * n + 2)
                wait(dve, hn_high, n)
                wait(dve, hn_low, n)
                wait(dve, hn_low_third, n)
                high_bits(nc.vector, hn_top[:], hnT[:]).then_inc(hn_top_ready, 1)
                dve.wait_ge(hn_top_ready, n + 1)
                rows, pair = slice(THIRD, 128), slice(PAD, 2 * PAD)
                nc.vector.tensor_tensor(hn_st[rows, 1, :], hnT[rows, pair], hn_top[rows, pair], ALU.subtract
                                        ).then_inc(hn_low_third, 1)

            def step(st_):
                for h in range(H):
                    unit(BEFORE[h], st_)
                    if SPLIT_AT == 2 * h and st_.front is not None:
                        take_parts(st_.front)
                    if st_.maxima is not None:
                        n, k, r = st_.maxima
                        dve.wait_ge(sm_ready, H * n + h + 1)
                        nc.vector.tensor_reduce(mx[:, :, h], sm[0:96, :, 0:NT], AX.X, ALU.max).then_inc(max_done, 1)
                    unit(AFTER[h], st_)
                    if SPLIT_AT == 2 * h + 1 and st_.front is not None:
                        take_parts(st_.front)
                    if st_.front is not None and 5 <= h < 8:
                        split_part(h - 5, st_)
                    if st_.next is not None and h == 3:
                        statistics(st_.next)

            dve.wait_ge(cleared, 2)
            statistics((0, 0, 0))
            dve.wait_ge(weights_in, 16 * N_WEIGHTS)
            nc.vector.memset(w_st[THIRD:128, NL - 1, :].bitcast(F32), 0.0).then_inc(w_top_ready, 1)
            high_bits(nc.vector, w_top[:], raw_qkv[:]).then_inc(w_top_ready, 1)
            dve.wait_ge(w_top_ready, 2)
            for o, whole, part in stack_parts(raw_qkv[:], w_top[:], w_st[:])[1]:
                last = nc.vector.tensor_tensor(o, whole, part, ALU.subtract)
            last.then_inc(w_parts, 1)
            steps(dve, step)


def mix_experts(nc, ctx, sems, sb_const, mixed, w1, b1, w2, b2, down_w, down_b, up_w, gamma, beta, out):
    NE, E, DH = down_w.shape
    RH = w1.shape[1]
    TP, T = 112, 4
    N = TP * T
    src = mixed.rearrange("b t e -> (b t) e")
    dst = out.rearrange("b t e -> (b t) e")
    NTILE = src.shape[0] // N
    M2 = DH // 128
    TOP_K = 2
    assert src.shape[0] == NTILE * N and NTILE >= 7 and E == 192 and RH == 96
    ident = sb_const["ident"]

    def sb(name, shape, dt=F32):
        return ctx.enter_context(nc.sbuf_tensor(name, shape, dt))

    def sem(name):
        return sems.enter_context(nc.semaphore(name))

    def ps(name):
        return ctx.enter_context(nc.psum_tensor(name, [128, BANK], F32))

    raw = sb("m_raw", [128, NE * 3 * DH])
    raw_w1 = sb("m_raw_w1", [128, 3, RH])
    w_top = [sb(f"m_w_top{a}", [128, 3 * DH]) for a in range(2)]
    w1_st = sb("m_w1_st", [128, NL, RH], F32R)
    down_st = sb("m_down_st", [128, NE, NL, DH], F32R)
    up_high = sb("m_up_high", [128, NE, M2, E], F32R)
    up_low = sb("m_up_low", [128, NE, M2, E], F32R)
    down_b_sb = sb("m_downb", [128, NE, M2])
    b1_sb = sb("m_b1", [RH, 1])
    w2_sb = sb("m_w2", [RH, NE])
    b2_bc = sb("m_b2", [TP, T, NE])
    gamma_bc = sb("m_gamma", [TP, 1, E])
    beta_bc = sb("m_beta", [TP, 1, E])
    minus_half = sb("m_mh", [TP, T])
    lower = sb("m_lower", [TP, NE, NE])
    h_in = [sb(f"m_h{p}", [TP, T, E]) for p in range(2)]
    h_beta = [sb(f"m_hb{p}", [TP, T, E]) for p in range(2)]
    xn = [sb(f"m_x{p}", [TP, T, E + THIRD]) for p in range(2)]
    xT = sb("m_xT", [128, 3, N])
    x_top = sb("m_x_top", [128, 3, N])
    x_st = [sb(f"m_x_st{p}", [128, 3, N], F32R) for p in range(2)]
    uT = sb("m_uT", [RH, N])
    bst = sb("m_bst", [TP, T, 6])
    mv = sb("m_mv", [TP, T, 2])
    rstd = sb("m_rstd", [TP, T, 2])
    fst = sb("m_fst", [TP, T, 6])
    fmv = sb("m_fmv", [TP, T, 2])
    frstd = sb("m_frstd", [TP, T, 2])
    logits = sb("m_logits", [TP, T, NE])
    lmax = sb("m_lmax", [TP, T])
    shifted = sb("m_shifted", [TP, T, NE])
    ex = sb("m_ex", [TP, T, NE])
    total = sb("m_total", [TP, T])
    rtotal = sb("m_rtotal", [TP, T])
    routing = sb("m_routing", [TP, T, NE])
    above = sb("m_above", [TP, T, NE, NE])
    equal = sb("m_equal", [TP, T, NE, NE])
    tie = sb("m_tie", [TP, T, NE, NE])
    ahead = sb("m_ahead", [TP, T, NE, NE])
    rank = sb("m_rank", [TP, T, NE])
    sparse = sb("m_sparse", [TP, T, NE])
    kept = sb("m_kept", [TP, T])
    kept_eps = sb("m_kept_eps", [TP, T])
    rkept = sb("m_rkept", [TP, T])
    gates = [sb(f"m_gates{p}", [TP, T, NE]) for p in range(2)]
    z = [sb(f"m_z{a}", [128, M2, N]) for a in range(2)]
    z_top = [sb(f"m_z_top{a}", [128, M2, N]) for a in range(2)]
    z_high = [sb(f"m_zh{a}", [128, M2, N], F32R) for a in range(2)]
    z_low = [sb(f"m_zl{a}", [128, M2, N], F32R) for a in range(2)]
    acc = [sb(f"m_acc{p}", [TP, T, E]) for p in range(2)]
    y = [sb(f"m_y{p}", [TP, T, E]) for p in range(2)]

    hid = [ps(f"m_hid{n}") for n in range(4)]
    upb = [ps(f"m_up{n}_ps") for n in range(2)]
    fb = [ps(f"m_front{n}") for n in range(2)]

    weights_in = sem("m_weights_in")
    lower_ready = sem("m_lower_ready")
    h_loaded = [sem(f"m_h_in{p}") for p in range(2)]
    stats = sem("m_stats")
    pool_own = sem("m_pool_own")
    xn_ready = sem("m_xn_ready")
    hb_ready = sem("m_hb_ready")
    front_ready = sem("m_front_ready")
    front_free = sem("m_front_free")
    gate_step = sem("m_gate_step")
    ex_ready = sem("m_ex_ready")
    hid_ready = sem("m_hid_ready")
    z_ready = sem("m_z_ready")
    z_top_ready = sem("m_z_top_ready")
    z_high_ready = sem("m_z_high_ready")
    z_low_ready = sem("m_z_low_ready")
    z_low_rest = sem("m_z_low_rest")
    x_top_ready = sem("m_x_top_ready")
    x_high_ready = sem("m_x_high_ready")
    x_low_ready = sem("m_x_low_ready")
    raw_in = [sem(f"m_raw_in_{w}") for w in ("w1", "down", "up")]
    x_low_third = sem("m_x_low_third")
    zeros = sem("m_zeros")
    w_top_ready = sem("m_w_top_ready")
    w_high = sem("m_w_high")
    w_low = sem("m_w_low")
    up_ready = sem("m_up_ready")
    acc_done = sem("m_acc_done")
    fstats = sem("m_fstats")
    final = sem("m_final")
    stored = [sem(f"m_stored{p}") for p in range(2)]
    GATE_OPS = 15
    FINAL_OPS = 5

    class Step:

        def __init__(self, k, p):
            self.s = 2 * k + p
            self.first = isinstance(self.s, int) and self.s == 0
            fixed = isinstance(k, int)
            self.next = self._tile(k, p, -1) if not fixed or self.s + 1 < NTILE else None
            self.front = self._tile(k, p, 0) if not fixed or self.s < NTILE else None
            self.experts = self._tile(k, p, 1) if not fixed or 1 <= self.s <= NTILE else None
            self.end = self._tile(k, p, 2) if not fixed or 2 <= self.s <= NTILE + 1 else None

        @staticmethod
        def _tile(k, p, back):
            q, pp = divmod(p - back, 2)
            return 2 * k + p - back, k + q, pp

    LOOPS = (NTILE - 1) // 2

    def steps(engine, do):
        for s in range(4):
            do(Step(s // 2, s % 2))
        with engine.Fori(2, LOOPS) as k:
            for p in range(2):
                do(Step(k, p))
        for s in range(2 * LOOPS, NTILE + 2):
            do(Step(s // 2, s % 2))

    def wait(eng, semaphore, value):
        if not (isinstance(value, int) and value <= 0):
            eng.wait_ge(semaphore, value)

    N_WEIGHTS = 7
    RAW_PARTS = [4, 4, 2]

    raw_down = raw[:].rearrange("p (n j o) -> p n j o", n=NE, j=3)
    raw_up = raw[:, 0:NE * M2 * E].rearrange("p (n m o) -> p n m o", n=NE, m=M2)
    UP = NE + 1

    def weight_split(i):
        which = 0 if i == 0 else 1 if i < UP else 2
        if which == 2:
            raw_w = raw_up[:, i - UP]
            top = w_top[i % 2][:, 0:M2 * E].rearrange("p (a o) -> p a o", a=M2)
            return which, raw_w, top, [(up_high[:, i - UP], top)], [(up_low[:, i - UP], raw_w, top)]
        raw_w, stack = (raw_down[:, i - 1], down_st[:, i - 1]) if which else (raw_w1[:], w1_st[:])
        size = stack.shape[2]
        top = w_top[i % 2][:, 0:3 * size].rearrange("p (a o) -> p a o", a=3)
        high, low = stack_parts(raw_w, top, stack)
        return which, raw_w, top, high, low

    def three_passes(pe, o, left, right, chunks):
        pairs = [(k, a, b) for a, b in ((0, 1), (1, 0), (0, 0)) for k in range(chunks)]
        for i, (k, a, b) in enumerate(pairs):
            last = pe.matmul(o, left[a](k), right[b](k),
                             start=(i == 0), stop=(i == len(pairs) - 1))
        return last

    with nc.Block() as block:

        @block.sync
        def _(sp):
            def dma(o, i, semaphore, **kw):
                sp.dma_start(o, i, **kw).then_inc(semaphore, 16)

            def load(tile):
                n, k, p = tile
                rows = src[bass.ds(n * N, N)].rearrange("(t p) e -> p t e", p=TP)
                dma(h_in[p][:], rows, h_loaded[p])

            load((0, 0, 0))
            for j, pair in enumerate(PAIRS):
                for o, i in thirds(pair):
                    dma(raw_w1[o, j, :], w1[i], raw_in[0])
            dma(b1_sb[:], b1.rearrange("(p a) -> p a", a=1), weights_in)
            dma(w2_sb[:], w2, weights_in)
            for m in range(M2):
                dma(down_b_sb[:, :, m], down_b[:, m * 128:(m + 1) * 128].rearrange("n p -> p n"), weights_in,
                    allow_slow_non_contiguous=True)
            for row, tile, size in ((gamma, gamma_bc, E), (beta, beta_bc, E), (b2, b2_bc, NE)):
                shape = [TP, tile.shape[1], size]
                dma(tile[:], row.rearrange("(a b o) -> a b o", a=1, b=1).to_broadcast(shape), weights_in)
            for j, pair in enumerate(PAIRS):
                for o, i in thirds(pair):
                    dma(raw_down[o, :, j, :], down_w[:, i, :].rearrange("n p o -> p n o"), raw_in[1])
            load((1, 0, 1))
            sp.wait_ge(w_low, UP)
            for m in range(M2):
                dma(raw_up[:, :, m, :], up_w[:, m * 128:(m + 1) * 128, :].rearrange("n p o -> p n o"), raw_in[2])

            def step(st):
                if st.next is not None and not st.first:
                    n, k, p = st.next
                    wait(sp, xn_ready, T * (n - 1))
                    wait(sp, hb_ready, n - 1)
                    load(st.next)
                if st.end is not None:
                    n, k, p = st.end
                    sp.wait_ge(final, FINAL_OPS * (n + 1))
                    rows = dst[bass.ds(n * N, N)].rearrange("(t p) e -> p t e", p=TP)
                    dma(rows, y[p][:], stored[p])

            steps(sp, step)
            for p in range(2):
                sp.wait_ge(stored[p], 16 * len(range(p, NTILE, 2)))

        @block.gpsimd
        def _(pool):
            nc.gpsimd.memset(minus_half[:], -0.5).then_inc(lower_ready, 1)
            nc.gpsimd.memset(lower[:], 1.0).then_inc(lower_ready, 1)
            pool.wait_ge(lower_ready, 2)
            nc.gpsimd.affine_select(out=lower[:], in_=lower[:], compare_op=ALU.is_gt, fill=0.0, base=0,
                                    pattern=[[1, NE], [-1, NE]], channel_multiplier=0).then_inc(lower_ready, 1)

            def deviation(tile):
                n, k, p = tile
                pool.wait_ge(stats, 2 * T * (n + 1))
                settled(pool, sb_const)
                nc.gpsimd.tensor_scalar(rstd[:, :, 0], mv[:, :, 1], LN_EPS, None, ALU.add).then_inc(pool_own, 1)
                pool.wait_ge(pool_own, 2 * n + 1)
                nc.gpsimd.tensor_tensor(rstd[:, :, 1], rstd[:, :, 0], minus_half[:], ALU.pow).then_inc(pool_own, 1)

            def residual(tile):
                n, k, p = tile
                wait(pool, final, FINAL_OPS * (n - 1))
                nc.gpsimd.tensor_tensor(h_beta[p][:], h_in[p][:], beta_bc[:].to_broadcast([TP, T, E]),
                                        ALU.add).then_inc(hb_ready, 1)

            def finish(tile, part):
                n, k, p = tile
                if part == 0:
                    pool.wait_ge(fstats, 2 * T * (n + 1))
                    settled(pool, sb_const)
                    nc.gpsimd.tensor_scalar(frstd[:, :, 0], fmv[:, :, 1], LN_EPS, None, ALU.add).then_inc(final, 1)
                    pool.wait_ge(final, FINAL_OPS * n + 1)
                    nc.gpsimd.tensor_tensor(frstd[:, :, 1], frstd[:, :, 0], minus_half[:], ALU.pow).then_inc(final, 1)
                elif part == 1:
                    pool.wait_ge(final, FINAL_OPS * n + 3)
                    nc.gpsimd.tensor_tensor(y[p][:], y[p][:], gamma_bc[:].to_broadcast([TP, T, E]), ALU.mult
                                            ).then_inc(final, 1)
                else:
                    pool.wait_ge(final, FINAL_OPS * n + 4)
                    pool.wait_ge(hb_ready, n + 1)
                    nc.gpsimd.tensor_tensor(y[p][:], y[p][:], h_beta[p][:], ALU.add).then_inc(final, 1)

            def low_x(tile):
                n, k, p = tile
                pool.wait_ge(x_top_ready, n + 1)
                nc.gpsimd.tensor_tensor(x_st[p][:, 2, :], xT[:, 2, :], x_top[:, 2, :], ALU.subtract
                                        ).then_inc(x_low_ready, 1)

            def low_z(e, st):
                n, k, p = st.experts
                pool.wait_ge(z_top_ready, NE * n + e + 1)
                wait(pool, up_ready, 2 * (NE * n + e - 1))
                nc.gpsimd.tensor_tensor(z_low[e % 2][:, 1, :], z[e % 2][:, 1, :], z_top[e % 2][:, 1, :],
                                        ALU.subtract).then_inc(z_low_rest, 1)

            def step(st):
                for e in range(NE):
                    if st.experts is not None:
                        low_z(e, st)
                    if st.next is not None and e == 3:
                        deviation(st.next)
                    if st.end is not None and e in (1, 3, 4):
                        finish(st.end, (1, 3, 4).index(e))
                    if st.front is not None and e == 2:
                        low_x(st.front)
                    if st.front is not None and e == 6:
                        residual(st.front)

            pool.wait_ge(weights_in, 16 * N_WEIGHTS)
            deviation((0, 0, 0))
            steps(pool, step)

        @block.tensor
        def _(pe):
            def front(u, st):
                n, k, p = st.front
                bank = fb[(p + u) % 2]
                wait(pe, front_free, 5 * n + u - (1 if u in (1, 2) else 0))
                if u < 3:
                    if u == 0:
                        pe.wait_ge(xn_ready, T * (n + 1))
                    start = STARTS[u]
                    for t in range(T):
                        last = pe.transpose(bank[0:128, t * TP:(t + 1) * TP], xn[p][:, t, start:start + 128],
                                            ident[0:TP, 0:TP])
                elif u == 3:
                    pe.wait_ge(x_high_ready, n + 1)
                    pe.wait_ge(x_low_third, n + 1)
                    pe.wait_ge(x_low_ready, n + 1)
                    if isinstance(n, int) and n == 0:
                        pe.wait_ge(zeros, 2)
                        pe.wait_ge(w_high, 1)
                        pe.wait_ge(w_low, 1)
                    last = stacked(bank[0:RH, 0:N], w1_st[:], x_st[p])
                else:
                    for t in range(T):
                        last = pe.matmul(bank[0:TP, t * NE:(t + 1) * NE], uT[:, t * TP:(t + 1) * TP], w2_sb[:],
                                         start=True, stop=True)
                last.then_inc(front_ready, 1)

            def stacked(o, left, right):
                for i, j in enumerate(RIGHT):
                    last = pe.matmul(o, left[:, i, :], right[:, j, :], start=(i == 0), stop=(i == NL - 1))
                return last

            def down(e, st):
                n, k, p = st.experts
                if isinstance(n, int) and n == 0:
                    pe.wait_ge(w_high, e + 2)
                    pe.wait_ge(w_low, e + 2)
                if e == 0:
                    pe.wait_ge(x_high_ready, n + 1)
                    pe.wait_ge(x_low_ready, n + 1)
                for m in range(M2):
                    wait(pe, z_ready, M2 * (NE * n + e - 2) + m + 1)
                    stacked(hid[M2 * (e % 2) + m][:, 0:N], down_st[:, e, :, m * 128:(m + 1) * 128], x_st[p]
                            ).then_inc(hid_ready, 1)

            def up(e, tile):
                n, k, p = tile
                if isinstance(n, int) and n == 0:
                    pe.wait_ge(w_high, UP + e + 1)
                    pe.wait_ge(w_low, UP + e + 1)
                pe.wait_ge(z_high_ready, NE * n + e + 1)
                pe.wait_ge(z_low_ready, NE * n + e + 1)
                pe.wait_ge(z_low_rest, NE * n + e + 1)
                for j in range(T // 2):
                    wait(pe, acc_done, T * (NE * n + e - 1) + 2 * j + 2)
                    for i in range(2):
                        rows = slice((2 * j + i) * TP, (2 * j + i + 1) * TP)
                        last = three_passes(pe, upb[j][0:TP, i * E:(i + 1) * E],
                                            (lambda m: z_high[e % 2][:, m, rows], lambda m: z_low[e % 2][:, m, rows]),
                                            (lambda m: up_high[:, e, m, :], lambda m: up_low[:, e, m, :]), M2)
                    last.then_inc(up_ready, 1)

            def step(st):
                for e in range(NE):
                    if st.experts is not None:
                        down(e, st)
                    if st.front is not None:
                        for u in ((0, 1), (2,), (), (), (3,), (4,), (), ())[e]:
                            front(u, st)
                    if e == 0 and st.end is not None:
                        up(NE - 1, st.end)
                    if e > 0 and st.experts is not None:
                        up(e - 1, st.experts)

            pe.wait_ge(weights_in, 16 * N_WEIGHTS)
            steps(pe, step)

        @block.scalar
        def _(act):
            def front(u, st):
                n, k, p = st.front
                if u == 4:
                    act.wait_ge(gate_step, GATE_OPS * n + 3)
                    nc.scalar.activation(ex[:], shifted[:], ACT.Exp).then_inc(ex_ready, 1)
                    return
                act.wait_ge(front_ready, 5 * n + u + 1)
                if u < 3:
                    if u == 0:
                        wait(act, x_low_third, n)
                        wait(act, x_low_ready, n)
                    ins = nc.scalar.copy(xT[:, u, :], fb[(p + u) % 2][:, 0:N])
                else:
                    ins = nc.scalar.activation(uT[:], fb[(p + u) % 2][0:RH, 0:N], ACT.Gelu, bias=b1_sb[:, 0:1])
                ins.then_inc(front_free, 1)

            def gelu(e, st):
                n, k, p = st.experts
                for m in range(M2):
                    act.wait_ge(hid_ready, M2 * (NE * n + e) + m + 1)
                    if m == 0:
                        wait(act, z_low_ready, NE * n + e - 1)
                        wait(act, z_low_rest, NE * n + e - 1)
                    nc.scalar.activation(z[e % 2][:, m, :], hid[M2 * (e % 2) + m][:, 0:N], ACT.Gelu,
                                         bias=down_b_sb[:, e, m:m + 1]).then_inc(z_ready, 1)

            def high_z(e, st):
                n, k, p = st.experts
                act.wait_ge(z_top_ready, NE * n + e + 1)
                wait(act, up_ready, 2 * (NE * n + e - 1))
                nc.scalar.copy(z_high[e % 2][:], z_top[e % 2][:]).then_inc(z_high_ready, 1)

            def high_x(tile):
                n, k, p = tile
                act.wait_ge(x_top_ready, n + 1)
                for rows, j in ((slice(0, 128), 0), (slice(0, THIRD), 1)):
                    last = nc.scalar.copy(x_st[p][rows, j, :], x_top[rows, j, :])
                last.then_inc(x_high_ready, 1)

            def high_weights(first, end):
                for i in range(first, end):
                    _, _, _, high, _ = weight_split(i)
                    act.wait_ge(w_top_ready, i + 1)
                    for o, top in high:
                        last = nc.scalar.copy(o, top)
                    last.then_inc(w_high, 1)

            def step(st):
                if st.first:
                    for u in range(3):
                        front(u, st)
                    high_weights(0, 1)
                    high_x(st.front)
                    front(3, st)
                    high_weights(1, UP)
                    front(4, st)
                    high_weights(UP, UP + NE)
                    return
                for e in range(NE):
                    if st.experts is not None:
                        gelu(e, st)
                        high_z(e, st)
                    if st.front is not None:
                        for u in ((0, 1), (2,), (), (), (3,), (4,), (), ())[e]:
                            front(u, st)
                    if st.front is not None and e == 2:
                        high_x(st.front)

            act.wait_ge(weights_in, 16 * N_WEIGHTS)
            steps(act, step)

        @block.vector
        def _(dve):
            def statistics(tile):
                n, k, p = tile
                dve.wait_ge(h_loaded[p], 16 * (k + 1))
                wait(dve, xn_ready, T * n)
                for t in range(T):
                    nc.vector.bn_stats(bst[:, t, :], h_in[p][:, t, :]).then_inc(stats, 1)
                dve.wait_ge(stats, 2 * T * n + T)
                settled(dve, sb_const)
                for t in range(T):
                    nc.vector.bn_aggr(mv[:, t, :], bst[:, t, :]).then_inc(stats, 1)

            def normalise(tile):
                n, k, p = tile
                dve.wait_ge(pool_own, 2 * n + 2)
                wait(dve, acc_done, T * NE * (n - 2) + T)
                for t in range(T):
                    for o, size in ((E, THIRD), (0, E)):
                        last = nc.vector.tensor_scalar(xn[p][:, t, o:o + size], h_in[p][:, t, 0:size],
                                                       mv[:, t, 0:1], rstd[:, t, 1:2], ALU.subtract, ALU.mult)
                    last.then_inc(xn_ready, 1)

            def final_normalise(tile):
                n, k, p = tile
                dve.wait_ge(final, FINAL_OPS * n + 2)
                wait(dve, stored[p], 16 * k)
                for t in range(T):
                    last = nc.vector.tensor_scalar(y[p][:, t, :], acc[p][:, t, :], fmv[:, t, 0:1],
                                                   frstd[:, t, 1:2], ALU.subtract, ALU.mult)
                last.then_inc(final, 1)

            def final_statistics(tile):
                n, k, p = tile
                wait(dve, final, FINAL_OPS * n)
                dve.wait_ge(acc_done, T * NE * (n + 1))
                for t in range(T):
                    nc.vector.bn_stats(fst[:, t, :], acc[p][:, t, :]).then_inc(fstats, 1)
                dve.wait_ge(fstats, 2 * T * n + T)
                settled(dve, sb_const)
                for t in range(T):
                    nc.vector.bn_aggr(fmv[:, t, :], fst[:, t, :]).then_inc(fstats, 1)

            def gate(tile, part):
                n, k, p = tile
                count = [(0, 3, 7, 11)[part]]

                def chain(ins):
                    count[0] += 1
                    ins.then_inc(gate_step, 1)
                    dve.wait_ge(gate_step, GATE_OPS * n + count[0])

                def wide(tile_, shape=(TP, T, NE)):
                    return tile_[:].unsqueeze(2).to_broadcast(list(shape))

                others = routing[:].unsqueeze(2).to_broadcast([TP, T, NE, NE])
                own = routing[:].unsqueeze(3).to_broadcast([TP, T, NE, NE])
                if part == 0:
                    dve.wait_ge(front_ready, 5 * n + 5)
                    chain(nc.vector.tensor_tensor(logits[:].rearrange("p t e -> p (t e)"), fb[p][0:TP, 0:T * NE],
                                                  b2_bc[:].rearrange("p t e -> p (t e)"), ALU.add))
                    dve.sem_inc(front_free, 1)
                    chain(nc.vector.tensor_reduce(lmax[:], logits[:], AX.X, ALU.max))
                    chain(nc.vector.tensor_tensor(shifted[:], logits[:], wide(lmax), ALU.subtract))
                elif part == 1:
                    dve.wait_ge(ex_ready, n + 1)
                    chain(nc.vector.tensor_reduce(total[:], ex[:], AX.X, ALU.add))
                    chain(nc.vector.reciprocal(rtotal[:], total[:]))
                    chain(nc.vector.tensor_tensor(routing[:], ex[:], wide(rtotal), ALU.mult))
                    chain(nc.vector.tensor_tensor(above[:], others, own, ALU.is_gt))
                elif part == 2:
                    chain(nc.vector.tensor_tensor(equal[:], others, own, ALU.is_equal))
                    chain(nc.vector.tensor_tensor(tie[:].rearrange("p t e j -> p t (e j)"),
                                                  equal[:].rearrange("p t e j -> p t (e j)"),
                                                  lower[:].rearrange("p e j -> p (e j)").unsqueeze(1)
                                                  .to_broadcast([TP, T, NE * NE]), ALU.mult))
                    chain(nc.vector.tensor_tensor(ahead[:], above[:], tie[:], ALU.add))
                    chain(nc.vector.tensor_reduce(rank[:], ahead[:], AX.X, ALU.add))
                else:
                    chain(nc.vector.scalar_tensor_tensor(sparse[:], rank[:], float(TOP_K), routing[:],
                                                         ALU.is_lt, ALU.mult))
                    chain(nc.vector.tensor_reduce(kept[:], sparse[:], AX.X, ALU.add))
                    chain(nc.vector.tensor_scalar(kept_eps[:], kept[:], GATE_EPS, None, ALU.add))
                    chain(nc.vector.reciprocal(rkept[:], kept_eps[:]))
                    assert count[0] == GATE_OPS
                    nc.vector.tensor_tensor(gates[p][:], sparse[:], wide(rkept), ALU.mult).then_inc(gates_ready, 1)

            def split_x(tile):
                n, k, p = tile
                dve.wait_ge(front_free, 5 * n + 3)
                wait(dve, x_high_ready, n)
                wait(dve, x_low_ready, n)
                wait(dve, x_low_third, n)
                high_bits(nc.vector, x_top[:], xT[:]).then_inc(x_top_ready, 1)
                dve.wait_ge(x_top_ready, n + 1)
                rows = slice(THIRD, 128)
                nc.vector.tensor_tensor(x_st[p][rows, 1, :], xT[rows, 1, :], x_top[rows, 1, :], ALU.subtract
                                        ).then_inc(x_low_third, 1)

            def split_z(e, st):
                n, k, p = st.experts
                dve.wait_ge(z_ready, M2 * (NE * n + e + 1))
                wait(dve, z_high_ready, NE * n + e - 1)
                wait(dve, z_low_rest, NE * n + e - 1)
                high_bits(nc.vector, z_top[e % 2][:], z[e % 2][:]).then_inc(z_top_ready, 1)
                dve.wait_ge(z_top_ready, NE * n + e + 1)
                wait(dve, up_ready, 2 * (NE * n + e - 1))
                nc.vector.tensor_tensor(z_low[e % 2][:, 0, :], z[e % 2][:, 0, :], z_top[e % 2][:, 0, :],
                                        ALU.subtract).then_inc(z_low_ready, 1)

            def split_weights(first, end):
                for i in range(first, end):
                    which, raw_w, top, _, low = weight_split(i)
                    if i in (0, 1, UP):
                        dve.wait_ge(raw_in[which], 16 * RAW_PARTS[which])
                    if i >= 2:
                        dve.wait_ge(w_high, i - 1)
                        dve.wait_ge(w_low, i - 1)
                    high_bits(nc.vector, top, raw_w).then_inc(w_top_ready, 1)
                    dve.wait_ge(w_top_ready, i + 1)
                    for o, whole, part in low:
                        last = nc.vector.tensor_tensor(o, whole, part, ALU.subtract)
                    last.then_inc(w_low, 1)

            def sums(e, tile):
                n, k, p = tile
                if e == 0:
                    dve.wait_ge(gates_ready, n + 1)
                    wait(dve, final, FINAL_OPS * (n - 2) + 3)
                for t in range(T):
                    if t % 2 == 0:
                        dve.wait_ge(up_ready, 2 * (NE * n + e) + t // 2 + 1)
                    if e > 0:
                        dve.wait_ge(acc_done, T * (NE * n + e - 1) + t + 1)
                    before = xn[p] if e == 0 else acc[p]
                    nc.vector.scalar_tensor_tensor(acc[p][:, t, :], upb[t // 2][0:TP, (t % 2) * E:(t % 2 + 1) * E],
                                                   gates[p][:, t, e:e + 1], before[:, t, 0:E], ALU.mult, ALU.add
                                                   ).then_inc(acc_done, 1)

            def step(st):
                if st.first:
                    split_weights(0, 1)
                    split_x(st.front)
                    split_weights(1, UP)
                    statistics(st.next)
                    normalise(st.next)
                    for part in range(4):
                        gate(st.front, part)
                    split_weights(UP, UP + NE)
                    return
                for e in range(NE):
                    if st.experts is not None:
                        split_z(e, st)
                        if e > 0:
                            sums(e - 1, st.experts)
                    if st.end is not None and e == 0:
                        sums(NE - 1, st.end)
                        final_statistics(st.end)
                    if st.front is not None and e == 1:
                        split_x(st.front)
                    if st.end is not None and e == 2:
                        final_normalise(st.end)
                    if st.next is not None and e == 3:
                        statistics(st.next)
                    if st.next is not None and e == 4:
                        normalise(st.next)
                    if st.front is not None and e >= 5:
                        gate(st.front, e - 5)
                if st.front is not None:
                    gate(st.front, 3)

            gates_ready = sb_const["gates_ready"]
            dve.wait_ge(lower_ready, 3)
            for stack in (w1_st[THIRD:128, NL - 1, :], down_st[THIRD:128, :, NL - 1, :]):
                nc.vector.memset(stack.bitcast(F32), 0.0).then_inc(zeros, 1)
            statistics((0, 0, 0))
            normalise((0, 0, 0))
            dve.wait_ge(weights_in, 16 * N_WEIGHTS)
            steps(dve, step)


def early_fusion(nc, x, txt, tok_w, tok_bias, w_qk, b_qk, w_v, b_v, scale, w_proj, b_proj,
                 w1, b1, w2, b2, down_w, down_b, up_w, gamma, beta, out):
    B, NT, E = out.shape
    tokens = nc.dram_tensor("tokens_scratch", (B, NT - txt.shape[1], E), F32).ap()
    mixed = nc.dram_tensor("mixed_scratch", (B, NT, E), F32).ap()
    with ExitStack() as sems:
        sb_const = constants(nc, sems)
        with ExitStack() as ctx:
            tokenize(nc, ctx, sems, sb_const, x, tok_w, tok_bias, tokens)
        with ExitStack() as ctx:
            attend(nc, ctx, sems, sb_const, tokens, txt, w_qk, b_qk, w_v, b_v, scale, w_proj, b_proj, mixed)
        with ExitStack() as ctx:
            mix_experts(nc, ctx, sems, sb_const, mixed, w1, b1, w2, b2, down_w, down_b, up_w, gamma, beta, out)




def by_head_pair(a, E=192, H=12):
    a = a[..., :2 * E]
    lead = a.shape[:-1]
    n = len(lead)
    a = a.reshape(lead + (2, H // 2, 2, E // H))
    return a.transpose(tuple(range(n)) + (n, n + 2, n + 3, n + 1)).reshape(lead + (2 * E,))


def kernel(x, txt, L0_tok_weight, L0_tok_bias, L0_attn_w_qkv, L0_attn_b_qkv, L0_attn_scale, L0_attn_w_proj,
           L0_attn_b_proj, L0_ffn_w1, L0_ffn_b1, L0_ffn_w2, L0_ffn_b2, L0_ffn_down_w, L0_ffn_down_b, L0_ffn_up_w,
           L0_ffn_gamma, L0_ffn_beta):
    import numpy as np
    import concourse.bacc as bacc
    from concourse.bass_utils import run_bass_kernel_spmd

    w_qkv, b_qkv = np.asarray(L0_attn_w_qkv), np.asarray(L0_attn_b_qkv)
    E = w_qkv.shape[0]
    arrays = {
        "x": x, "txt": txt, "tok_w": np.asarray(L0_tok_weight).T, "tok_bias": L0_tok_bias,
        "w_qk": by_head_pair(w_qkv), "b_qk": by_head_pair(b_qkv), "w_v": w_qkv[:, 2 * E:], "b_v": b_qkv[2 * E:],
        "scale": L0_attn_scale, "w_proj": L0_attn_w_proj, "b_proj": L0_attn_b_proj, "w1": L0_ffn_w1,
        "b1": L0_ffn_b1, "w2": L0_ffn_w2, "b2": L0_ffn_b2, "down_w": L0_ffn_down_w, "down_b": L0_ffn_down_b,
        "up_w": L0_ffn_up_w, "gamma": L0_ffn_gamma, "beta": L0_ffn_beta,
    }
    arrays = {name: np.ascontiguousarray(a) for name, a in arrays.items()}
    B, IMG_T = x.shape[0], (x.shape[2] // 16) ** 2
    nc = bacc.Bacc("TRN2", target_bir_lowering=False, num_devices=1)
    aps = [nc.dram_tensor(name, a.shape, mybir.dt.from_np(a.dtype), kind="ExternalInput").ap()
           for name, a in arrays.items()]
    out = nc.dram_tensor("out", (B, IMG_T + txt.shape[1], E), F32, kind="ExternalOutput").ap()
    early_fusion(nc, *aps, out)
    r = run_bass_kernel_spmd(nc, [arrays], core_ids=[0])
    return r.results[0]["out"]
```
